# Optimizing a Trainium2 kernel written in Bass

```python
import numpy as np
import jax
import jax.numpy as jnp

def _softmax(x, axis=-1):
    return jax.nn.softmax(x, axis=axis)

def _gelu(x):
    return jax.nn.gelu(x, approximate=True)

def _silu(x):
    return jax.nn.silu(x)

def _sigmoid(x):
    return jax.nn.sigmoid(x)

def _layernorm(x, axis=-1, eps=1e-05):
    m = jnp.mean(x, axis=axis, keepdims=True)
    v = jnp.var(x, axis=axis, keepdims=True)
    return (x - m) / jnp.sqrt(v + eps)

def _scatter_add(tgt, idx, src, axis=0):
    return tgt.at[idx].add(src)

def _segment_sum(src, seg, n):
    return jax.ops.segment_sum(src, seg, n)
kernel_name = 'mk_flamingo_gated_d2_seqx_r4_4aa9a5'

def setup_inputs(seed: int=0):
    np.random.seed(seed)
    _w = jnp.asarray

    def _rec_inputs():
        import jax
        import jax.numpy as jnp
        _rk = jax.random.key(seed)
        x = -0.0005146 + 1 * jax.random.normal(jax.random.fold_in(_rk, 1), (16, 256, 256), jnp.float32)
        _lenS = 256 - jax.random.randint(jax.random.fold_in(_rk, 7), (16,), 0, max(1, 256 // 4) + 1, jnp.int32)
        _lenS2 = 256 - jax.random.randint(jax.random.fold_in(_rk, 8), (16,), 0, max(1, 256 // 4) + 1, jnp.int32)
        _ctx_768P = jax.random.normal(jax.random.fold_in(_rk, 11), (16, 16, 192), jnp.float32)
        _ctx_768c = jax.random.dirichlet(jax.random.fold_in(_rk, 511), 0.3 * jnp.ones((16,), jnp.float32), (16, 256))
        _ctx_768t = jnp.einsum('bsk,bkd->bsd', _ctx_768c, _ctx_768P)
        _ctx_768t = _ctx_768t * jax.lax.rsqrt(jnp.mean(jnp.square(_ctx_768t)) + 1e-12) * 0.953939
        ctx_768 = -0.00040386 + 0.999972 * (_ctx_768t + 0.3 * jax.random.normal(jax.random.fold_in(_rk, 611), (16, 256, 192), jnp.float32))
        _validS = jnp.arange(256)[None, :] < _lenS[:, None]
        _validS2 = jnp.arange(256)[None, :] < _lenS2[:, None]
        _causal = jnp.tril(jnp.ones((256, 256), dtype=bool))
        mask_BxS2_bk0 = jnp.logical_not(jnp.broadcast_to(_validS2[:, :], (16, 256)))
        _g = jax.random.normal(jax.random.fold_in(_rk, 9001), (2, 2), jnp.float32)
        _g = jnp.sign(_g) * jnp.maximum(jnp.abs(_g), 1.0) + (_g == 0) * 1.0
        g_xattn = _g[0]
        g_ffn = _g[1]
        return (x, ctx_768, mask_BxS2_bk0, g_xattn, g_ffn)
    x, ctx_768, mask_BxS2_bk0, g_xattn, g_ffn = _rec_inputs()

    def _L0_xattn_setup():
        import jax, jax.numpy as jnp
        import numpy as np
        DIM_IN, DIM_LAT, DIM_HEAD = (192, 256, 64)
        INNER = max(DIM_LAT, DIM_IN)
        HEADS = INNER // DIM_HEAD
        SCALE = DIM_HEAD ** (-0.5)
        RMS_EPS = 1e-08
        LN_EPS = 1e-05

        def layernorm(x, g, b):
            mu = jnp.mean(x, axis=-1, keepdims=True)
            var = jnp.mean((x - mu) ** 2, axis=-1, keepdims=True)
            return (x - mu) * jax.lax.rsqrt(var + LN_EPS) * g + b

        def rmsnorm(x, gamma):
            norm = jnp.sqrt(jnp.sum(x * x, axis=-1, keepdims=True)) * x.shape[-1] ** (-0.5)
            return x / jnp.maximum(norm, RMS_EPS) * gamma
        key = jax.random.key(seed)
        ks = jax.random.split(key, 12)
        b, n, m = (4, 1024, 128)
        x = jax.random.normal(ks[0], (b, n, DIM_IN), jnp.float32)
        latents = jax.random.normal(ks[1], (b, m, DIM_LAT), jnp.float32)
        mask = jax.random.randint(ks[2], (b, n), 0, 2).astype(bool)
        s = lambda k, sh, fan: jax.random.normal(k, sh, jnp.float32) * fan ** (-0.5)
        return {'x': x, 'latents': latents, 'mask': mask, 'ln_x_g': jnp.ones((DIM_IN,), jnp.float32), 'ln_x_b': jnp.zeros((DIM_IN,), jnp.float32), 'ln_l_g': jnp.ones((DIM_LAT,), jnp.float32), 'ln_l_b': jnp.zeros((DIM_LAT,), jnp.float32), 'qn_g': jnp.ones((DIM_HEAD,), jnp.float32), 'kn_g': jnp.ones((DIM_HEAD,), jnp.float32), 'Wq': s(ks[3], (INNER, DIM_LAT), DIM_LAT), 'Wkv': s(ks[4], (2 * INNER, DIM_IN), DIM_IN), 'Wlkv': s(ks[5], (2 * INNER, DIM_LAT), DIM_LAT), 'Wo': s(ks[6], (DIM_LAT, INNER), INNER), 'bo': jnp.zeros((DIM_LAT,), jnp.float32)}
    _L0_xattn_all = _L0_xattn_setup()
    _L0_xattn_in = {k: v for k, v in _L0_xattn_all.items() if k in ('ln_x_g', 'ln_x_b', 'ln_l_g', 'ln_l_b', 'qn_g', 'kn_g', 'Wq', 'Wkv', 'Wlkv', 'Wo', 'bo')}
    del _L0_xattn_all

    def _L0_ffn_setup():
        import jax, jax.numpy as jnp
        import numpy as np
        B, T, C = (4, 512, 256)
        E, I, K = (8, 352, 2)
        N_SHARED = 1
        IS = I * N_SHARED
        key = jax.random.key(seed)
        ks = jax.random.split(key, 8)
        s = 0.02
        return {'x': jax.random.normal(ks[0], (B, T, C), dtype=jnp.float32), 'Wg': jax.random.normal(ks[1], (E, C), dtype=jnp.float32) * s, 'W1': jax.random.normal(ks[2], (E, I, C), dtype=jnp.float32) * s, 'W2': jax.random.normal(ks[3], (E, I, C), dtype=jnp.float32) * s, 'W3': jax.random.normal(ks[4], (E, C, I), dtype=jnp.float32) * s, 'Ws1': jax.random.normal(ks[5], (IS, C), dtype=jnp.float32) * s, 'Ws2': jax.random.normal(ks[6], (IS, C), dtype=jnp.float32) * s, 'Ws3': jax.random.normal(ks[7], (C, IS), dtype=jnp.float32) * s}
    _L0_ffn_all = _L0_ffn_setup()
    _L0_ffn_in = {k: v for k, v in _L0_ffn_all.items() if k in ('Wg', 'W1', 'W2', 'W3', 'Ws1', 'Ws2', 'Ws3')}
    del _L0_ffn_all

    def _L1_xattn_setup():
        import jax, jax.numpy as jnp
        import numpy as np
        B, LQ, LK = (4, 512, 512)
        D1, D2, H = (256, 192, 256)
        key = jax.random.key(seed)
        ks = jax.random.split(key, 9)
        s1, s2, sh = (1.0 / np.sqrt(D1), 1.0 / np.sqrt(D2), 1.0 / np.sqrt(H))
        return {'query': jax.random.normal(ks[0], (B, LQ, D1), jnp.float32), 'key': jax.random.normal(ks[1], (B, LK, D2), jnp.float32), 'value': jax.random.normal(ks[2], (B, LK, D2), jnp.float32), 'Wq': jax.random.normal(ks[3], (D1, H), jnp.float32) * s1, 'bq': jax.random.normal(ks[4], (H,), jnp.float32) * s1, 'Wk': jax.random.normal(ks[5], (D2, H), jnp.float32) * s2, 'bk': jax.random.normal(ks[6], (H,), jnp.float32) * s2, 'Wv': jax.random.normal(ks[7], (D2, H), jnp.float32) * s2, 'bv': jax.random.normal(ks[8], (H,), jnp.float32) * s2}
    _L1_xattn_all = _L1_xattn_setup()
    _L1_xattn_in = {k: v for k, v in _L1_xattn_all.items() if k in ('Wq', 'bq', 'Wk', 'bk', 'Wv', 'bv')}
    del _L1_xattn_all

    def _L1_ffn_setup():
        import jax, jax.numpy as jnp
        import numpy as np
        B, T, E, C, H, G = (2, 512, 8, 256, 512, 16)
        key = jax.random.key(seed)
        ks = jax.random.split(key, 7)
        return {'hidden_states': jax.random.normal(ks[0], (B, T, C), jnp.float32), 'w_red': jax.random.normal(ks[1], (C, G), jnp.float32) * 0.02, 'wg': jax.random.normal(ks[2], (E, G), jnp.float32), 'W1': jax.random.normal(ks[3], (E, C, H), jnp.float32) * 0.02, 'b1': jax.random.normal(ks[4], (E, H), jnp.float32) * 0.02, 'W2': jax.random.normal(ks[5], (E, H, C), jnp.float32) * 0.02, 'b2': jax.random.normal(ks[6], (E, C), jnp.float32) * 0.02}
    _L1_ffn_all = _L1_ffn_setup()
    _L1_ffn_in = {k: v for k, v in _L1_ffn_all.items() if k in ('w_red', 'wg', 'W1', 'b1', 'W2', 'b2')}
    del _L1_ffn_all
    return {'x': x, 'ctx_768': ctx_768, 'mask_BxS2_bk0': mask_BxS2_bk0, 'g_xattn': g_xattn, 'g_ffn': g_ffn, 'L0_xattn_ln_x_g': _L0_xattn_in['ln_x_g'], 'L0_xattn_ln_x_b': _L0_xattn_in['ln_x_b'], 'L0_xattn_ln_l_g': _L0_xattn_in['ln_l_g'], 'L0_xattn_ln_l_b': _L0_xattn_in['ln_l_b'], 'L0_xattn_qn_g': _L0_xattn_in['qn_g'], 'L0_xattn_kn_g': _L0_xattn_in['kn_g'], 'L0_xattn_Wq': _L0_xattn_in['Wq'], 'L0_xattn_Wkv': _L0_xattn_in['Wkv'], 'L0_xattn_Wlkv': _L0_xattn_in['Wlkv'], 'L0_xattn_Wo': _L0_xattn_in['Wo'], 'L0_xattn_bo': _L0_xattn_in['bo'], 'L0_ffn_Wg': _L0_ffn_in['Wg'], 'L0_ffn_W1': _L0_ffn_in['W1'], 'L0_ffn_W2': _L0_ffn_in['W2'], 'L0_ffn_W3': _L0_ffn_in['W3'], 'L0_ffn_Ws1': _L0_ffn_in['Ws1'], 'L0_ffn_Ws2': _L0_ffn_in['Ws2'], 'L0_ffn_Ws3': _L0_ffn_in['Ws3'], 'L1_xattn_Wq': _L1_xattn_in['Wq'], 'L1_xattn_bq': _L1_xattn_in['bq'], 'L1_xattn_Wk': _L1_xattn_in['Wk'], 'L1_xattn_bk': _L1_xattn_in['bk'], 'L1_xattn_Wv': _L1_xattn_in['Wv'], 'L1_xattn_bv': _L1_xattn_in['bv'], 'L1_ffn_w_red': _L1_ffn_in['w_red'], 'L1_ffn_wg': _L1_ffn_in['wg'], 'L1_ffn_W1': _L1_ffn_in['W1'], 'L1_ffn_b1': _L1_ffn_in['b1'], 'L1_ffn_W2': _L1_ffn_in['W2'], 'L1_ffn_b2': _L1_ffn_in['b2']}

def reference(x, ctx_768, mask_BxS2_bk0, g_xattn, g_ffn, L0_xattn_ln_x_g, L0_xattn_ln_x_b, L0_xattn_ln_l_g, L0_xattn_ln_l_b, L0_xattn_qn_g, L0_xattn_kn_g, L0_xattn_Wq, L0_xattn_Wkv, L0_xattn_Wlkv, L0_xattn_Wo, L0_xattn_bo, L0_ffn_Wg, L0_ffn_W1, L0_ffn_W2, L0_ffn_W3, L0_ffn_Ws1, L0_ffn_Ws2, L0_ffn_Ws3, L1_xattn_Wq, L1_xattn_bq, L1_xattn_Wk, L1_xattn_bk, L1_xattn_Wv, L1_xattn_bv, L1_ffn_w_red, L1_ffn_wg, L1_ffn_W1, L1_ffn_b1, L1_ffn_W2, L1_ffn_b2):
    import jax
    import jax.numpy as jnp

    def _L0_xattn_ref(x, latents, mask, ln_x_g, ln_x_b, ln_l_g, ln_l_b, qn_g, kn_g, Wq, Wkv, Wlkv, Wo, bo):
        import jax, jax.numpy as jnp
        import numpy as np
        DIM_IN, DIM_LAT, DIM_HEAD = (192, 256, 64)
        INNER = max(DIM_LAT, DIM_IN)
        HEADS = INNER // DIM_HEAD
        SCALE = DIM_HEAD ** (-0.5)
        RMS_EPS = 1e-08
        LN_EPS = 1e-05

        def layernorm(x, g, b):
            mu = jnp.mean(x, axis=-1, keepdims=True)
            var = jnp.mean((x - mu) ** 2, axis=-1, keepdims=True)
            return (x - mu) * jax.lax.rsqrt(var + LN_EPS) * g + b

        def rmsnorm(x, gamma):
            norm = jnp.sqrt(jnp.sum(x * x, axis=-1, keepdims=True)) * x.shape[-1] ** (-0.5)
            return x / jnp.maximum(norm, RMS_EPS) * gamma
        b, n, _ = x.shape
        m = latents.shape[1]
        xn = layernorm(x, ln_x_g, ln_x_b)
        ln = layernorm(latents, ln_l_g, ln_l_b)
        q = ln @ Wq.T
        kv = jnp.concatenate([xn @ Wkv.T, ln @ Wlkv.T], axis=1)
        k, v = (kv[..., :INNER], kv[..., INNER:])
        split_heads = lambda t: t.reshape(t.shape[0], t.shape[1], HEADS, DIM_HEAD).transpose(0, 2, 1, 3)
        q, k, v = (split_heads(q), split_heads(k), split_heads(v))
        qn = rmsnorm(q, qn_g) * SCALE
        kn = rmsnorm(k, kn_g)
        attn = jnp.einsum('bhid,bhjd->bhij', qn, kn)
        full_mask = jnp.pad(mask, ((0, 0), (0, m)), constant_values=True)
        attn = jnp.where(full_mask[:, None, None, :], attn, -jnp.finfo(attn.dtype).max)
        attn = jax.nn.softmax(attn, axis=-1)
        out = jnp.einsum('bhij,bhjd->bhid', attn, v)
        out = out.transpose(0, 2, 1, 3).reshape(b, m, INNER)
        return out @ Wo.T + bo

    def _L0_ffn_ref(x, Wg, W1, W2, W3, Ws1, Ws2, Ws3):
        import jax, jax.numpy as jnp
        import numpy as np
        B, T, C = (4, 512, 256)
        E, I, K = (8, 352, 2)
        N_SHARED = 1
        IS = I * N_SHARED
        b, t, c = x.shape
        xf = x.reshape(-1, c)
        n = xf.shape[0]
        logits = xf @ Wg.T
        probs = jax.nn.softmax(logits.astype(jnp.float32), axis=-1)
        topk_p, topk_i = jax.lax.top_k(probs, K)
        topk_p = topk_p.astype(x.dtype)
        comb = jnp.zeros((n, E), dtype=x.dtype).at[jnp.arange(n)[:, None], topk_i].add(topk_p)
        g = jnp.einsum('nc,eic->nei', xf, W1)
        u = jnp.einsum('nc,eic->nei', xf, W2)
        h = jax.nn.silu(g) * u
        o = jnp.einsum('nei,eci->nec', h, W3)
        y = jnp.einsum('nec,ne->nc', o, comb).reshape(b, t, c)
        shared = jax.nn.silu(x @ Ws1.T) * (x @ Ws2.T) @ Ws3.T
        return y + shared

    def _L1_xattn_ref(query, key, value, Wq, bq, Wk, bk, Wv, bv):
        import jax, jax.numpy as jnp
        import numpy as np
        B, LQ, LK = (4, 512, 512)
        D1, D2, H = (256, 192, 256)
        q = jnp.einsum('bqd,dh->bqh', query, Wq) + bq
        k = jnp.einsum('bkd,dh->bkh', key, Wk) + bk
        v = jnp.einsum('bkd,dh->bkh', value, Wv) + bv
        scores = jnp.einsum('bqh,bkh->bqk', q, k)
        weights = jax.nn.softmax(scores, axis=-1)
        return jnp.einsum('bqk,bkh->bqh', weights, v)

    def _L1_ffn_ref(hidden_states, w_red, wg, W1, b1, W2, b2):
        import jax, jax.numpy as jnp
        import numpy as np
        B, T, E, C, H, G = (2, 512, 8, 256, 512, 16)
        b, t, c = hidden_states.shape
        x = hidden_states.reshape(-1, c)
        x_red = x @ w_red
        wg_n = wg / jnp.maximum(jnp.linalg.norm(wg, axis=1, keepdims=True), 0.0001)
        logits = x_red @ wg_n.T
        gates = jax.nn.softmax(logits, axis=1)
        scores = jnp.max(gates, axis=1)
        idx = jnp.argmax(gates, axis=1)
        h = jnp.einsum('nc,ech->neh', x, W1) + b1[None]
        h = jnp.take_along_axis(h, idx[:, None, None], axis=1)[:, 0, :]
        h = jax.nn.gelu(h, approximate=False)
        o = jnp.einsum('nh,ehc->nec', h, W2) + b2[None]
        o = jnp.take_along_axis(o, idx[:, None, None], axis=1)[:, 0, :]
        o = o * scores[:, None]
        return o.reshape(b, t, c)
    x = x + jnp.tanh(g_xattn[0]) * _L0_xattn_ref(ctx_768, _layernorm(x, axis=-1), mask_BxS2_bk0, L0_xattn_ln_x_g, L0_xattn_ln_x_b, L0_xattn_ln_l_g, L0_xattn_ln_l_b, L0_xattn_qn_g, L0_xattn_kn_g, L0_xattn_Wq, L0_xattn_Wkv, L0_xattn_Wlkv, L0_xattn_Wo, L0_xattn_bo)
    x = x + jnp.tanh(g_ffn[0]) * _L0_ffn_ref(_layernorm(x, axis=-1), L0_ffn_Wg, L0_ffn_W1, L0_ffn_W2, L0_ffn_W3, L0_ffn_Ws1, L0_ffn_Ws2, L0_ffn_Ws3)
    x = x + jnp.tanh(g_xattn[1]) * _L1_xattn_ref(_layernorm(x, axis=-1), ctx_768, ctx_768, L1_xattn_Wq, L1_xattn_bq, L1_xattn_Wk, L1_xattn_bk, L1_xattn_Wv, L1_xattn_bv)
    x = x + jnp.tanh(g_ffn[1]) * _L1_ffn_ref(_layernorm(x, axis=-1), L1_ffn_w_red, L1_ffn_wg, L1_ffn_W1, L1_ffn_b1, L1_ffn_W2, L1_ffn_b2)
    return x

_drawn_inputs = setup_inputs


def setup_inputs(seed=0):
    import zlib

    import numpy as np

    out = dict(_drawn_inputs(seed))
    spreads = {'g_ffn': (-1.0, 0.6),
     'L0_xattn_ln_x_g': (1.0, 0.589),
     'L0_xattn_ln_x_b': (0.0, 0.32),
     'L0_xattn_ln_l_g': (1.0, 0.2),
     'L0_xattn_ln_l_b': (0.0, 0.1),
     'L0_xattn_qn_g': (1.0, 0.2),
     'L0_xattn_kn_g': (1.0, 0.2),
     'L0_xattn_bo': (0.0, 0.1)}
    factors = {'L0_ffn_Wg': 7.833,
     'L0_ffn_W1': 6.881,
     'L0_ffn_W2': 6.925,
     'L0_ffn_W3': 6.925,
     'L1_xattn_bk': 64.0,
     'L1_ffn_w_red': 7.153,
     'L1_ffn_wg': 7.087,
     'L1_ffn_W1': 7.105,
     'L1_ffn_b1': 8.0,
     'L1_ffn_W2': 6.917,
     'L1_ffn_b2': 26.585,
     'L0_ffn_Ws1': 2.955,
     'L0_ffn_Ws3': 3.086}
    for name, (base, spread) in spreads.items():
        noise = np.random.default_rng([zlib.crc32(name.encode()), seed]).standard_normal(out[name].shape)
        drawn = base * np.exp(spread * noise) if base else spread * noise
        out[name] = jnp.asarray(drawn.astype(out[name].dtype))
    for name, factor in factors.items():
        out[name] = (out[name] * factor).astype(out[name].dtype)
    return out
```

```python
import numpy as np
import concourse.bass as bass
from concourse import mybir
from contextlib import ExitStack

F32 = mybir.dt.float32
F16 = mybir.dt.float16
I32 = mybir.dt.int32
U32 = mybir.dt.uint32
U8 = mybir.dt.uint8
ALU = mybir.AluOpType
ACT = mybir.ActivationFunctionType
AX = mybir.AxisListType
ds = bass.ds

P = 128
B, S, C = 16, 256, 256
DC = 192
H, D = 4, 64
T = S // P
KC = C // P
NT = B * T
NTOK = B * S
E = 8
CTX_CHUNKS = [(0, P), (P, DC - P)]
F0 = 352
F0_CHUNKS = [(0, P), (P, P), (2 * P, F0 - 2 * P)]
F1 = 512
REG = NTOK + P
SHARED = E * REG
DUMMY0 = SHARED + NTOK
DUMMY1 = E * REG
WSCALE = 64.0
ROUTED0 = 2 * NT + E
ROUTED1 = NT + E
TILES0 = ROUTED0 + NT
EPS = 1e-5
BIG = 1e30


class Chain:

    def __init__(self, eng, sem, base=0):
        self.eng, self.sem, self.base, self.n = eng, sem, base, 0

    def link(self, ins):
        self.n += 1
        ins.then_inc(self.sem, 1)
        self.eng.wait_ge(self.sem, self.base + self.n)

    def mark(self, ins):
        self.n += 1
        ins.then_inc(self.sem, 1)

    def wait(self):
        self.eng.wait_ge(self.sem, self.base + self.n)


def phase_semaphore(nc, g, name):
    g["semaphores"].append(nc.alloc_semaphore(name=name))
    return g["semaphores"][-1]


def end_of_phase(nc, g):
    nc.clear_and_free_semaphores(g["semaphores"])
    nc.all_engine_barrier()
    g["semaphores"] = []


def program(nc, a, out):
    root = ExitStack()
    with root:
        def sb(name, shape, dt=F32, ctx=root):
            return ctx.enter_context(nc.sbuf_tensor(name, shape, dt))

        def sem(name, ctx=root):
            return ctx.enter_context(nc.semaphore(name))

        def dram(name, shape, dt=F32):
            return nc.dram_tensor(name, shape, dt, kind="Internal").ap()

        g = {"semaphores": []}
        g["z0"] = dram("z0_rows", (DUMMY0 + E * P, C))
        g["y0"] = dram("y0_rows", (TILES0 * P, C))
        g["z1"] = dram("z1_rows", (DUMMY1 + E * P, C))
        g["y1"] = dram("y1_rows", (ROUTED1 * P, C))
        g["XR"] = sb("residual", [P, NT, C])
        g["ident"] = sb("ident", [P, P])
        g["ones"] = sb("ones", [P, P])
        g["triu"] = sb("strictly_upper", [P, P])
        g["headsel"] = sb("head_select", [P, 2])
        g["reviota"] = sb("reverse_iota", [P, T, E])
        g["regbase"] = sb("region_base", [P, E])
        g["mhalf"] = sb("minus_half", [P, 32])
        g["epst"] = sb("eps_tile", [P, 4])
        g["gate"] = sb("tanh_gates", [P, 4])
        g["SL0"] = sb("slots0", [P, NT, 2], I32)
        g["PR0"] = sb("probs0", [P, NT, 2])
        g["SL1"] = sb("slots1", [P, NT, 1], I32)
        g["PR1"] = sb("probs1", [P, NT, 1])
        g["RUN0"] = sb("running0", [P, E])
        g["RUN1"] = sb("running1", [P, E])
        g["tabrow"] = sb("tile_rows", [1, TILES0], I32)
        g["tabexp"] = sb("tile_experts", [1, TILES0], I32)
        g["carried"], g["carried_v"] = sem("carried_pool"), sem("carried_dve")
        g["zeros"] = sb("zero_rows", [P, C])
        with ExitStack() as l0:
            g["w13h"] = sb("w13_high", [P, KC * (E + 1) * 2 * F0], F16, l0)
            g["w13l"] = sb("w13_low", [P, KC * (E + 1) * 2 * F0], F16, l0)
            g["w2h"] = sb("w2_high", [P, 3 * (E + 1) * C], F16, l0)
            g["w2l"] = sb("w2_low", [P, 3 * (E + 1) * C], F16, l0)
            phase_constants(nc, a, g)
            end_of_phase(nc, g)
            phase_weights0(nc, a, g)
            end_of_phase(nc, g)
            phase_attn0(nc, a, g)
            end_of_phase(nc, g)
            phase_table(nc, a, g, 0)
            end_of_phase(nc, g)
            phase_experts(nc, a, g, 0)
            end_of_phase(nc, g)
        with ExitStack() as l1:
            g["v1h"] = sb("v1_high", [P, KC * E * F1], F16, l1)
            g["v1l"] = sb("v1_low", [P, KC * E * F1], F16, l1)
            g["v2h"] = sb("v2_high", [P, 4 * E * C], F16, l1)
            g["v2l"] = sb("v2_low", [P, 4 * E * C], F16, l1)
            g["b1"] = sb("b1_rows", [P, E * F1], F32, l1)
            g["b2"] = sb("b2_rows", [P, E * C], F32, l1)
            phase_weights1(nc, a, g)
            end_of_phase(nc, g)
            phase_attn1(nc, a, g)
            end_of_phase(nc, g)
            phase_table(nc, a, g, 1)
            end_of_phase(nc, g)
            phase_experts(nc, a, g, 1)
            end_of_phase(nc, g)
        phase_out(nc, a, g, out)
        end_of_phase(nc, g)


def phase_constants(nc, a, g):
    with ExitStack() as c:
        sem = lambda n: phase_semaphore(nc, g, n)
        filled, chosen, gates_in, gates_done = sem("c_filled"), sem("c_chosen"), sem("c_gates_in"), sem("c_gates_done")
        graw = c.enter_context(nc.sbuf_tensor("gates_raw", [P, 4], F32))
        with nc.Block() as block:
            @block.sync
            def _(sp):
                sp.dma_start(graw[:, 0:2], a["g_xattn"].rearrange("(o n) -> o n", o=1).to_broadcast([P, 2])).then_inc(gates_in, 16)
                sp.dma_start(graw[:, 2:4], a["g_ffn"].rearrange("(o n) -> o n", o=1).to_broadcast([P, 2])).then_inc(gates_in, 16)

            @block.scalar
            def _(act):
                act.wait_ge(gates_in, 32)
                act.activation(g["gate"][:], graw[:], ACT.Tanh).then_inc(gates_done, 1)

            @block.vector
            def _(v):
                v.memset(g["ones"][:], 1.0)
                v.memset(g["mhalf"][:], -0.5)
                v.memset(g["epst"][:], EPS)
                v.memset(g["zeros"][:], 0.0)
                v.memset(g["headsel"][:], 0.0).then_inc(filled, 1)
                v.wait_ge(filled, 1)
                v.memset(g["headsel"][0:D, 0:1], 1.0)
                v.memset(g["headsel"][D:P, 1:2], 1.0)
                for e in range(E):
                    v.memset(g["regbase"][:, e:e + 1], float(e * REG))
                    v.memset(g["RUN0"][:, e:e + 1], float(e * REG))
                    v.memset(g["RUN1"][:, e:e + 1], float(e * REG))
                    v.memset(g["reviota"][:, :, e:e + 1], float(E - e))

            @block.gpsimd
            def _(pool):
                pool.memset(g["ident"][:], 0.0).then_inc(chosen, 1)
                pool.memset(g["triu"][:], 1.0).then_inc(chosen, 1)
                pool.wait_ge(chosen, 2)
                pool.affine_select(out=g["ident"][:], in_=g["ident"][:], compare_op=ALU.not_equal, fill=1.0,
                                   base=0, pattern=[[-1, P]], channel_multiplier=1)
                pool.affine_select(out=g["triu"][:], in_=g["triu"][:], compare_op=ALU.is_gt, fill=0.0,
                                   base=0, pattern=[[1, P]], channel_multiplier=-1)


def split_weights(nc, g, name, pieces):
    with ExitStack() as c:
        sem = lambda n: phase_semaphore(nc, g, n)
        width = max(int(np.prod(s.shape)) // s.shape[0] for s, _, _ in pieces)
        NS = 3
        stage = [c.enter_context(nc.sbuf_tensor(f"{name}_stage{i}", [P, width], F32)) for i in range(NS)]
        landed = [sem(f"{name}_landed{i}") for i in range(NS)]
        high_done, low_done = sem(f"{name}_high"), sem(f"{name}_low")

        def view(i, src):
            rows, k, f = src.shape
            return stage[i % NS][0:rows, 0:k * f]

        with nc.Block() as block:
            @block.sync
            def _(sp):
                for i, (src, hi, lo) in enumerate(pieces):
                    if i >= NS:
                        sp.wait_ge(low_done, i - NS + 1)
                    sp.dma_start(view(i, src).rearrange("p (k f) -> p k f", k=src.shape[1]), src).then_inc(landed[i % NS], 16)

            @block.scalar
            def _(act):
                for i, (src, hi, lo) in enumerate(pieces):
                    act.wait_ge(landed[i % NS], 16 * (i // NS + 1))
                    act.activation(hi, view(i, src).rearrange("p (k f) -> p k f", k=src.shape[1]), ACT.Copy, scale=WSCALE).then_inc(high_done, 1)

            @block.vector
            def _(v):
                for i, (src, hi, lo) in enumerate(pieces):
                    v.wait_ge(high_done, i + 1)
                    v.scalar_tensor_tensor(lo, view(i, src).rearrange("p (k f) -> p k f", k=src.shape[1]), WSCALE, hi,
                                           ALU.mult, ALU.subtract).then_inc(low_done, 1)


def phase_weights0(nc, a, g):
    v13 = {x: g[x][:].rearrange("p (k e f) -> p k e f", k=KC, e=E + 1) for x in ("w13h", "w13l")}
    v2 = {x: g[x][:].rearrange("p (k e f) -> p k e f", k=3, e=E + 1) for x in ("w2h", "w2l")}
    pieces = []
    for e in range(E + 1):
        pieces.append((a["w13"][e].rearrange("(k p) f -> p k f", p=P), v13["w13h"][:, :, e, :], v13["w13l"][:, :, e, :]))
    for e in range(E + 1):
        pieces.append((a["w2"][e, 0:2 * P].rearrange("(k p) f -> p k f", p=P), v2["w2h"][:, 0:2, e, :], v2["w2l"][:, 0:2, e, :]))
        n = F0 - 2 * P
        pieces.append((a["w2"][e, 2 * P:F0].rearrange("(k p) f -> p k f", k=1), v2["w2h"][0:n, 2:3, e, :], v2["w2l"][0:n, 2:3, e, :]))
    split_weights(nc, g, "w0", pieces)


def phase_weights1(nc, a, g):
    u1 = {x: g[x][:].rearrange("p (k e f) -> p k e f", k=KC, e=E) for x in ("v1h", "v1l")}
    u2 = {x: g[x][:].rearrange("p (k e f) -> p k e f", k=4, e=E) for x in ("v2h", "v2l")}
    pieces = []
    for e in range(E):
        pieces.append((a["v1"][e].rearrange("(k p) f -> p k f", p=P), u1["v1h"][:, :, e, :], u1["v1l"][:, :, e, :]))
        pieces.append((a["v2"][e].rearrange("(k p) f -> p k f", p=P), u2["v2h"][:, :, e, :], u2["v2l"][:, :, e, :]))
    split_weights(nc, g, "w1", pieces)
    b_in = phase_semaphore(nc, g, "b_in")
    with nc.Block() as block:
        @block.sync
        def _(sp):
            sp.dma_start(g["b1"][:], a["b1"].rearrange("(o e) f -> o (e f)", o=1).to_broadcast([P, E * F1])).then_inc(b_in, 16)
            sp.dma_start(g["b2"][:], a["b2"].rearrange("(o e) f -> o (e f)", o=1).to_broadcast([P, E * C])).then_inc(b_in, 16)
            sp.wait_ge(b_in, 32)



def count(value):
    return max(value, 0) if isinstance(value, int) else value


def over_batches(eng, first, both, last):
    first(0, 0)
    both(0, 0)
    both(1, 1)
    with eng.Fori(2, B - 5, 2) as n:
        both(n, 0)
        both(n + 1, 1)
    for n in range(B - 4, B - 1):
        both(n, n % 2)
    last(B - 1, 1)


class Route:

    def __init__(self, nc, g, c, tag, K, SL, PR, RUN, rows, wg):
        self.nc, self.g, self.K, self.SL, self.PR, self.RUN, self.rows, self.wg = nc, g, K, SL, PR, RUN, rows, wg
        sb = lambda n, s, d=F32: c.enter_context(nc.sbuf_tensor(f"{tag}_{n}", s, d))
        sem = lambda n: phase_semaphore(nc, g, f"{tag}_{n}")
        self.mv = sb("mean_var", [P, T, 2])
        self.st = sb("stats", [P, T, 6])
        self.rstd = sb("rstd", [P, T])
        self.L = sb("logits", [P, T, E])
        self.work = sb("logits_rest", [P, T, E])
        self.eq = sb("equal", [P, T, E])
        self.m = [sb(f"max{k}", [P, T]) for k in range(2)]
        self.best = sb("best", [P, T])
        self.oh = [sb(f"onehot{k}", [P, T, E]) for k in range(K)]
        self.A = sb("assigned", [P, T, E]) if K == 2 else self.oh[0]
        self.d = sb("shifted", [P, T, E + 1])
        self.ex = sb("exps", [P, T, E + 1])
        self.sum = sb("expsum", [P, T])
        self.pos = sb("position", [P, T, E])
        self.slf = sb("slot_f", [P, T, K])
        self.idx = [sb(f"slot_idx{p}", [P, K, T], I32) for p in range(2)]
        self.z = [sb(f"z_tokens{p}", [P, T, C]) for p in range(2)]
        self.zT = sb("z_cols", [P, KC, S])
        self.stats_ready = sem("stats_ready")
        self.rstd_ready = sem("rstd_ready")
        self.z_ready = sem("z_ready")
        self.z_turned = sem("z_turned")
        self.cols_ready = sem("cols_ready")
        self.logits_ready = sem("logits_ready")
        self.shifted_ready = sem("shifted_ready")
        self.exp_ready = sem("exp_ready")
        self.assigned_ready = sem("assigned_ready")
        self.prefix_ready = sem("prefix_ready")
        self.idx_ready = sem("idx_ready")
        self.scattered = [sem(f"scattered{p}") for p in range(2)]
        self.stored = [sem(f"stored{p}") for p in range(2)]
        self.step = sem("route_step")
        self.pool_step = sem("route_pool_step")
        self.steps = 29 if K == 2 else 19
        self.zsteps = 6

    def pool_rstd(self, pool, n):
        ch = Chain(pool, self.pool_step, n * 2)
        pool.wait_ge(self.stats_ready, n + 1)
        ch.link(pool.tensor_tensor(self.rstd[:], self.mv[:, :, 1], self.g["epst"][:, 0:T], ALU.add))
        ch.mark(pool.tensor_tensor(self.rstd[:], self.rstd[:], self.g["mhalf"][:, 0:T], ALU.pow))
        ch.wait()
        pool.sem_inc(self.rstd_ready, 1)

    def vector_z(self, v, n, p, x, ch, shared):
        for t in range(T):
            ch.mark(v.bn_stats(self.st[:, t, :], x[:, t, :]))
        ch.wait()
        v.sem_inc(self.g["carried_v"], 1)
        for t in range(T):
            ins = v.bn_aggr(self.mv[:, t, :], self.st[:, t, :])
        ins.then_inc(self.stats_ready, 1)
        v.wait_ge(self.rstd_ready, n + 1)
        v.wait_ge(self.scattered[p], count((n - p) * (8 * self.K * T)))
        if shared:
            v.wait_ge(self.stored[p], count((n - p) * 8))
        for t in range(T):
            ins = v.tensor_scalar(self.z[p][:, t, :], x[:, t, :], self.mv[:, t, 0:1], self.rstd[:, t:t + 1], ALU.subtract, ALU.mult)
        ins.then_inc(self.z_ready, 1)

    def pe_turn(self, pe, n, p, bank):
        pe.wait_ge(self.z_ready, n + 1)
        for k in range(KC):
            for t in range(T):
                ins = pe.transpose(bank[:, k, t * P:(t + 1) * P], self.z[p][:, t, k * P:(k + 1) * P], self.g["ident"][:])
        ins.then_inc(self.z_turned, 1)

    def act_cols(self, act, n, bank):
        act.wait_ge(self.logits_ready, count(n))
        act.wait_ge(self.z_turned, n + 1)
        act.activation(self.zT[:], bank, ACT.Copy).then_inc(self.cols_ready, 1)

    def pe_logits(self, pe, n, bank):
        pe.wait_ge(self.cols_ready, n + 1)
        for t in range(T):
            for k in range(KC):
                ins = pe.matmul(bank[:, t, :], self.zT[:, k, t * P:(t + 1) * P], self.wg[:, k, :], start=k == 0, stop=k == KC - 1)
        ins.then_inc(self.logits_ready, 1)

    def pe_prefix(self, pe, n, bank):
        pe.wait_ge(self.assigned_ready, n + 1)
        g = self.g
        pe.matmul(bank[:, 0, :], g["triu"][:], self.A[:, 0, :], start=True, stop=True)
        pe.matmul(bank[:, 1, :], g["triu"][:], self.A[:, 1, :], start=True, stop=False)
        pe.matmul(bank[:, 1, :], g["ones"][:], self.A[:, 0, :], start=False, stop=True)
        pe.matmul(bank[:, 2, :], g["ones"][:], self.A[:, 0, :], start=True, stop=False)
        pe.matmul(bank[:, 2, :], g["ones"][:], self.A[:, 1, :], start=False, stop=True).then_inc(self.prefix_ready, 1)

    def act_exp(self, act, n):
        act.wait_ge(self.shifted_ready, n + 1)
        act.activation(self.ex[:], self.d[:], ACT.Exp).then_inc(self.exp_ready, 1)

    def vector_choose(self, v, n, p, logits, ch):
        bc = lambda x: x.unsqueeze(2).to_broadcast([P, T, E])
        v.wait_ge(self.logits_ready, n + 1)
        ch.link(v.tensor_copy(self.L[:], logits))
        src = self.L
        for k in range(self.K):
            ch.link(v.tensor_reduce(self.m[k][:], src[:], AX.X, ALU.max))
            ch.link(v.tensor_tensor(self.eq[:], src[:], bc(self.m[k][:]), ALU.is_equal))
            ch.link(v.tensor_tensor(self.eq[:], self.eq[:], self.g["reviota"][:], ALU.mult))
            ch.link(v.tensor_reduce(self.best[:], self.eq[:], AX.X, ALU.max))
            ch.link(v.tensor_tensor(self.oh[k][:], self.eq[:], bc(self.best[:]), ALU.is_equal))
            if k == 0 and self.K == 2:
                ch.link(v.scalar_tensor_tensor(self.work[:], self.oh[0][:], -BIG, self.L[:], ALU.mult, ALU.add))
                src = self.work
        if self.K == 2:
            ch.link(v.tensor_tensor(self.A[:], self.oh[0][:], self.oh[1][:], ALU.add))
        v.sem_inc(self.assigned_ready, 1)
        ch.mark(v.tensor_tensor(self.d[:, :, 0:E], self.L[:], bc(self.m[0][:]), ALU.subtract))
        ch.mark(v.tensor_tensor(self.d[:, :, E], self.m[self.K - 1][:], self.m[0][:], ALU.subtract))
        ch.wait()
        v.sem_inc(self.shifted_ready, 1)

    def vector_slots(self, v, n, p, prefix, ch):
        v.wait_ge(self.exp_ready, n + 1)
        ch.link(v.tensor_reduce(self.sum[:], self.ex[:, :, 0:E], AX.X, ALU.add))
        ch.link(v.reciprocal(self.sum[:], self.sum[:]))
        ch.mark(v.tensor_copy(self.PR[:, ds(n * T, T), 0], self.sum[:]))
        if self.K == 2:
            ch.mark(v.tensor_tensor(self.PR[:, ds(n * T, T), 1], self.sum[:], self.ex[:, :, E], ALU.mult))
        v.wait_ge(self.prefix_ready, n + 1)
        ch.link(v.tensor_tensor(self.pos[:], prefix[:, 0:T, :], self.RUN[:].unsqueeze(1).to_broadcast([P, T, E]), ALU.add))
        ch.mark(v.tensor_tensor(self.RUN[:], self.RUN[:], prefix[:, T, :], ALU.add))
        for k in range(self.K):
            ch.link(v.tensor_tensor(self.eq[:], self.oh[k][:], self.pos[:], ALU.mult))
            ch.link(v.tensor_reduce(self.slf[:, :, k], self.eq[:], AX.X, ALU.add))
        ch.mark(v.tensor_copy(self.SL[:, ds(n * T, T), :], self.slf[:]))
        ch.link(v.tensor_copy(self.idx[p][:].rearrange("p k t -> p t k"), self.slf[:]))
        v.sem_inc(self.idx_ready, 1)
        assert ch.n == self.steps, ch.n

    def pool_scatter(self, pool, n, p):
        pool.wait_ge(self.idx_ready, n + 1)
        pool.sem_inc(self.g["carried"], 1)
        for k in range(self.K):
            for t in range(T):
                pool.indirect_dma_start(self.rows, bass.IndirectOffsetOnAxis(ap=self.idx[p][:, k, t:t + 1], axis=0),
                                        self.z[p][:, t, :], None).then_inc(self.scattered[p], 16)

    def finish(self, eng, shared):
        for p in range(2):
            eng.wait_ge(self.scattered[p], (B // 2) * self.K * T * 16)
            if shared:
                eng.wait_ge(self.stored[p], (B // 2) * 16)


def phase_attn0(nc, a, g):
    NS1 = DC - P
    with ExitStack() as c:
        sb = lambda n, s, d=F32: c.enter_context(nc.sbuf_tensor(f"a0_{n}", s, d))
        pb = lambda n: c.enter_context(nc.psum_tensor(f"a0_{n}", [P, 512], F32))
        sem = lambda n: phase_semaphore(nc, g, f"a0_{n}")
        wq, wo = sb("wq", [P, KC, C]), sb("wo", [P, KC, C])
        wl, wc = sb("wlkv", [P, KC, 2 * C]), sb("wkv", [P, 2, 2 * C])
        wg = sb("wg", [P, KC, E])
        lng, lnb = sb("ln_l_g", [P, KC]), sb("ln_l_b", [P, KC])
        cng, cnb = sb("ln_x_g", [P, 2]), sb("ln_x_b", [P, 2])
        gqk, knraw = sb("qk_gain", [P, 1]), sb("kn_gain", [P, 1])
        gains, gmax, gneg = sb("gain_rows", [P, 2, D]), sb("gain_bound", [P, 1]), sb("gain_products", [P, D])
        masku, maskf, bias = sb("mask_bytes", [P, B * T], U8), sb("mask_bias", [P, B, T]), sb("latent_bias", [P, 1])
        bo = sb("bo", [P, C])
        xin = [sb(f"x_in{p}", [P, T, C]) for p in range(2)]
        cin = [sb(f"ctx_in{p}", [P, T, DC]) for p in range(2)]
        st, mv, r1, r2 = sb("stats", [P, 4, 6]), sb("mean_var", [P, 4, 2]), sb("rstd", [P, 4]), sb("rstd2", [P, 2])
        xn, cn = sb("x_norm", [P, T, C]), sb("ctx_norm", [P, T, DC])
        lT, cT = sb("lat_cols", [P, KC, S]), sb("ctx_cols", [P, 2, S])
        qs, sq = sb("q_tokens", [P, T * H, D]), sb("q_squares", [P, T * H, D])
        qn = sb("q_norm", [P, T, C])
        ksq = sb("k_squares", [P, 2, 512])
        ss = sb("square_sums", [P, 24])
        rr = [sb(f"rms_scales{p}", [P, 24]) for p in range(2)]
        qT = [sb(f"q_cols{p}", [P, 2, S]) for p in range(2)]
        kT = [sb(f"k_cols{p}", [P, 2, 512]) for p in range(2)]
        va = [sb(f"v_ones{p}", [P, 4, H, D + 1]) for p in range(2)]
        pm = [sb(f"probs{i}", [P, 4, S]) for i in range(2)]
        rs = sb("o_rsum", [P, T, H])
        on = sb("o_norm", [P, T, C])
        onT = sb("o_cols", [P, KC, S])
        xo = sb("x_mid", [P, T, C])
        BT, BC = pb("turn"), pb("turn_ctx")
        PJ = [pb("proj0"), pb("proj1")]
        SC = [pb("scores0"), pb("scores1")]
        O = [pb("out0"), pb("out1")]
        rt = Route(nc, g, c, "r0", 2, g["SL0"], g["PR0"], g["RUN0"], g["z0"], wg)

        consts_in, consts_ready, const_step, pconst = sem("consts_in"), sem("consts_ready"), sem("const_step"), sem("pool_const_step")
        landed = [sem(f"landed{p}") for p in range(2)]
        s1_stats, s1_rstd, s1_norm, s1_turned, s1_cols = (sem(f"s1_{x}") for x in ("stats", "rstd", "norm", "turned", "cols"))
        proj_ready, freed_act, freed_dve = sem("proj_ready"), sem("proj_freed_act"), sem("proj_freed_dve")
        s1_ksq, s1_ssk, s1_ss, s1_rr = (sem(f"s1_{x}") for x in ("ksq", "ssk", "ss", "rr"))
        s1_qn, s1_qturned, s1_qT = (sem(f"s1_{x}") for x in ("qn", "qturned", "qT"))
        scores, exps, pv = sem("scores"), sem("exps"), sem("pv")
        s2_on, s2_turned, s2_cols, s2_wo, s2_x1 = (sem(f"s2_{x}") for x in ("on", "turned", "cols", "wo", "x1"))
        d1, d2, p1 = sem("dve_step1"), sem("dve_step2"), sem("pool_step1")
        D1, D2, P1 = 8, 4, 8

        col = lambda x: x.rearrange("(k p) -> p k", p=P)
        loads = [(wq[:], a["wq0"].rearrange("(k p) f -> p k f", p=P)), (wo[:], a["wo0"].rearrange("(k p) f -> p k f", p=P)),
                 (wl[:], a["wlkv0"].rearrange("(k p) f -> p k f", p=P)),
                 (wc[:, 0, :], a["wkv0"][0:P]), (wc[0:NS1, 1, :], a["wkv0"][P:DC]),
                 (wg[:], a["wg0"].rearrange("(k p) e -> p k e", p=P)),
                 (bo[:], a["bo0"].rearrange("(o n) -> o n", o=1).to_broadcast([P, C])),
                 (gains[:, 0, :], a["qn"].rearrange("(o n) -> o n", o=1).to_broadcast([P, D])),
                 (gains[:, 1, :], a["kn"].rearrange("(o n) -> o n", o=1).to_broadcast([P, D])),
                 (masku[:], a["mask"])]
        small = [(lng[:, k:k + 1], a["ln_l_g"][k * P:(k + 1) * P]) for k in range(KC)] + \
                [(lnb[:, k:k + 1], a["ln_l_b"][k * P:(k + 1) * P]) for k in range(KC)] + \
                [(cng[0:n, k:k + 1], a["ln_x_g"][o:o + n]) for k, (o, n) in enumerate(CTX_CHUNKS)] + \
                [(cnb[0:n, k:k + 1], a["ln_x_b"][o:o + n]) for k, (o, n) in enumerate(CTX_CHUNKS)] + \
                [(gqk[h * D:(h + 1) * D, :], a["qn"]) for h in range(2)] + [(knraw[h * D:(h + 1) * D, :], a["kn"]) for h in range(2)]
        small = [(dst, src.rearrange("(p o) -> p o", o=1)) for dst, src in small]
        n_consts = 16 * (len(loads) + len(small))

        with nc.Block() as block:
            @block.sync
            def _(sp):
                for dst, src in loads + small:
                    sp.dma_start(dst, src).then_inc(consts_in, 16)

                def load(n, p):
                    sp.wait_ge(s2_x1, count(n - 1))
                    sp.dma_start(xin[p][:], a["x"][ds(n * S, S), :].rearrange("(t p) c -> p t c", p=P)).then_inc(landed[p], 16)
                    sp.dma_start(cin[p][:], a["ctx"][ds(n * S, S), :].rearrange("(t p) c -> p t c", p=P)).then_inc(landed[p], 16)

                def store(n, p):
                    sp.wait_ge(rt.z_ready, n + 1)
                    sp.dma_start(g["z0"][ds(n * S + SHARED, S), :].rearrange("(t p) c -> p t c", p=P), rt.z[p][:]).then_inc(rt.stored[p], 16)

                def both(n, p):
                    load(n + 1, 1 - p)
                    store(n, p)
                over_batches(sp, load, both, store)
                rt.finish(sp, True)

            @block.gpsimd
            def _(pool):
                def rstd(n):
                    ch = Chain(pool, p1, n * P1)
                    pool.wait_ge(s1_stats, n + 1)
                    ch.link(pool.tensor_tensor(r1[:], mv[:, :, 1], g["epst"][:], ALU.add))
                    ch.link(pool.tensor_tensor(r1[:], r1[:], g["mhalf"][:, 0:4], ALU.pow))
                    ch.link(pool.tensor_tensor(r2[:], mv[:, 0:T, 1], r1[:, 0:T], ALU.mult))
                    ch.link(pool.tensor_tensor(r2[:], r2[:], r1[:, 0:T], ALU.mult))
                    ch.link(pool.tensor_tensor(r2[:], r2[:], g["epst"][:, 0:T], ALU.add))
                    ch.link(pool.tensor_tensor(r2[:], r2[:], g["mhalf"][:, 0:T], ALU.pow))
                    ch.link(pool.tensor_tensor(r1[:, 0:T], r1[:, 0:T], r2[:], ALU.mult))
                    pool.sem_inc(s1_rstd, 1)
                    return ch

                def first(n, p):
                    ch = rstd(n)
                    pool.wait_ge(s1_ssk, count(n))
                    for i in range(2):
                        pool.wait_ge(freed_act, 3 * n + 2 + i)
                        ins = pool.tensor_tensor(ksq[:, i, :], kT[p][:, i, :], kT[p][:, i, :], ALU.mult)
                    ins.then_inc(s1_ksq, 1)
                    pool.wait_ge(s1_ss, n + 1)
                    pool.wait_ge(exps, count(16 * (n - 1)))
                    ch.link(pool.tensor_tensor(rr[p][:], ss[:], g["mhalf"][:, 0:24], ALU.pow))
                    pool.sem_inc(s1_rr, 1)
                    assert ch.n == P1, ch.n

                def second(n, p):
                    rt.pool_rstd(pool, n)
                    rt.pool_scatter(pool, n, p)

                def both(n, p):
                    second(n, p)
                    first(n + 1, 1 - p)
                over_batches(pool, first, both, second)

            @block.scalar
            def _(act):
                act.wait_ge(consts_ready, 1)

                def first(n, p):
                    act.wait_ge(proj_ready, count(5 * n))
                    act.wait_ge(s1_turned, n + 1)
                    for k in range(KC):
                        act.activation(lT[:, k, :], BT[:, k * S:(k + 1) * S], ACT.Identity, bias=lnb[:, k:k + 1], scale=lng[:, k:k + 1])
                    for k, (o, m) in enumerate(CTX_CHUNKS):
                        ins = act.activation(cT[0:m, k, :], BC[0:m, k * S:(k + 1) * S], ACT.Identity, bias=cnb[0:m, k:k + 1], scale=cng[0:m, k:k + 1])
                    ins.then_inc(s1_cols, 1)
                    act.wait_ge(s1_qn, count(n))
                    act.wait_ge(proj_ready, 5 * n + 1)
                    act.activation(qs[:].rearrange("p h d -> p (h d)"), PJ[p][:], ACT.Copy).then_inc(freed_act, 1)
                    act.wait_ge(scores, count(8 * (n - 1)))
                    for i in range(2):
                        act.wait_ge(proj_ready, 5 * n + 2 + i)
                        act.activation(kT[p][:, i, :], PJ[(p + 1 + i) % 2][:], ACT.Copy).then_inc(freed_act, 1)
                    act.wait_ge(s1_qturned, n + 1)
                    act.activation(qT[p][:].rearrange("p k s -> p (k s)"), BT[:], ACT.Copy, scale=gqk[:, 0:1]).then_inc(s1_qT, 1)

                def heads(n, p, h):
                    for jp in range(2):
                        if jp == 0:
                            act.wait_ge(pv, count(4 * n + h - 1 if h else 4 * n))
                        act.wait_ge(scores, 8 * n + 2 * h + jp + 1)
                        if h == 0 and jp == 0:
                            act.wait_ge(s1_rr, n + 1)
                        for j in range(2):
                            jt = jp + 2 * (1 - j)
                            b = maskf[:, ds(n, 1), jt] if jt < 2 else bias[:, 0:1]
                            act.activation(pm[h % 2][:, jt, :], SC[jp][:, j * S:(j + 1) * S], ACT.Exp, bias=b,
                                           scale=rr[p][:, 8 + jt * 4 + h:9 + jt * 4 + h]).then_inc(exps, 1)

                def tail(n, p):
                    act.wait_ge(s2_wo, count(n))
                    act.wait_ge(s2_turned, n + 1)
                    act.activation(onT[:].rearrange("p k s -> p (k s)"), O[0][:], ACT.Copy).then_inc(s2_cols, 1)
                    rt.act_cols(act, n, O[0][:].rearrange("p (k s) -> p k s", k=KC))
                    rt.act_exp(act, n)

                def second(n, p):
                    for h in range(H):
                        heads(n, p, h)
                    tail(n, p)

                def both(n, p):
                    second(n, p)
                    first(n + 1, 1 - p)
                over_batches(act, first, both, second)

            @block.vector
            def _(v):
                v.wait_ge(consts_in, n_consts)
                ch = Chain(v, const_step)
                ch.link(v.scalar_tensor_tensor(gqk[:], gqk[:], D ** -0.5, knraw[:], ALU.mult, ALU.mult))
                ch.link(v.tensor_tensor(gneg[:], gains[:, 0, :], gains[:, 1, :], ALU.mult))
                ch.link(v.tensor_reduce(gmax[:], gneg[:], AX.X, ALU.max, apply_absolute_value=True))
                ch.link(v.tensor_scalar(bias[:], gmax[:], -(D ** 0.5), None, ALU.mult))
                ch.link(v.tensor_copy(maskf[:].rearrange("p b t -> p (b t)"), masku[:]))
                ch.link(v.tensor_scalar(maskf[:], maskf[:], BIG, -BIG, ALU.mult, ALU.add))
                ch.link(v.tensor_scalar(maskf[:], maskf[:], bias[:, 0:1], None, ALU.add))
                ch.link(v.tensor_scalar(bo[:], bo[:], g["gate"][:, 0:1], None, ALU.mult))
                for p in range(2):
                    ch.mark(v.memset(va[p][:], 1.0))
                ch.wait()
                v.sem_inc(consts_ready, 3)

                def first(n, p):
                    ch = Chain(v, d1, n * D1)
                    v.wait_ge(landed[p], count((n - p) * 16 + 32))
                    for t in range(T):
                        ch.mark(v.bn_stats(st[:, t, :], xin[p][:, t, :]))
                        ch.mark(v.bn_stats(st[:, 2 + t, :], cin[p][:, t, :]))
                    ch.wait()
                    v.sem_inc(g["carried_v"], 1)
                    for t in range(4):
                        ins = v.bn_aggr(mv[:, t, :], st[:, t, :])
                    ins.then_inc(s1_stats, 1)
                    v.wait_ge(s1_turned, count(n))
                    v.wait_ge(s1_rstd, n + 1)
                    for t in range(T):
                        v.tensor_scalar(xn[:, t, :], xin[p][:, t, :], mv[:, t, 0:1], r1[:, t:t + 1], ALU.subtract, ALU.mult)
                        ins = v.tensor_scalar(cn[:, t, :], cin[p][:, t, :], mv[:, 2 + t, 0:1], r1[:, 2 + t:3 + t], ALU.subtract, ALU.mult)
                    ins.then_inc(s1_norm, 1)
                    v.wait_ge(freed_act, 3 * n + 1)
                    ch.link(v.tensor_tensor(sq[:], qs[:], qs[:], ALU.mult))
                    v.wait_ge(s1_rr, count(n))
                    ch.link(v.tensor_reduce(ss[:, 0:8], sq[:], AX.X, ALU.add))
                    ch.mark(v.tensor_scalar(ss[:, 0:8], ss[:, 0:8], 1.0 / D, 1e-16, ALU.mult, ALU.max))
                    v.wait_ge(pv, count(4 * (n - 1)))
                    for i in range(2):
                        v.wait_ge(proj_ready, 5 * n + 4 + i)
                        v.tensor_copy(va[p][:, 2 * i:2 * i + 2, :, 0:D].rearrange("p j h d -> p (j h) d"), PJ[(p + 3 + i) % 2][:].rearrange("p (x d) -> p x d", d=D)).then_inc(freed_dve, 1)
                    v.wait_ge(s1_ssk, n + 1)
                    ch.link(v.tensor_scalar(ss[:, 8:24], BC[:, 0:16], 1.0 / D, 1e-16, ALU.mult, ALU.max))
                    v.sem_inc(s1_ss, 1)
                    v.wait_ge(s1_qturned, count(n))
                    v.wait_ge(s1_rr, n + 1)
                    v.tensor_tensor(qn[:].rearrange("p t (h d) -> p (t h) d", d=D), qs[:], rr[p][:, 0:8].unsqueeze(2).to_broadcast([P, 8, D]),
                                    ALU.mult).then_inc(s1_qn, 1)
                    assert ch.n == D1, ch.n

                def second(n, p):
                    ch = Chain(v, d2, n * D2)
                    v.wait_ge(pv, 4 * n + 4)
                    ov = [O[t][:, 0:H * (D + 1)].rearrange("p (h e) -> p h e", h=H) for t in range(T)]
                    for t in range(T):
                        ch.mark(v.reciprocal(rs[:, t, :], ov[t][:, :, D]))
                    ch.wait()
                    v.wait_ge(s2_turned, count(n))
                    for t in range(T):
                        ins = v.tensor_tensor(on[:, t, :].rearrange("p (h d) -> p h d", h=H), ov[t][:, :, 0:D],
                                              rs[:, t, :].unsqueeze(2).to_broadcast([P, H, D]), ALU.mult)
                    ins.then_inc(s2_on, 1)
                    v.wait_ge(s2_wo, n + 1)
                    ch.link(v.scalar_tensor_tensor(xo[:].rearrange("p t c -> p (t c)"), O[1][:], g["gate"][:, 0:1], xin[p][:].rearrange("p t c -> p (t c)"), ALU.mult, ALU.add))
                    xr = g["XR"][:, ds(n * T, T), :]
                    ch.link(v.tensor_tensor(xr, xo[:], bo[:].unsqueeze(1).to_broadcast([P, T, C]), ALU.add))
                    v.sem_inc(s2_x1, 1)
                    ch2 = Chain(v, rt.step, n * rt.steps)
                    rt.vector_z(v, n, p, XRTile(g["XR"], n), ch2, True)
                    rt.vector_choose(v, n, p, O[1][:, 0:T * E].rearrange("p (t e) -> p t e", t=T), ch2)
                    rt.vector_slots(v, n, p, O[1][:, 128:128 + (T + 1) * E].rearrange("p (t e) -> p t e", t=T + 1), ch2)
                    assert ch.n == 4, ch.n

                def both(n, p):
                    second(n, p)
                    first(n + 1, 1 - p)
                over_batches(v, first, both, second)

            @block.tensor
            def _(pe):
                pe.wait_ge(consts_ready, 2)
                ident = g["ident"]

                def turn(n, p):
                    pe.wait_ge(s1_norm, n + 1)
                    pe.wait_ge(s1_qT, count(n))
                    pe.wait_ge(s1_ss, count(n))
                    for k in range(KC):
                        for t in range(T):
                            pe.transpose(BT[:, k * S + t * P:k * S + (t + 1) * P], xn[:, t, k * P:(k + 1) * P], ident[:])
                    for k, (o, m) in enumerate(CTX_CHUNKS):
                        for t in range(T):
                            ins = pe.transpose(BC[0:m, k * S + t * P:k * S + (t + 1) * P], cn[:, t, o:o + m], ident[:])
                    ins.then_inc(s1_turned, 1)

                def project(n, p):
                    pe.wait_ge(s1_cols, n + 1)
                    pe.wait_ge(freed_dve, count(2 * n - 1))
                    for t in range(T):
                        for k in range(KC):
                            ins = pe.matmul(PJ[p][:, t * C:(t + 1) * C], lT[:, k, t * P:(t + 1) * P], wq[:, k, :], start=k == 0, stop=k == KC - 1)
                    ins.then_inc(proj_ready, 1)
                    for i in range(2):
                        pe.wait_ge(freed_dve, count(2 * n)) if i == 0 else pe.wait_ge(freed_act, 3 * n + 1)
                        bank = PJ[(p + 1 + i) % 2]
                        for k, (o, m) in enumerate(CTX_CHUNKS):
                            pe.matmul(bank[:, 0:S], wc[0:m, k, i * P:(i + 1) * P], cT[0:m, k, :], start=k == 0, stop=k == 1)
                        for k in range(KC):
                            ins = pe.matmul(bank[:, S:2 * S], wl[:, k, i * P:(i + 1) * P], lT[:, k, :], start=k == 0, stop=k == KC - 1)
                        ins.then_inc(proj_ready, 1)
                    pe.wait_ge(freed_act, 3 * n + 2)
                    for t in range(T):
                        for k, (o, m) in enumerate(CTX_CHUNKS):
                            ins = pe.matmul(PJ[(p + 3) % 2][:, t * C:(t + 1) * C], cT[0:m, k, t * P:(t + 1) * P], wc[0:m, k, C:2 * C], start=k == 0, stop=k == 1)
                    ins.then_inc(proj_ready, 1)
                    pe.wait_ge(freed_act, 3 * n + 3)
                    for t in range(T):
                        for k in range(KC):
                            ins = pe.matmul(PJ[(p + 4) % 2][:, t * C:(t + 1) * C], lT[:, k, t * P:(t + 1) * P], wl[:, k, C:2 * C], start=k == 0, stop=k == KC - 1)
                    ins.then_inc(proj_ready, 1)

                def key_sums(n, p):
                    pe.wait_ge(s1_ksq, n + 1)
                    for jt in range(4):
                        for i in range(2):
                            ins = pe.matmul(BC[:, jt * 4 + i * 2:jt * 4 + i * 2 + 2], ksq[:, i, jt * P:(jt + 1) * P], g["headsel"][:], start=True, stop=True)
                    ins.then_inc(s1_ssk, 1)

                def turn_q(n, p):
                    pe.wait_ge(s1_qn, n + 1)
                    for i in range(2):
                        for t in range(T):
                            ins = pe.transpose(BT[:, i * S + t * P:i * S + (t + 1) * P], qn[:, t, i * P:(i + 1) * P], ident[:])
                    ins.then_inc(s1_qturned, 1)

                def first(n, p):
                    turn(n, p)
                    project(n, p)
                    key_sums(n, p)
                    turn_q(n, p)

                def score(n, p, h):
                    lo = (h % 2) * D
                    for jp in range(2):
                        i = 2 * h + jp
                        pe.wait_ge(exps, count(16 * n + 2 * i - 2 if i else 16 * n))
                        if i == 0:
                            pe.wait_ge(s1_qT, n + 1)
                            pe.wait_ge(freed_act, 3 * n + 3)
                        for j in range(2):
                            jt = jp + 2 * (1 - j)
                            ins = pe.matmul(SC[jp][:, j * S:(j + 1) * S], kT[p][lo:lo + D, h // 2, jt * P:(jt + 1) * P],
                                            qT[p][lo:lo + D, h // 2, :], start=True, stop=True)
                        ins.then_inc(scores, 1)

                def products(n, p, h):
                    if h == 0:
                        pe.wait_ge(freed_dve, 2 * n + 2)
                        pe.wait_ge(rt.cols_ready, count(n))
                        pe.wait_ge(rt.idx_ready, count(n))
                    pe.wait_ge(exps, 16 * n + 4 * h + 4)
                    for t in range(T):
                        for jt in range(4):
                            ins = pe.matmul(O[t][:, h * (D + 1):(h + 1) * (D + 1)], pm[h % 2][:, jt, t * P:(t + 1) * P], va[p][:, jt, h, :],
                                            start=jt == 0, stop=jt == 3)
                    ins.then_inc(pv, 1)

                def turn_o(n):
                    pe.wait_ge(s2_on, n + 1)
                    for k in range(KC):
                        for t in range(T):
                            ins = pe.transpose(O[0][:, k * S + t * P:k * S + (t + 1) * P], on[:, t, k * P:(k + 1) * P], ident[:])
                    ins.then_inc(s2_turned, 1)

                def project_o(n):
                    pe.wait_ge(s2_cols, n + 1)
                    for t in range(T):
                        for k in range(KC):
                            ins = pe.matmul(O[1][:, t * C:(t + 1) * C], onT[:, k, t * P:(t + 1) * P], wo[:, k, :], start=k == 0, stop=k == KC - 1)
                    ins.then_inc(s2_wo, 1)

                def second(n, p):
                    for h in range(H):
                        score(n, p, h)
                        if h:
                            products(n, p, h - 1)
                    products(n, p, H - 1)
                    turn_o(n)
                    project_o(n)
                    rt.pe_turn(pe, n, p, O[0][:].rearrange("p (k s) -> p k s", k=KC))
                    rt.pe_logits(pe, n, O[1][:, 0:T * E].rearrange("p (t e) -> p t e", t=T))
                    rt.pe_prefix(pe, n, O[1][:, 128:128 + (T + 1) * E].rearrange("p (t e) -> p t e", t=T + 1))

                def both(n, p):
                    second(n, p)
                    first(n + 1, 1 - p)
                over_batches(pe, first, both, second)


class XRTile:

    def __init__(self, xr, n):
        self.xr, self.n = xr, n

    def __getitem__(self, k):
        _, t, _ = k
        return self.xr[:, ds(self.n * T + t, 1), :].rearrange("p o c -> p (o c)")



def phase_table(nc, a, g, layer):
    RUN, routed, dummy, zd = ((g["RUN0"], ROUTED0, DUMMY0, g["z0"]), (g["RUN1"], ROUTED1, DUMMY1, g["z1"]))[layer]
    tiles = TILES0 if layer == 0 else ROUTED1
    E1 = E + 1
    with ExitStack() as c:
        sb = lambda n, s, d=F32: c.enter_context(nc.sbuf_tensor(f"t{layer}_{n}", s, d))
        sem = lambda n: phase_semaphore(nc, g, f"t{layer}_{n}")
        tiota, tf = sb("tile_iota", [P, tiles], I32), sb("tile_number", [P, tiles])
        jiota, jf = sb("fill_iota", [P, NT], I32), sb("fill", [P, NT])
        eiota, ef = sb("expert_iota", [P, E1], I32), sb("expert", [P, E1])
        cnt, more = sb("count", [P, E]), sb("more", [P, E, NT])
        nt, before, upto, base = sb("tiles_of", [P, E]), sb("tiles_before", [P, E1]), sb("tiles_upto", [P, E1]), sb("base", [P, E1])
        ge, lt = sb("after_first", [P, routed, E1]), sb("before_last", [P, routed, E1])
        row, ex, runi = sb("row", [P, tiles]), sb("ex", [P, tiles]), sb("run_int", [P, E], I32)
        iotas, step, run_ready, padded = sem("iotas"), sem("step"), sem("run_ready"), sem("padded")
        K = 2 - layer
        SL = g[f"SL{layer}"][:].rearrange("p n k -> p (n k)")
        slf, sel, less, dbase = sb("slots", [P, NT * K]), sb("slot_after", [P, NT * K, E]), sb("slot_less", [P, NT * K]), sb("base_steps", [P, E])
        with nc.Block() as block:
            @block.gpsimd
            def _(pool):
                pool.iota(tiota[:], pattern=[[1, tiles]], base=0, channel_multiplier=0).then_inc(iotas, 1)
                pool.iota(jiota[:], pattern=[[P, NT]], base=0, channel_multiplier=0).then_inc(iotas, 1)
                pool.iota(eiota[:], pattern=[[1, E1]], base=0, channel_multiplier=0).then_inc(iotas, 1)

            @block.vector
            def _(v):
                ch = Chain(v, step)
                tt = v.tensor_tensor
                ch.link(v.tensor_copy(runi[:], RUN[:]))
                v.sem_inc(run_ready, 1)
                v.wait_ge(iotas, 3)
                ch.mark(v.tensor_copy(tf[:], tiota[:]))
                ch.mark(v.tensor_copy(jf[:], jiota[:]))
                ch.mark(v.tensor_copy(ef[:], eiota[:]))
                ch.link(tt(cnt[:], RUN[:], g["regbase"][:], ALU.subtract))
                ch.link(tt(more[:], cnt[:].unsqueeze(2).to_broadcast([P, E, NT]), jf[:].unsqueeze(1).to_broadcast([P, E, NT]), ALU.is_gt))
                ch.mark(v.tensor_reduce(nt[:], more[:], AX.X, ALU.add))
                ch.mark(v.memset(before[:, 0:1], 0.0))
                ch.mark(v.memset(upto[:, E:E + 1], BIG))
                ch.wait()
                for e in range(E):
                    ch.link(tt(upto[:, e:e + 1], before[:, e:e + 1], nt[:, e:e + 1], ALU.add))
                    ch.link(v.tensor_copy(before[:, e + 1:e + 2], upto[:, e:e + 1]))
                ch.mark(v.tensor_copy(base[:, 0:E], g["regbase"][:]))
                ch.mark(v.memset(base[:, E:E1], float(dummy)))
                ch.wait()
                ch.link(v.scalar_tensor_tensor(base[:], before[:], -float(P), base[:], ALU.mult, ALU.add))
                full = [P, routed, E1]
                tb = tf[:, 0:routed].unsqueeze(2).to_broadcast(full)
                ch.mark(tt(ge[:], tb, before[:].unsqueeze(1).to_broadcast(full), ALU.is_ge))
                ch.link(tt(lt[:], tb, upto[:].unsqueeze(1).to_broadcast(full), ALU.is_lt))
                ch.link(tt(ge[:], ge[:], lt[:], ALU.mult))
                ch.link(tt(lt[:], ge[:], base[:].unsqueeze(1).to_broadcast(full), ALU.mult))
                ch.link(v.tensor_reduce(row[:, 0:routed], lt[:], AX.X, ALU.add))
                ch.link(v.scalar_tensor_tensor(row[:, 0:routed], tf[:, 0:routed], float(P), row[:, 0:routed], ALU.mult, ALU.add))
                ch.link(tt(lt[:, :, 0:E], ge[:, :, 0:E], ef[:, 0:E].unsqueeze(1).to_broadcast([P, routed, E]), ALU.mult))
                ch.link(v.tensor_reduce(ex[:, 0:routed], lt[:, :, 0:E], AX.X, ALU.add))
                if layer == 0:
                    ch.mark(v.tensor_scalar(row[:, routed:tiles], tf[:, routed:tiles], float(P), float(SHARED - P * routed), ALU.mult, ALU.add))
                    ch.link(v.memset(ex[:, routed:tiles], float(E)))
                ch.mark(v.tensor_copy(g["tabrow"][:, 0:tiles], row[0:1, :]))
                ch.link(v.tensor_copy(g["tabexp"][:, 0:tiles], ex[0:1, :]))

                ch.mark(v.tensor_copy(slf[:], SL))
                ch.mark(v.tensor_copy(dbase[:, 0:1], base[:, 0:1]))
                ch.link(tt(dbase[:, 1:E], base[:, 1:E], base[:, 0:E - 1], ALU.subtract))
                full = [P, NT * K, E]
                ch.link(tt(sel[:], slf[:].unsqueeze(2).to_broadcast(full), g["regbase"][:].unsqueeze(1).to_broadcast(full), ALU.is_ge))
                ch.link(tt(sel[:], sel[:], dbase[:].unsqueeze(1).to_broadcast(full), ALU.mult))
                ch.link(v.tensor_reduce(less[:], sel[:], AX.X, ALU.add))
                ch.link(tt(SL, slf[:], less[:], ALU.subtract))

            @block.sync
            def _(sp):
                for d in range(E):
                    sp.dma_start(zd[dummy + d * P:dummy + (d + 1) * P, :], g["zeros"][:]).then_inc(padded, 16)
                sp.wait_ge(run_ready, 1)
                for e in range(E):
                    r = sp.value_load(runi[0:1, e:e + 1], min_val=e * REG, max_val=e * REG + NTOK)
                    sp.dma_start(zd[ds(r, P), :], g["zeros"][:]).then_inc(padded, 16)
                sp.wait_ge(padded, 16 * 2 * E)


def tile_pipeline(eng, step, n):
    for s in range(-1, 4):
        step(s, s % 2)
    with eng.Fori(4, n - 3, 2) as s:
        step(s, 0)
        step(s + 1, 1)
    for s in range(n - 2, n + 2):
        step(s, s % 2)


def within(i, n):
    return not isinstance(i, int) or 0 <= i < n


def phase_experts(nc, a, g, layer):
    if layer == 0:
        tiles, F, zd, yd, EW = TILES0, F0, g["z0"], g["y0"], E + 1
        wh, wl, uh, ul, NF = g["w13h"], g["w13l"], g["w2h"], g["w2l"], 2
        chunks = F0_CHUNKS
    else:
        tiles, F, zd, yd, EW = ROUTED1, F1, g["z1"], g["y1"], E
        wh, wl, uh, ul, NF = g["v1h"], g["v1l"], g["v2h"], g["v2l"], 1
        chunks = [(k * P, P) for k in range(F1 // P)]
    NCH = len(chunks)
    HW = NCH * P
    rows = zd.shape[0]
    with ExitStack() as c:
        sb = lambda n, s, d=F32: c.enter_context(nc.sbuf_tensor(f"e{layer}_{n}", s, d))
        pb = lambda n: c.enter_context(nc.psum_tensor(f"e{layer}_{n}", [P, 512], F32))
        sem = lambda n: phase_semaphore(nc, g, f"e{layer}_{n}")
        zs = [sb(f"z_rows{p}", [P, C]) for p in range(2)]
        xh = [sb(f"z_high{p}", [P, KC, P], F16) for p in range(2)]
        xl = [sb(f"z_low{p}", [P, KC, P], F16) for p in range(2)]
        act_out = sb("act_out", [P, F])
        hs = [sb(f"hidden{p}", [P, F]) for p in range(2)]
        hh = [sb(f"hidden_high{p}", [P, NCH, P], F16) for p in range(2)]
        hl = [sb(f"hidden_low{p}", [P, NCH, P], F16) for p in range(2)]
        ys = [sb(f"y_rows{p}", [P, C]) for p in range(2)]
        ZT, HT, Y = pb("z_cols"), pb("hidden_cols"), pb("y")
        GU = [[pb(f"first{f}_{p}") for f in range(NF)] for p in range(2)]
        landed, stored = [sem(f"landed{p}") for p in range(2)], [sem(f"stored{p}") for p in range(2)]
        turned, zhigh, zlow, first_done, act_done, hidden_done = (sem(x) for x in ("turned", "zhigh", "zlow", "first_done", "act_done", "hidden_done"))
        h_turned, hhigh, hlow, y_done, y_out, blank = (sem(x) for x in ("h_turned", "hhigh", "hlow", "y_done", "y_out", "blank"))
        biased = sem("biased")

        def expert(eng, i):
            return eng.value_load(g["tabexp"][0:1, ds(i, 1)], min_val=0, max_val=EW - 1)

        with nc.Block() as block:
            @block.sync
            def _(sp):
                def row(i):
                    return sp.value_load(g["tabrow"][0:1, ds(i, 1)], min_val=0, max_val=rows - P)

                def step(s, q):
                    i, p = s + 1, 1 - q
                    if within(i, tiles):
                        r = row(i)
                        sp.wait_ge(turned, count(i - 1))
                        sp.dma_start(zs[p][:], zd[ds(r, P), :]).then_inc(landed[p], 16)
                    i, p = s - 2, q
                    if within(i, tiles):
                        sp.wait_ge(y_out, i + 1)
                        sp.dma_start(yd[ds(i * P, P), :], ys[p][:]).then_inc(stored[p], 16)
                tile_pipeline(sp, step, tiles)
                for p in range(2):
                    sp.wait_ge(stored[p], 8 * tiles)

            @block.tensor
            def _(pe):
                pe.wait_ge(blank, 1)

                def step(s, q):
                    i, p = s + 1, 1 - q
                    if within(i, tiles):
                        pe.wait_ge(landed[p], count((i - p) * 8 + 16))
                        pe.wait_ge(zlow, count(i))
                        for k in range(KC):
                            ins = pe.transpose(ZT[:, k * P:(k + 1) * P], zs[p][:, k * P:(k + 1) * P], g["ident"][:])
                        ins.then_inc(turned, 1)
                    i, p = s, q
                    if within(i, tiles):
                        e = expert(pe, i)
                        pe.wait_ge(hidden_done, count(i - 1))
                        pe.wait_ge(zlow, i + 1)
                        for k in range(KC):
                            for x, w in ((xh, wh), (xh, wl), (xl, wh)):
                                for f in range(NF):
                                    off = e * (NF * F) + (k * EW * NF * F + f * F)
                                    ins = pe.matmul(GU[p][f][:, 0:F], x[p][:, k, :], w[:, ds(off, F)],
                                                    start=(k == 0 and x is xh and w is wh), stop=(k == KC - 1 and x is xl))
                        ins.then_inc(first_done, 1)
                    i, p = s - 2, q
                    if within(i, tiles):
                        e = expert(pe, i)
                        pe.wait_ge(y_out, count(i))
                        pe.wait_ge(hlow, i + 1)
                        for n, (o, m) in enumerate(chunks):
                            for x, w in ((hh, uh), (hh, ul), (hl, uh)):
                                ins = pe.matmul(Y[:, 0:C], x[p][0:m, n, :], w[0:m, ds(e * C + n * EW * C, C)],
                                                start=(n == 0 and x is hh and w is uh), stop=(n == NCH - 1 and x is hl))
                        ins.then_inc(y_done, 1)
                    i, p = s - 1, 1 - q
                    if within(i, tiles):
                        pe.wait_ge(hlow, count(i))
                        pe.wait_ge(hidden_done, i + 1)
                        for n, (o, m) in enumerate(chunks):
                            ins = pe.transpose(HT[0:m, n * P:(n + 1) * P], hs[p][:, o:o + m], g["ident"][:])
                        ins.then_inc(h_turned, 1)
                tile_pipeline(pe, step, tiles)

            @block.scalar
            def _(act):
                def step(s, q):
                    i, p = s + 1, 1 - q
                    if within(i, tiles):
                        act.wait_ge(first_done, count(i - 1))
                        act.wait_ge(turned, i + 1)
                        act.activation(xh[p][:].rearrange("p k s -> p (k s)"), ZT[:, 0:KC * P], ACT.Copy).then_inc(zhigh, 1)
                    i, p = s, q
                    if within(i, tiles):
                        if layer == 0:
                            act.wait_ge(hidden_done, count(i))
                            act.wait_ge(first_done, i + 1)
                            act.activation(act_out[:], GU[p][0][:, 0:F], ACT.Silu, scale=1.0 / WSCALE).then_inc(act_done, 1)
                        else:
                            act.wait_ge(h_turned, count(i - 1))
                            act.wait_ge(biased, i + 1)
                            act.activation(hs[p][:], act_out[:], ACT.Gelu).then_inc(hidden_done, 1)
                    i, p = s - 2, q
                    if within(i, tiles) and layer == 0:
                        act.wait_ge(stored[p], count((i - p) * 8))
                        act.wait_ge(y_done, i + 1)
                        act.activation(ys[p][:], Y[:, 0:C], ACT.Copy, scale=1.0 / WSCALE).then_inc(y_out, 1)
                    i, p = s - 1, 1 - q
                    if within(i, tiles):
                        act.wait_ge(y_done, count(i - 1))
                        act.wait_ge(h_turned, i + 1)
                        act.activation(hh[p][:].rearrange("p k s -> p (k s)"), HT[:, 0:HW], ACT.Copy).then_inc(hhigh, 1)
                tile_pipeline(act, step, tiles)

            @block.vector
            def _(v):
                v.memset(HT[:], 0.0).then_inc(blank, 1)

                def step(s, q):
                    i, p = s + 1, 1 - q
                    if within(i, tiles):
                        v.wait_ge(first_done, count(i - 1))
                        v.wait_ge(zhigh, i + 1)
                        v.tensor_tensor(xl[p][:].rearrange("p k s -> p (k s)"), ZT[:, 0:KC * P], xh[p][:].rearrange("p k s -> p (k s)"), ALU.subtract).then_inc(zlow, 1)
                    i, p = s, q
                    if within(i, tiles):
                        if layer == 0:
                            v.wait_ge(h_turned, count(i - 1))
                            v.wait_ge(act_done, i + 1)
                            v.scalar_tensor_tensor(hs[p][:], GU[p][1][:, 0:F], 1.0 / WSCALE, act_out[:], ALU.mult, ALU.mult).then_inc(hidden_done, 1)
                        else:
                            e = expert(v, i)
                            v.wait_ge(hidden_done, count(i))
                            v.wait_ge(first_done, i + 1)
                            v.scalar_tensor_tensor(act_out[:], GU[p][0][:, 0:F], 1.0 / WSCALE, g["b1"][:, ds(e * F, F)], ALU.mult, ALU.add).then_inc(biased, 1)
                    i, p = s - 2, q
                    if within(i, tiles) and layer == 1:
                        e = expert(v, i)
                        v.wait_ge(stored[p], count((i - p) * 8))
                        v.wait_ge(y_done, i + 1)
                        v.scalar_tensor_tensor(ys[p][:], Y[:, 0:C], 1.0 / WSCALE, g["b2"][:, ds(e * C, C)], ALU.mult, ALU.add).then_inc(y_out, 1)
                    i, p = s - 1, 1 - q
                    if within(i, tiles):
                        v.wait_ge(y_done, count(i - 1))
                        v.wait_ge(hhigh, i + 1)
                        v.tensor_tensor(hl[p][:].rearrange("p k s -> p (k s)"), HT[:, 0:HW], hh[p][:].rearrange("p k s -> p (k s)"), ALU.subtract).then_inc(hlow, 1)
                tile_pipeline(v, step, tiles)


def gather(pool, idx, k, t, rows, dst, done):
    pool.indirect_dma_start(dst, None, rows, bass.IndirectOffsetOnAxis(ap=idx[:, k, t:t + 1], axis=0)).then_inc(done, 16)


def phase_attn1(nc, a, g):
    with ExitStack() as c:
        sb = lambda n, s, d=F32: c.enter_context(nc.sbuf_tensor(f"a1_{n}", s, d))
        pb = lambda n: c.enter_context(nc.psum_tensor(f"a1_{n}", [P, 512], F32))
        sem = lambda n: phase_semaphore(nc, g, f"a1_{n}")
        wq, wk, wv = sb("wq", [P, KC, C]), sb("wk", [P, 2, C]), sb("wv", [P, 2, C])
        bq, bk, bv = sb("bq", [P, KC]), sb("bk", [P, KC]), sb("bv", [P, C])
        w_red, wg1, wgn, wg = sb("w_red", [16, C]), sb("wg1", [E, 16]), sb("wg_norm", [16, E]), sb("wg_joint", [P, KC, E])
        wsq, wnorm = sb("wg_squares", [E, 16]), sb("wg_norms", [E, 1])
        idx = [sb(f"slots{p}", [P, 2, T], I32) for p in range(2)]
        pr = [sb(f"probs_chosen{p}", [P, T, 2]) for p in range(2)]
        yk = [sb(f"y_chosen{p}", [P, 2, T, C]) for p in range(2)]
        ysh = [sb(f"y_shared{p}", [P, T, C]) for p in range(2)]
        cin = [sb(f"ctx_in{p}", [P, T, DC]) for p in range(2)]
        x2 = [sb(f"x2_{p}", [P, T, C]) for p in range(2)]
        st, mv, r1 = sb("stats", [P, T, 6]), sb("mean_var", [P, T, 2]), sb("rstd", [P, T])
        xn = sb("x_norm", [P, T, C])
        lT, cT = sb("x_cols", [P, KC, S]), sb("ctx_cols", [P, 2, S])
        qT = [sb(f"q_cols{p}", [P, KC, S]) for p in range(2)]
        kT = [sb(f"k_cols{p}", [P, KC, S]) for p in range(2)]
        vt = [sb(f"v_tokens{p}", [P, T, C]) for p in range(2)]
        nmax, esum, rs = sb("minus_max", [P, T]), sb("exp_sum", [P, T]), sb("exp_rsum", [P, T])
        pm, pT = sb("probs", [P, T, S]), sb("prob_cols", [P, T, S])
        BT, BC = pb("turn"), pb("turn_ctx")
        PJ = [pb("proj0"), pb("proj1")]
        SC, PT, O, R = pb("scores"), pb("prob_turn"), pb("out"), pb("route")
        rt = Route(nc, g, c, "r1", 1, g["SL1"], g["PR1"], g["RUN1"], g["z1"], wg)

        consts_in, consts_ready, cstep, wg_turned, wg_norms = (sem(x) for x in ("consts_in", "consts_ready", "cstep", "wg_turned", "wg_norms"))
        landed = [sem(f"landed{p}") for p in range(2)]
        gathered = [sem(f"gathered{p}") for p in range(2)]
        slots_ready, s1_x2, s1_stats, s1_rstd, s1_norm, s1_turned, s1_cols = (sem(f"s1_{x}") for x in ("slots", "x2", "stats", "rstd", "norm", "turned", "cols"))
        proj_ready, freed_act, freed_dve = sem("proj_ready"), sem("proj_freed_act"), sem("proj_freed_dve")
        scored, maxed, expd, p_turned, p_cols, pv, x3 = (sem(x) for x in ("scored", "maxed", "expd", "p_turned", "p_cols", "pv", "x3"))
        d1, d2, p1 = sem("dve_step1"), sem("dve_step2"), sem("pool_step1")
        D1, D2, P1 = 7, 4, 2
        loads = [(wq[:], a["wq1"].rearrange("(k p) f -> p k f", p=P)),
                 (wk[:, 0, :], a["wk1"][0:P]), (wk[0:DC - P, 1, :], a["wk1"][P:DC]),
                 (wv[:, 0, :], a["wv1"][0:P]), (wv[0:DC - P, 1, :], a["wv1"][P:DC]),
                 (bv[:], a["bv1"].rearrange("(o n) -> o n", o=1).to_broadcast([P, C])),
                 (w_red[:], a["w_red"]), (wg1[:], a["wg1"])] + \
                [(t[:, k:k + 1], a[n][k * P:(k + 1) * P].rearrange("(p o) -> p o", o=1)) for t, n in ((bq, "bq1"), (bk, "bk1")) for k in range(KC)]
        n_consts = 16 * len(loads)

        with nc.Block() as block:
            @block.sync
            def _(sp):
                for dst, src in loads:
                    sp.dma_start(dst, src).then_inc(consts_in, 16)

                def load(n, p):
                    sp.wait_ge(s1_norm, count(n - 1))
                    sp.dma_start(ysh[p][:], g["y0"][ds(n * S + ROUTED0 * P, S), :].rearrange("(t p) c -> p t c", p=P)).then_inc(landed[p], 16)
                    sp.wait_ge(s1_turned, count(n - 1))
                    sp.dma_start(cin[p][:], a["ctx"][ds(n * S, S), :].rearrange("(t p) c -> p t c", p=P)).then_inc(landed[p], 16)

                def both(n, p):
                    load(n + 1, 1 - p)
                over_batches(sp, load, both, lambda n, p: None)
                rt.finish(sp, False)

            @block.gpsimd
            def _(pool):
                pool.wait_ge(wg_norms, 1)
                pool.tensor_tensor(wnorm[:], wnorm[:], g["mhalf"][0:E, 0:1], ALU.pow).then_inc(wg_norms, 1)

                def fetch(n, p):
                    pool.wait_ge(slots_ready, n + 1)
                    pool.sem_inc(g["carried"], 1)
                    for k in range(2):
                        for t in range(T):
                            gather(pool, idx[p], k, t, g["y0"], yk[p][:, k, t, :], gathered[p])

                def first(n, p):
                    ch = Chain(pool, p1, n * P1)
                    pool.wait_ge(s1_stats, n + 1)
                    ch.link(pool.tensor_tensor(r1[:], mv[:, :, 1], g["epst"][:, 0:T], ALU.add))
                    ch.link(pool.tensor_tensor(r1[:], r1[:], g["mhalf"][:, 0:T], ALU.pow))
                    pool.sem_inc(s1_rstd, 1)
                    assert ch.n == P1

                def second(n, p):
                    rt.pool_rstd(pool, n)
                    rt.pool_scatter(pool, n, p)

                def start(n, p):
                    fetch(0, 0)
                    fetch(1, 1)
                    first(0, 0)
                    fetch(2, 0)

                def both(n, p):
                    second(n, p)
                    first(n + 1, 1 - p)
                    if within(n + 3, B):
                        fetch(n + 3, 1 - p)
                over_batches(pool, start, both, second)

            @block.scalar
            def _(act):
                act.wait_ge(consts_ready, 1)

                def first(n, p):
                    act.wait_ge(proj_ready, count(3 * n))
                    act.wait_ge(s1_turned, n + 1)
                    act.activation(lT[:].rearrange("p k s -> p (k s)"), BT[:], ACT.Copy)
                    for k, (o, m) in enumerate(CTX_CHUNKS):
                        ins = act.activation(cT[0:m, k, :], BC[0:m, k * S:(k + 1) * S], ACT.Copy)
                    ins.then_inc(s1_cols, 1)
                    act.wait_ge(scored, count(n - 1))
                    for i, (dst, b) in enumerate(((qT, bq), (kT, bk))):
                        act.wait_ge(proj_ready, 3 * n + 1 + i)
                        for k in range(KC):
                            ins = act.activation(dst[p][:, k, :], PJ[i][:, k * S:(k + 1) * S], ACT.Identity, bias=b[:, k:k + 1])
                        ins.then_inc(freed_act, 1)

                def second(n, p):
                    act.wait_ge(p_turned, count(n))
                    act.wait_ge(maxed, n + 1)
                    for t in range(T):
                        ins = act.activation(pm[:, t, :], SC[:, t * S:(t + 1) * S], ACT.Exp, bias=nmax[:, t:t + 1], accum_out=esum[:, t:t + 1])
                    ins.then_inc(expd, 1)
                    act.wait_ge(pv, count(n))
                    act.wait_ge(p_turned, n + 1)
                    act.activation(pT[:].rearrange("p j s -> p (j s)"), PT[:], ACT.Copy).then_inc(p_cols, 1)
                    rt.act_cols(act, n, O[:].rearrange("p (k s) -> p k s", k=KC))
                    rt.act_exp(act, n)

                def both(n, p):
                    second(n, p)
                    first(n + 1, 1 - p)
                over_batches(act, first, both, second)

            @block.vector
            def _(v):
                v.wait_ge(consts_in, n_consts)
                ch = Chain(v, cstep)
                ch.link(v.tensor_tensor(wsq[:], wg1[:], wg1[:], ALU.mult))
                ch.link(v.tensor_reduce(wnorm[:], wsq[:], AX.X, ALU.add))
                ch.link(v.tensor_scalar(wnorm[:], wnorm[:], 1e-8, None, ALU.max))
                v.sem_inc(wg_norms, 1)
                v.wait_ge(wg_norms, 2)
                ch.link(v.tensor_scalar(wg1[:], wg1[:], wnorm[:, 0:1], None, ALU.mult))
                v.sem_inc(consts_ready, 1)
                v.wait_ge(wg_turned, 1)
                ch.link(v.tensor_copy(wgn[:], R[0:16, 0:E]))
                v.sem_inc(consts_ready, 1)
                v.wait_ge(wg_turned, 2)
                ch.link(v.tensor_copy(wg[:].rearrange("p k e -> p (k e)"), R[:, 16:16 + KC * E]))
                v.sem_inc(consts_ready, 1)

                def slots(n, p):
                    v.wait_ge(gathered[p], count((n - p) * 32))
                    v.tensor_copy(pr[p][:], g["PR0"][:, ds(n * T, T), :])
                    v.tensor_copy(idx[p][:].rearrange("p k t -> p t k"), g["SL0"][:, ds(n * T, T), :]).then_inc(slots_ready, 1)

                def first(n, p):
                    ch = Chain(v, d1, n * D1)
                    v.wait_ge(landed[p], count((n - p) * 16 + 32))
                    v.wait_ge(gathered[p], count((n - p) * 32 + 64))
                    for t in range(T):
                        ch.mark(v.scalar_tensor_tensor(ysh[p][:, t, :], yk[p][:, 0, t, :], pr[p][:, t, 0:1], ysh[p][:, t, :], ALU.mult, ALU.add))
                    ch.wait()
                    for t in range(T):
                        ch.mark(v.scalar_tensor_tensor(ysh[p][:, t, :], yk[p][:, 1, t, :], pr[p][:, t, 1:2], ysh[p][:, t, :], ALU.mult, ALU.add))
                    ch.wait()
                    v.wait_ge(x3, count(n - 1))
                    ch.link(v.scalar_tensor_tensor(x2[p][:], ysh[p][:], g["gate"][:, 2:3], g["XR"][:, ds(n * T, T), :], ALU.mult, ALU.add))
                    for t in range(T):
                        ch.mark(v.bn_stats(st[:, t, :], x2[p][:, t, :]))
                    ch.wait()
                    v.sem_inc(g["carried_v"], 1)
                    for t in range(T):
                        ins = v.bn_aggr(mv[:, t, :], st[:, t, :])
                    ins.then_inc(s1_stats, 1)
                    v.wait_ge(s1_turned, count(n))
                    v.wait_ge(s1_rstd, n + 1)
                    for t in range(T):
                        ins = v.tensor_scalar(xn[:, t, :], x2[p][:, t, :], mv[:, t, 0:1], r1[:, t:t + 1], ALU.subtract, ALU.mult)
                    ins.then_inc(s1_norm, 1)
                    v.wait_ge(pv, count(n - 1))
                    v.wait_ge(proj_ready, 3 * n + 3)
                    v.tensor_tensor(vt[p][:], PJ[0][:].rearrange("p (t c) -> p t c", t=T), bv[:].unsqueeze(1).to_broadcast([P, T, C]), ALU.add).then_inc(freed_dve, 1)

                def second(n, p):
                    ch = Chain(v, d2, n * D2)
                    v.wait_ge(expd, count(n))
                    v.wait_ge(scored, n + 1)
                    v.tensor_reduce(nmax[:], SC[:].rearrange("p (t s) -> p t s", t=T), AX.X, ALU.max, negate=True).then_inc(maxed, 1)
                    v.wait_ge(expd, n + 1)
                    ch.link(v.reciprocal(rs[:], esum[:]))
                    ch.link(v.tensor_scalar(rs[:], rs[:], g["gate"][:, 1:2], None, ALU.mult))
                    v.wait_ge(pv, n + 1)
                    xr = XRTile(g["XR"], n)
                    for t in range(T):
                        ch.mark(v.scalar_tensor_tensor(xr[:, t, :], O[:, t * C:(t + 1) * C], rs[:, t:t + 1], x2[p][:, t, :], ALU.mult, ALU.add))
                    ch.wait()
                    v.sem_inc(x3, 1)
                    assert ch.n == D2, ch.n
                    ch2 = Chain(v, rt.step, n * rt.steps)
                    rt.vector_z(v, n, p, xr, ch2, False)
                    rt.vector_choose(v, n, p, R[:, 0:T * E].rearrange("p (t e) -> p t e", t=T), ch2)
                    rt.vector_slots(v, n, p, R[:, 128:128 + (T + 1) * E].rearrange("p (t e) -> p t e", t=T + 1), ch2)

                def start(n, p):
                    slots(0, 0)
                    slots(1, 1)
                    first(0, 0)
                    slots(2, 0)

                def both(n, p):
                    second(n, p)
                    first(n + 1, 1 - p)
                    if within(n + 3, B):
                        slots(n + 3, 1 - p)
                over_batches(v, start, both, second)

            @block.tensor
            def _(pe):
                ident = g["ident"]
                pe.wait_ge(consts_ready, 1)
                pe.transpose(R[0:16, 0:E], wg1[:], ident[0:E, 0:E]).then_inc(wg_turned, 1)
                pe.wait_ge(consts_ready, 2)
                for k in range(KC):
                    ins = pe.matmul(R[:, 16 + k * E:16 + (k + 1) * E], w_red[:, k * P:(k + 1) * P], wgn[:], start=True, stop=True)
                ins.then_inc(wg_turned, 1)
                pe.wait_ge(consts_ready, 3)

                def first(n, p):
                    pe.wait_ge(s1_norm, n + 1)
                    pe.wait_ge(s1_cols, count(n))
                    for k in range(KC):
                        for t in range(T):
                            pe.transpose(BT[:, k * S + t * P:k * S + (t + 1) * P], xn[:, t, k * P:(k + 1) * P], ident[:])
                    for k, (o, m) in enumerate(CTX_CHUNKS):
                        for t in range(T):
                            ins = pe.transpose(BC[0:m, k * S + t * P:k * S + (t + 1) * P], cin[p][:, t, o:o + m], ident[:])
                    ins.then_inc(s1_turned, 1)
                    pe.wait_ge(s1_cols, n + 1)
                    pe.wait_ge(freed_dve, count(n))
                    for i in range(KC):
                        for k in range(KC):
                            ins = pe.matmul(PJ[0][:, i * S:(i + 1) * S], wq[:, k, i * P:(i + 1) * P], lT[:, k, :], start=k == 0, stop=k == KC - 1)
                    ins.then_inc(proj_ready, 1)
                    pe.wait_ge(freed_act, count(2 * n))
                    for i in range(KC):
                        for k, (o, m) in enumerate(CTX_CHUNKS):
                            ins = pe.matmul(PJ[1][:, i * S:(i + 1) * S], wk[0:m, k, i * P:(i + 1) * P], cT[0:m, k, :], start=k == 0, stop=k == 1)
                    ins.then_inc(proj_ready, 1)
                    pe.wait_ge(freed_act, 2 * n + 1)
                    for t in range(T):
                        for k, (o, m) in enumerate(CTX_CHUNKS):
                            ins = pe.matmul(PJ[0][:, t * C:(t + 1) * C], cT[0:m, k, t * P:(t + 1) * P], wv[0:m, k, :], start=k == 0, stop=k == 1)
                    ins.then_inc(proj_ready, 1)

                def second(n, p):
                    pe.wait_ge(freed_act, 2 * n + 2)
                    pe.wait_ge(expd, count(n))
                    for t in range(T):
                        for k in range(KC):
                            ins = pe.matmul(SC[:, t * S:(t + 1) * S], qT[p][:, k, t * P:(t + 1) * P], kT[p][:, k, :], start=k == 0, stop=k == KC - 1)
                    ins.then_inc(scored, 1)
                    pe.wait_ge(p_cols, count(n))
                    pe.wait_ge(expd, n + 1)
                    for j in range(T):
                        for t in range(T):
                            ins = pe.transpose(PT[:, j * S + t * P:j * S + (t + 1) * P], pm[:, t, j * P:(j + 1) * P], ident[:])
                    ins.then_inc(p_turned, 1)
                    pe.wait_ge(rt.cols_ready, count(n))
                    pe.wait_ge(freed_dve, n + 1)
                    pe.wait_ge(p_cols, n + 1)
                    for t in range(T):
                        for j in range(T):
                            ins = pe.matmul(O[:, t * C:(t + 1) * C], pT[:, j, t * P:(t + 1) * P], vt[p][:, j, :], start=j == 0, stop=j == T - 1)
                    ins.then_inc(pv, 1)
                    rt.pe_turn(pe, n, p, O[:].rearrange("p (k s) -> p k s", k=KC))
                    pe.wait_ge(rt.idx_ready, count(n))
                    rt.pe_logits(pe, n, R[:, 0:T * E].rearrange("p (t e) -> p t e", t=T))
                    rt.pe_prefix(pe, n, R[:, 128:128 + (T + 1) * E].rearrange("p (t e) -> p t e", t=T + 1))

                def both(n, p):
                    second(n, p)
                    first(n + 1, 1 - p)
                over_batches(pe, first, both, second)


def phase_out(nc, a, g, out):
    with ExitStack() as c:
        sb = lambda n, s, d=F32: c.enter_context(nc.sbuf_tensor(f"o_{n}", s, d))
        sem = lambda n: phase_semaphore(nc, g, f"o_{n}")
        NB = 4
        prs = sb("scaled_probs", [P, NT])
        idx = [sb(f"slots{p}", [P, 1, T], I32) for p in range(NB)]
        y = [sb(f"y{p}", [P, T, C]) for p in range(NB)]
        o = [sb(f"x4_{p}", [P, T, C]) for p in range(NB)]
        pb = [sb(f"scale{p}", [P, T]) for p in range(NB)]
        scaled, slots_ready, done = sem("scaled"), sem("slots_ready"), sem("done")
        gathered, stored = [sem(f"gathered{p}") for p in range(NB)], [sem(f"stored{p}") for p in range(NB)]
        with nc.Block() as block:
            @block.vector
            def _(v):
                v.tensor_scalar(prs[:], g["PR1"][:].rearrange("p n o -> p (n o)"), g["gate"][:, 3:4], None, ALU.mult).then_inc(scaled, 1)
                v.wait_ge(scaled, 1)

                def slots(n, p):
                    v.wait_ge(done, count(n - NB + 1))
                    v.tensor_copy(pb[p][:], prs[:, ds(n * T, T)])
                    v.tensor_copy(idx[p][:].rearrange("p k t -> p t k"), g["SL1"][:, ds(n * T, T), :]).then_inc(slots_ready, 1)

                def add(n, p):
                    v.wait_ge(slots_ready, n + 1)
                    v.wait_ge(stored[p], count((n - p) * (16 // NB)))
                    v.wait_ge(gathered[p], count((n - p) * (32 // NB) + 32))
                    for t in range(T):
                        ins = v.scalar_tensor_tensor(o[p][:, t, :], y[p][:, t, :], pb[p][:, t:t + 1], XRTile(g["XR"], n)[:, t, :], ALU.mult, ALU.add)
                    ins.then_inc(done, 1)
                for p in range(NB):
                    slots(p, p)
                for p in range(NB):
                    add(p, p)
                    slots(p + NB, p)
                with v.Fori(NB, B - 2 * NB + 1, NB) as n:
                    for p in range(NB):
                        add(n + p, p)
                        slots(n + p + NB, p)
                for p in range(NB):
                    add(B - NB + p, p)

            @block.gpsimd
            def _(pool):
                with pool.Fori(0, B - NB + 1, NB) as n:
                    for p in range(NB):
                        pool.wait_ge(slots_ready, n + p + 1)
                        pool.sem_inc(g["carried"], 1)
                        for t in range(T):
                            gather(pool, idx[p], 0, t, g["y1"], y[p][:, t, :], gathered[p])

            @block.sync
            def _(sp):
                with sp.Fori(0, B - NB + 1, NB) as n:
                    for p in range(NB):
                        sp.wait_ge(done, n + p + 1)
                        sp.dma_start(out[ds((n + p) * S, S), :].rearrange("(t p) c -> p t c", p=P), o[p][:]).then_inc(stored[p], 16)
                for p in range(NB):
                    sp.wait_ge(stored[p], B // NB * 16)


def lay_out(inputs):
    i = {k: np.asarray(v) for k, v in inputs.items()}
    T_ = lambda x: np.ascontiguousarray(np.swapaxes(x, -1, -2))
    return {
        "x": i["x"].reshape(NTOK, C), "ctx": i["ctx_768"].reshape(NTOK, DC),
        "mask": np.ascontiguousarray(i["mask_BxS2_bk0"].reshape(B * T, P).T),
        "g_xattn": i["g_xattn"], "g_ffn": i["g_ffn"],
        "ln_x_g": i["L0_xattn_ln_x_g"], "ln_x_b": i["L0_xattn_ln_x_b"], "ln_l_g": i["L0_xattn_ln_l_g"], "ln_l_b": i["L0_xattn_ln_l_b"],
        "qn": i["L0_xattn_qn_g"], "kn": i["L0_xattn_kn_g"],
        "wq0": T_(i["L0_xattn_Wq"]), "wkv0": T_(i["L0_xattn_Wkv"]), "wlkv0": T_(i["L0_xattn_Wlkv"]), "wo0": T_(i["L0_xattn_Wo"]), "bo0": i["L0_xattn_bo"],
        "wg0": T_(i["L0_ffn_Wg"]),
        "w13": np.concatenate([np.concatenate([T_(i["L0_ffn_W1"]), T_(i["L0_ffn_Ws1"])[None]]),
                               np.concatenate([T_(i["L0_ffn_W2"]), T_(i["L0_ffn_Ws2"])[None]])], axis=2),
        "w2": np.concatenate([T_(i["L0_ffn_W3"]), T_(i["L0_ffn_Ws3"])[None]]),
        "wq1": i["L1_xattn_Wq"], "bq1": i["L1_xattn_bq"], "wk1": i["L1_xattn_Wk"], "bk1": i["L1_xattn_bk"],
        "wv1": i["L1_xattn_Wv"], "bv1": i["L1_xattn_bv"],
        "w_red": T_(i["L1_ffn_w_red"]), "wg1": i["L1_ffn_wg"],
        "v1": i["L1_ffn_W1"], "b1": i["L1_ffn_b1"], "v2": i["L1_ffn_W2"], "b2": i["L1_ffn_b2"],
    }


def kernel(**inputs):
    import concourse.bacc as bacc
    from concourse.bass_utils import run_bass_kernel_spmd

    nc = bacc.Bacc("TRN2", target_bir_lowering=False, num_devices=1)
    arrays, args = {}, {}
    for name, array in lay_out(inputs).items():
        array = np.ascontiguousarray(array)
        arrays[f"in_{name}"] = array
        args[name] = nc.dram_tensor(f"in_{name}", array.shape, mybir.dt.from_np(array.dtype), kind="ExternalInput").ap()
    out = nc.dram_tensor("out_x", (NTOK, C), F32, kind="ExternalOutput").ap()
    program(nc, args, out)
    result = run_bass_kernel_spmd(nc, [arrays], core_ids=[0])
    return np.asarray(result.results[0]["out_x"]).reshape(B, S, C)
```

```python
import numpy as np
import concourse.bass as bass
from concourse import mybir
from contextlib import ExitStack

F32 = mybir.dt.float32
F16 = mybir.dt.float16
I32 = mybir.dt.int32
U32 = mybir.dt.uint32
U8 = mybir.dt.uint8
ALU = mybir.AluOpType
ACT = mybir.ActivationFunctionType
AX = mybir.AxisListType
ds = bass.ds

P = 128
B, S, C = 16, 256, 256
DC = 192
H, D = 4, 64
T = S // P
KC = C // P
NT = B * T
NTOK = B * S
E = 8
CTX_CHUNKS = [(0, P), (P, DC - P)]
F0 = 352
F0_CHUNKS = [(0, P), (P, P), (2 * P, F0 - 2 * P)]
F1 = 512
REG = NTOK + P
SHARED = E * REG
DUMMY0 = SHARED + NTOK
DUMMY1 = E * REG
WSCALE = 64.0
ROUTED0 = 2 * NT + E
ROUTED1 = NT + E
TILES0 = ROUTED0 + NT
EPS = 1e-5
BIG = 1e30


class Chain:

    def __init__(self, eng, sem, base=0):
        self.eng, self.sem, self.base, self.n = eng, sem, base, 0

    def link(self, ins):
        self.n += 1
        ins.then_inc(self.sem, 1)
        self.eng.wait_ge(self.sem, self.base + self.n)

    def mark(self, ins):
        self.n += 1
        ins.then_inc(self.sem, 1)

    def wait(self):
        self.eng.wait_ge(self.sem, self.base + self.n)


def phase_semaphore(nc, g, name):
    g["semaphores"].append(nc.alloc_semaphore(name=name))
    return g["semaphores"][-1]


def end_of_phase(nc, g):
    nc.clear_and_free_semaphores(g["semaphores"])
    nc.all_engine_barrier()
    g["semaphores"] = []


def program(nc, a, out):
    root = ExitStack()
    with root:
        def sb(name, shape, dt=F32, ctx=root):
            return ctx.enter_context(nc.sbuf_tensor(name, shape, dt))

        def sem(name, ctx=root):
            return ctx.enter_context(nc.semaphore(name))

        def dram(name, shape, dt=F32):
            return nc.dram_tensor(name, shape, dt, kind="Internal").ap()

        g = {"semaphores": []}
        g["z0"] = dram("z0_rows", (DUMMY0 + E * P, C))
        g["y0"] = dram("y0_rows", (TILES0 * P, C))
        g["z1"] = dram("z1_rows", (DUMMY1 + E * P, C))
        g["y1"] = dram("y1_rows", (ROUTED1 * P, C))
        g["XR"] = sb("residual", [P, NT, C])
        g["ident"] = sb("ident", [P, P])
        g["ones"] = sb("ones", [P, P], F16)
        g["triu"] = sb("strictly_upper", [P, P], F16)
        g["headsel"] = sb("head_select", [P, 2])
        g["reviota"] = sb("reverse_iota", [P, T, E])
        g["regbase"] = sb("region_base", [P, E])
        g["mhalf"] = sb("minus_half", [P, 32])
        g["epst"] = sb("eps_tile", [P, 4])
        g["gate"] = sb("tanh_gates", [P, 4])
        g["SL0"] = sb("slots0", [P, NT, 2], I32)
        g["PR0"] = sb("probs0", [P, NT, 2])
        g["SL1"] = sb("slots1", [P, NT, 1], I32)
        g["PR1"] = sb("probs1", [P, NT, 1])
        g["RUN0"] = sb("running0", [P, E])
        g["RUN1"] = sb("running1", [P, E])
        g["tabrow"] = sb("tile_rows", [1, TILES0], I32)
        g["tabexp"] = sb("tile_experts", [1, TILES0], I32)
        g["carried"], g["carried_v"] = sem("carried_pool"), sem("carried_dve")
        g["zeros"] = sb("zero_rows", [P, C])
        with ExitStack() as l0:
            g["w13h"] = sb("w13_high", [P, KC * (E + 1) * 2 * F0], F16, l0)
            g["w13l"] = sb("w13_low", [P, KC * (E + 1) * 2 * F0], F16, l0)
            g["w2h"] = sb("w2_high", [P, 3 * (E + 1) * C], F16, l0)
            g["w2l"] = sb("w2_low", [P, 3 * (E + 1) * C], F16, l0)
            phase_constants(nc, a, g)
            end_of_phase(nc, g)
            phase_weights0(nc, a, g)
            end_of_phase(nc, g)
            phase_attn0(nc, a, g)
            end_of_phase(nc, g)
            phase_table(nc, a, g, 0)
            end_of_phase(nc, g)
            phase_experts(nc, a, g, 0)
            end_of_phase(nc, g)
        with ExitStack() as l1:
            g["v1h"] = sb("v1_high", [P, KC * E * F1], F16, l1)
            g["v1l"] = sb("v1_low", [P, KC * E * F1], F16, l1)
            g["v2h"] = sb("v2_high", [P, 4 * E * C], F16, l1)
            g["v2l"] = sb("v2_low", [P, 4 * E * C], F16, l1)
            g["b1"] = sb("b1_rows", [P, E * F1], F32, l1)
            g["b2"] = sb("b2_rows", [P, E * C], F32, l1)
            phase_weights1(nc, a, g)
            end_of_phase(nc, g)
            phase_attn1(nc, a, g)
            end_of_phase(nc, g)
            phase_table(nc, a, g, 1)
            end_of_phase(nc, g)
            phase_experts(nc, a, g, 1)
            end_of_phase(nc, g)
        phase_out(nc, a, g, out)
        end_of_phase(nc, g)


def phase_constants(nc, a, g):
    with ExitStack() as c:
        sem = lambda n: phase_semaphore(nc, g, n)
        filled, chosen, gates_in, gates_done = sem("c_filled"), sem("c_chosen"), sem("c_gates_in"), sem("c_gates_done")
        graw = c.enter_context(nc.sbuf_tensor("gates_raw", [P, 4], F32))
        with nc.Block() as block:
            @block.sync
            def _(sp):
                sp.dma_start(graw[:, 0:2], a["g_xattn"].rearrange("(o n) -> o n", o=1).to_broadcast([P, 2])).then_inc(gates_in, 16)
                sp.dma_start(graw[:, 2:4], a["g_ffn"].rearrange("(o n) -> o n", o=1).to_broadcast([P, 2])).then_inc(gates_in, 16)

            @block.scalar
            def _(act):
                act.wait_ge(gates_in, 32)
                act.activation(g["gate"][:], graw[:], ACT.Tanh).then_inc(gates_done, 1)

            @block.vector
            def _(v):
                v.memset(g["ones"][:], 1.0)
                v.memset(g["mhalf"][:], -0.5)
                v.memset(g["epst"][:], EPS)
                v.memset(g["zeros"][:], 0.0)
                v.memset(g["headsel"][:], 0.0).then_inc(filled, 1)
                v.wait_ge(filled, 1)
                v.memset(g["headsel"][0:D, 0:1], 1.0)
                v.memset(g["headsel"][D:P, 1:2], 1.0)
                for e in range(E):
                    v.memset(g["regbase"][:, e:e + 1], float(e * REG))
                    v.memset(g["RUN0"][:, e:e + 1], float(e * REG))
                    v.memset(g["RUN1"][:, e:e + 1], float(e * REG))
                    v.memset(g["reviota"][:, :, e:e + 1], float(E - e))

            @block.gpsimd
            def _(pool):
                pool.memset(g["ident"][:], 0.0).then_inc(chosen, 1)
                pool.memset(g["triu"][:], 1.0).then_inc(chosen, 1)
                pool.wait_ge(chosen, 2)
                pool.affine_select(out=g["ident"][:], in_=g["ident"][:], compare_op=ALU.not_equal, fill=1.0,
                                   base=0, pattern=[[-1, P]], channel_multiplier=1)
                pool.affine_select(out=g["triu"][:], in_=g["triu"][:], compare_op=ALU.is_gt, fill=0.0,
                                   base=0, pattern=[[1, P]], channel_multiplier=-1)


def split_weights(nc, g, name, pieces):
    with ExitStack() as c:
        sem = lambda n: phase_semaphore(nc, g, n)
        width = max(int(np.prod(s.shape)) // s.shape[0] for s, _, _ in pieces)
        NS = 3
        stage = [c.enter_context(nc.sbuf_tensor(f"{name}_stage{i}", [P, width], F32)) for i in range(NS)]
        landed = [sem(f"{name}_landed{i}") for i in range(NS)]
        high_done, low_done = sem(f"{name}_high"), sem(f"{name}_low")

        def view(i, src):
            rows, k, f = src.shape
            return stage[i % NS][0:rows, 0:k * f]

        with nc.Block() as block:
            @block.sync
            def _(sp):
                for i, (src, hi, lo) in enumerate(pieces):
                    if i >= NS:
                        sp.wait_ge(low_done, i - NS + 1)
                    sp.dma_start(view(i, src).rearrange("p (k f) -> p k f", k=src.shape[1]), src).then_inc(landed[i % NS], 16)

            @block.scalar
            def _(act):
                for i, (src, hi, lo) in enumerate(pieces):
                    act.wait_ge(landed[i % NS], 16 * (i // NS + 1))
                    act.activation(hi, view(i, src).rearrange("p (k f) -> p k f", k=src.shape[1]), ACT.Copy, scale=WSCALE).then_inc(high_done, 1)

            @block.vector
            def _(v):
                for i, (src, hi, lo) in enumerate(pieces):
                    v.wait_ge(high_done, i + 1)
                    v.scalar_tensor_tensor(lo, view(i, src).rearrange("p (k f) -> p k f", k=src.shape[1]), WSCALE, hi,
                                           ALU.mult, ALU.subtract).then_inc(low_done, 1)


def phase_weights0(nc, a, g):
    v13 = {x: g[x][:].rearrange("p (k e f) -> p k e f", k=KC, e=E + 1) for x in ("w13h", "w13l")}
    v2 = {x: g[x][:].rearrange("p (k e f) -> p k e f", k=3, e=E + 1) for x in ("w2h", "w2l")}
    pieces = []
    for e in range(E + 1):
        pieces.append((a["w13"][e].rearrange("(k p) f -> p k f", p=P), v13["w13h"][:, :, e, :], v13["w13l"][:, :, e, :]))
    for e in range(E + 1):
        pieces.append((a["w2"][e, 0:2 * P].rearrange("(k p) f -> p k f", p=P), v2["w2h"][:, 0:2, e, :], v2["w2l"][:, 0:2, e, :]))
        n = F0 - 2 * P
        pieces.append((a["w2"][e, 2 * P:F0].rearrange("(k p) f -> p k f", k=1), v2["w2h"][0:n, 2:3, e, :], v2["w2l"][0:n, 2:3, e, :]))
    split_weights(nc, g, "w0", pieces)


def phase_weights1(nc, a, g):
    u1 = {x: g[x][:].rearrange("p (k e f) -> p k e f", k=KC, e=E) for x in ("v1h", "v1l")}
    u2 = {x: g[x][:].rearrange("p (k e f) -> p k e f", k=4, e=E) for x in ("v2h", "v2l")}
    pieces = []
    for e in range(E):
        pieces.append((a["v1"][e].rearrange("(k p) f -> p k f", p=P), u1["v1h"][:, :, e, :], u1["v1l"][:, :, e, :]))
        pieces.append((a["v2"][e].rearrange("(k p) f -> p k f", p=P), u2["v2h"][:, :, e, :], u2["v2l"][:, :, e, :]))
    split_weights(nc, g, "w1", pieces)
    b_in = phase_semaphore(nc, g, "b_in")
    with nc.Block() as block:
        @block.sync
        def _(sp):
            sp.dma_start(g["b1"][:], a["b1"].rearrange("(o e) f -> o (e f)", o=1).to_broadcast([P, E * F1])).then_inc(b_in, 16)
            sp.dma_start(g["b2"][:], a["b2"].rearrange("(o e) f -> o (e f)", o=1).to_broadcast([P, E * C])).then_inc(b_in, 16)
            sp.wait_ge(b_in, 32)



def count(value):
    return max(value, 0) if isinstance(value, int) else value


def within(i, n):
    return not isinstance(i, int) or 0 <= i < n


def over_batches(eng, first, step, last=B - 3, peeled=4):
    for n in range(first, peeled):
        step(n, n % 2)
    end = peeled + (last + 1 - peeled) // 2 * 2
    with eng.Fori(peeled, end - 1, 2) as n:
        step(n, 0)
        step(n + 1, 1)
    for n in range(end, B + 2):
        step(n, n % 2)


class Route:

    def __init__(self, nc, g, c, tag, K, SL, PR, RUN, rows, wg):
        self.nc, self.g, self.K, self.SL, self.PR, self.RUN, self.rows, self.wg = nc, g, K, SL, PR, RUN, rows, wg
        sb = lambda n, s, d=F32: c.enter_context(nc.sbuf_tensor(f"{tag}_{n}", s, d))
        sem = lambda n: phase_semaphore(nc, g, f"{tag}_{n}")
        self.mv = sb("mean_var", [P, T, 2])
        self.st = sb("stats", [P, T, 6])
        self.rstd = sb("rstd", [P, T])
        self.L = sb("logits", [P, T, E])
        self.work = sb("logits_rest", [P, T, E])
        self.eq = sb("equal", [P, T, E])
        self.m = [sb(f"max{k}", [P, T]) for k in range(2)]
        self.best = sb("best", [P, T])
        self.oh = [sb(f"onehot{k}", [P, T, E]) for k in range(K)]
        self.A = sb("assigned", [P, T, E], F16)
        self.d = sb("shifted", [P, T, E + 1])
        self.ex = sb("exps", [P, T, E + 1])
        self.sum = sb("expsum", [P, T])
        self.pos = sb("position", [P, T, E])
        self.slf = sb("slot_f", [P, T, K])
        self.idx = [sb(f"slot_idx{p}", [P, K, T], I32) for p in range(2)]
        self.z = [sb(f"z_tokens{p}", [P, T, C]) for p in range(2)]
        self.zT = sb("z_cols", [P, KC, S])
        self.stats_ready = sem("stats_ready")
        self.rstd_ready = sem("rstd_ready")
        self.z_ready = sem("z_ready")
        self.z_turned = sem("z_turned")
        self.cols_ready = sem("cols_ready")
        self.logits_ready = sem("logits_ready")
        self.shifted_ready = sem("shifted_ready")
        self.exp_ready = sem("exp_ready")
        self.assigned_ready = sem("assigned_ready")
        self.prefix_ready = sem("prefix_ready")
        self.idx_ready = sem("idx_ready")
        self.scattered = [sem(f"scattered{p}") for p in range(2)]
        self.stored = [sem(f"stored{p}") for p in range(2)]
        self.step = sem("route_step")
        self.pool_step = sem("route_pool_step")
        self.steps = 29 if K == 2 else 20
        self.chosen_steps = 17 if K == 2 else 11

    def pool_rstd(self, pool, n):
        ch = Chain(pool, self.pool_step, n * 2)
        pool.wait_ge(self.stats_ready, n + 1)
        ch.link(pool.tensor_tensor(self.rstd[:], self.mv[:, :, 1], self.g["epst"][:, 0:T], ALU.add))
        ch.mark(pool.tensor_tensor(self.rstd[:], self.rstd[:], self.g["mhalf"][:, 0:T], ALU.pow))
        ch.wait()
        pool.sem_inc(self.rstd_ready, 1)

    def vector_stats(self, v, n, x, ch):
        v.sem_inc(self.g["carried_v"], 1)
        for t in range(T):
            ch.mark(v.bn_stats(self.st[:, t, :], x[:, t, :]))
        ch.wait()
        v.sem_inc(self.g["carried_v"], 1)
        for t in range(T):
            ins = v.bn_aggr(self.mv[:, t, :], self.st[:, t, :])
        ins.then_inc(self.stats_ready, 1)

    def vector_z(self, v, n, p, x, shared):
        v.wait_ge(self.rstd_ready, n + 1)
        v.wait_ge(self.scattered[p], count((n - p) * (8 * self.K * T)))
        if shared:
            v.wait_ge(self.stored[p], count((n - p) * 8))
        for t in range(T):
            ins = v.tensor_scalar(self.z[p][:, t, :], x[:, t, :], self.mv[:, t, 0:1], self.rstd[:, t:t + 1], ALU.subtract, ALU.mult)
        ins.then_inc(self.z_ready, 1)

    def pe_turn(self, pe, n, p, bank):
        pe.wait_ge(self.z_ready, n + 1)
        for k in range(KC):
            for t in range(T):
                ins = pe.transpose(bank[:, k, t * P:(t + 1) * P], self.z[p][:, t, k * P:(k + 1) * P], self.g["ident"][:])
        ins.then_inc(self.z_turned, 1)

    def act_cols(self, act, n, bank):
        act.wait_ge(self.logits_ready, count(n))
        act.wait_ge(self.z_turned, n + 1)
        act.activation(self.zT[:], bank, ACT.Copy).then_inc(self.cols_ready, 1)

    def pe_logits(self, pe, n, bank):
        pe.wait_ge(self.cols_ready, n + 1)
        for t in range(T):
            for k in range(KC):
                ins = pe.matmul(bank[:, t, :], self.zT[:, k, t * P:(t + 1) * P], self.wg[:, k, :], start=k == 0, stop=k == KC - 1)
        ins.then_inc(self.logits_ready, 1)

    def pe_prefix(self, pe, n, bank):
        pe.wait_ge(self.assigned_ready, n + 1)
        g = self.g
        pe.matmul(bank[:, 0, :], g["triu"][:], self.A[:, 0, :], start=True, stop=True)
        pe.matmul(bank[:, 1, :], g["triu"][:], self.A[:, 1, :], start=True, stop=False)
        pe.matmul(bank[:, 1, :], g["ones"][:], self.A[:, 0, :], start=False, stop=True)
        pe.matmul(bank[:, 2, :], g["ones"][:], self.A[:, 0, :], start=True, stop=False)
        pe.matmul(bank[:, 2, :], g["ones"][:], self.A[:, 1, :], start=False, stop=True).then_inc(self.prefix_ready, 1)

    def act_exp(self, act, n):
        act.wait_ge(self.shifted_ready, n + 1)
        act.activation(self.ex[:], self.d[:], ACT.Exp).then_inc(self.exp_ready, 1)

    def vector_choose(self, v, n, p, logits, ch):
        bc = lambda x: x.unsqueeze(2).to_broadcast([P, T, E])
        v.wait_ge(self.logits_ready, n + 1)
        ch.link(v.tensor_copy(self.L[:], logits))
        src = self.L
        for k in range(self.K):
            ch.link(v.tensor_reduce(self.m[k][:], src[:], AX.X, ALU.max))
            ch.link(v.tensor_tensor(self.eq[:], src[:], bc(self.m[k][:]), ALU.is_equal))
            ch.link(v.tensor_tensor(self.eq[:], self.eq[:], self.g["reviota"][:], ALU.mult))
            ch.link(v.tensor_reduce(self.best[:], self.eq[:], AX.X, ALU.max))
            ch.link(v.tensor_tensor(self.oh[k][:], self.eq[:], bc(self.best[:]), ALU.is_equal))
            if k == 0 and self.K == 2:
                ch.link(v.scalar_tensor_tensor(self.work[:], self.oh[0][:], -BIG, self.L[:], ALU.mult, ALU.add))
                src = self.work
        if self.K == 2:
            ch.link(v.tensor_tensor(self.A[:], self.oh[0][:], self.oh[1][:], ALU.add))
        else:
            ch.link(v.tensor_copy(self.A[:], self.oh[0][:]))
        v.sem_inc(self.assigned_ready, 1)
        ch.mark(v.tensor_tensor(self.d[:, :, 0:E], self.L[:], bc(self.m[0][:]), ALU.subtract))
        ch.mark(v.tensor_tensor(self.d[:, :, E], self.m[self.K - 1][:], self.m[0][:], ALU.subtract))
        ch.wait()
        v.sem_inc(self.shifted_ready, 1)
        assert ch.n == self.chosen_steps, ch.n

    def vector_slots(self, v, n, p, prefix):
        ch = Chain(v, self.step, n * self.steps)
        ch.n = self.chosen_steps
        v.wait_ge(self.exp_ready, n + 1)
        ch.link(v.tensor_reduce(self.sum[:], self.ex[:, :, 0:E], AX.X, ALU.add))
        ch.link(v.reciprocal(self.sum[:], self.sum[:]))
        ch.mark(v.tensor_copy(self.PR[:, ds(n * T, T), 0], self.sum[:]))
        if self.K == 2:
            ch.mark(v.tensor_tensor(self.PR[:, ds(n * T, T), 1], self.sum[:], self.ex[:, :, E], ALU.mult))
        v.wait_ge(self.prefix_ready, n + 1)
        ch.link(v.tensor_tensor(self.pos[:], prefix[:, 0:T, :], self.RUN[:].unsqueeze(1).to_broadcast([P, T, E]), ALU.add))
        ch.mark(v.tensor_tensor(self.RUN[:], self.RUN[:], prefix[:, T, :], ALU.add))
        for k in range(self.K):
            ch.link(v.tensor_tensor(self.eq[:], self.oh[k][:], self.pos[:], ALU.mult))
            ch.link(v.tensor_reduce(self.slf[:, :, k], self.eq[:], AX.X, ALU.add))
        ch.mark(v.tensor_copy(self.SL[:, ds(n * T, T), :], self.slf[:]))
        ch.link(v.tensor_copy(self.idx[p][:].rearrange("p k t -> p t k"), self.slf[:]))
        v.sem_inc(self.idx_ready, 1)
        assert ch.n == self.steps, ch.n

    def pool_scatter(self, pool, n, p):
        pool.wait_ge(self.idx_ready, n + 1)
        pool.sem_inc(self.g["carried"], 1)
        for k in range(self.K):
            for t in range(T):
                pool.indirect_dma_start(self.rows, bass.IndirectOffsetOnAxis(ap=self.idx[p][:, k, t:t + 1], axis=0),
                                        self.z[p][:, t, :], None).then_inc(self.scattered[p], 16)

    def finish(self, eng, shared):
        for p in range(2):
            eng.wait_ge(self.scattered[p], (B // 2) * self.K * T * 16)
            if shared:
                eng.wait_ge(self.stored[p], (B // 2) * 16)


def phase_attn0(nc, a, g):
    NS1 = DC - P
    with ExitStack() as c:
        sb = lambda n, s, d=F32: c.enter_context(nc.sbuf_tensor(f"a0_{n}", s, d))
        pb = lambda n: c.enter_context(nc.psum_tensor(f"a0_{n}", [P, 512], F32))
        sem = lambda n: phase_semaphore(nc, g, f"a0_{n}")
        wq, wo = sb("wq", [P, KC, C]), sb("wo", [P, KC, C])
        wl, wc = sb("wlkv", [P, KC, 2 * C]), sb("wkv", [P, 2, 2 * C])
        wg = sb("wg", [P, KC, E])
        lng, lnb = sb("ln_l_g", [P, KC]), sb("ln_l_b", [P, KC])
        cng, cnb = sb("ln_x_g", [P, 2]), sb("ln_x_b", [P, 2])
        gqk, knraw = sb("qk_gain", [P, 1]), sb("kn_gain", [P, 1])
        gains, gmax, gneg = sb("gain_rows", [P, 2, D]), sb("gain_bound", [P, 1]), sb("gain_products", [P, D])
        masku, maskf, bias = sb("mask_bytes", [P, B * T], U8), sb("mask_bias", [P, B, T]), sb("latent_bias", [P, 1])
        bo = sb("bo", [P, C])
        cin = [sb(f"ctx_in{p}", [P, T, DC]) for p in range(2)]
        st, mv, r1, r2 = sb("stats", [P, 4, 6]), sb("mean_var", [P, 4, 2]), sb("rstd", [P, 4]), sb("rstd2", [P, 2])
        xn, cn = sb("x_norm", [P, T, C]), sb("ctx_norm", [P, T, DC])
        lT, cT = sb("lat_cols", [P, KC, S]), sb("ctx_cols", [P, 2, S])
        qs, sq = sb("q_tokens", [P, T * H, D]), sb("q_squares", [P, T * H, D])
        qn = sb("q_norm", [P, T, C])
        ksq = sb("k_squares", [P, 2, 512])
        ss = sb("square_sums", [P, 24])
        rq = sb("q_scales", [P, 8])
        rr = [sb(f"k_scales{p}", [P, 16]) for p in range(2)]
        qT = [sb(f"q_cols{p}", [P, 2, S]) for p in range(2)]
        kT = [sb(f"k_cols{p}", [P, 2, 512]) for p in range(2)]
        va = [sb(f"v_ones{p}", [P, 4, H, D + 1]) for p in range(2)]
        pm = [sb(f"probs{i}", [P, 4, S]) for i in range(2)]
        rs = sb("o_rsum", [P, T, H])
        on = sb("o_norm", [P, T, C])
        onT = sb("o_cols", [P, KC, S])
        xo = sb("x_mid", [P, T, C])
        RB = [pb("front0"), pb("front1")]
        TA, TB = pb("tail_cols"), pb("tail_rows")
        SC = [pb("scores0"), pb("scores1")]
        O = [pb("out0"), pb("out1")]
        rt = Route(nc, g, c, "r0", 2, g["SL0"], g["PR0"], g["RUN0"], g["z0"], wg)

        consts_in, consts_ready, const_step, pconst = sem("consts_in"), sem("consts_ready"), sem("const_step"), sem("pool_const_step")
        landed = [sem(f"landed{p}") for p in range(2)]
        s1_stats, s1_rstd, s1_norm, s1_turned, s1_cols = (sem(f"s1_{x}") for x in ("stats", "rstd", "norm", "turned", "cols"))
        proj_ready, freed_act, freed_dve = sem("proj_ready"), sem("proj_freed_act"), sem("proj_freed_dve")
        s1_ksq, s1_ssq, s1_ssk, s1_ss, s1_rq, s1_rr = (sem(f"s1_{x}") for x in ("ksq", "ssq", "ssk", "ss", "rq", "rr"))
        KSUM = TB[:, 256:256 + 16]
        s1_qn, s1_qturned, s1_qT = (sem(f"s1_{x}") for x in ("qn", "qturned", "qT"))
        scores, exps, pv = sem("scores"), sem("exps"), sem("pv")
        s2_on, s2_turned, s2_cols, s2_wo = (sem(f"s2_{x}") for x in ("on", "turned", "cols", "wo"))
        d0, d1, d2, p1 = sem("dve_step0"), sem("dve_step1"), sem("dve_step2"), sem("pool_step1")
        D0, D1, D2, P1 = 4, 4, 4, 7

        col = lambda x: x.rearrange("(k p) -> p k", p=P)
        loads = [(wq[:], a["wq0"].rearrange("(k p) f -> p k f", p=P)), (wo[:], a["wo0"].rearrange("(k p) f -> p k f", p=P)),
                 (wl[:], a["wlkv0"].rearrange("(k p) f -> p k f", p=P)),
                 (wc[:, 0, :], a["wkv0"][0:P]), (wc[0:NS1, 1, :], a["wkv0"][P:DC]),
                 (wg[:], a["wg0"].rearrange("(k p) e -> p k e", p=P)),
                 (bo[:], a["bo0"].rearrange("(o n) -> o n", o=1).to_broadcast([P, C])),
                 (gains[:, 0, :], a["qn"].rearrange("(o n) -> o n", o=1).to_broadcast([P, D])),
                 (gains[:, 1, :], a["kn"].rearrange("(o n) -> o n", o=1).to_broadcast([P, D])),
                 (masku[:], a["mask"])]
        small = [(lng[:, k:k + 1], a["ln_l_g"][k * P:(k + 1) * P]) for k in range(KC)] + \
                [(lnb[:, k:k + 1], a["ln_l_b"][k * P:(k + 1) * P]) for k in range(KC)] + \
                [(cng[0:n, k:k + 1], a["ln_x_g"][o:o + n]) for k, (o, n) in enumerate(CTX_CHUNKS)] + \
                [(cnb[0:n, k:k + 1], a["ln_x_b"][o:o + n]) for k, (o, n) in enumerate(CTX_CHUNKS)] + \
                [(gqk[h * D:(h + 1) * D, :], a["qn"]) for h in range(2)] + [(knraw[h * D:(h + 1) * D, :], a["kn"]) for h in range(2)]
        small = [(dst, src.rearrange("(p o) -> p o", o=1)) for dst, src in small]
        n_consts = 16 * (len(loads) + len(small))

        with nc.Block() as block:
            @block.sync
            def _(sp):
                for dst, src in loads + small:
                    sp.dma_start(dst, src).then_inc(consts_in, 16)

                def load(m, p):
                    sp.wait_ge(landed[p], count((m - p) * 16))
                    sp.dma_start(g["XR"][:, ds(m * T, T), :], a["x"][ds(m * S, S), :].rearrange("(t p) c -> p t c", p=P)).then_inc(landed[p], 16)
                    sp.wait_ge(s1_norm, count(m - 1))
                    sp.dma_start(cin[p][:], a["ctx"][ds(m * S, S), :].rearrange("(t p) c -> p t c", p=P)).then_inc(landed[p], 16)

                def store(m, p):
                    sp.wait_ge(rt.z_ready, m + 1)
                    sp.dma_start(g["z0"][ds(m * S + SHARED, S), :].rearrange("(t p) c -> p t c", p=P), rt.z[p][:]).then_inc(rt.stored[p], 16)

                def step(n, q):
                    if within(n + 3, B):
                        load(n + 3, 1 - q)
                    if within(n - 1, B):
                        store(n - 1, 1 - q)
                over_batches(sp, -3, step, B - 4)
                rt.finish(sp, True)

            @block.gpsimd
            def _(pool):
                def rstd(m):
                    ch = Chain(pool, p1, m * P1)
                    pool.wait_ge(s1_stats, m + 1)
                    ch.link(pool.tensor_tensor(r1[:], mv[:, :, 1], g["epst"][:], ALU.add))
                    ch.link(pool.tensor_tensor(r1[:], r1[:], g["mhalf"][:, 0:4], ALU.pow))
                    ch.link(pool.tensor_tensor(r2[:], mv[:, 0:T, 1], r1[:, 0:T], ALU.mult))
                    ch.link(pool.tensor_tensor(r2[:], r2[:], r1[:, 0:T], ALU.mult))
                    ch.link(pool.tensor_tensor(r2[:], r2[:], g["epst"][:, 0:T], ALU.add))
                    ch.link(pool.tensor_tensor(r2[:], r2[:], g["mhalf"][:, 0:T], ALU.pow))
                    ch.link(pool.tensor_tensor(r1[:, 0:T], r1[:, 0:T], r2[:], ALU.mult))
                    pool.sem_inc(s1_rstd, 1)
                    assert ch.n == P1, ch.n

                def squares(m, p):
                    pool.wait_ge(s1_ssk, count(m))
                    for i in range(2):
                        pool.wait_ge(freed_act, 3 * m + 2 + i)
                        ins = pool.tensor_tensor(ksq[:, i, :], kT[p][:, i, :], kT[p][:, i, :], ALU.mult)
                    ins.then_inc(s1_ksq, 1)

                def q_scales(m):
                    pool.wait_ge(s1_qn, count(m))
                    pool.wait_ge(s1_ssq, m + 1)
                    pool.tensor_tensor(rq[:], ss[:, 0:8], g["mhalf"][:, 0:8], ALU.pow).then_inc(s1_rq, 1)

                def k_scales(m, p):
                    pool.wait_ge(exps, count(16 * (m - 1)))
                    pool.wait_ge(s1_ss, m + 1)
                    pool.tensor_tensor(rr[p][:], ss[:, 8:24], g["mhalf"][:, 0:16], ALU.pow).then_inc(s1_rr, 1)

                def step(n, q):
                    if within(n + 2, B):
                        rstd(n + 2)
                    if within(n - 1, B):
                        rt.pool_rstd(pool, n - 1)
                    if within(n + 1, B):
                        squares(n + 1, 1 - q)
                        q_scales(n + 1)
                        k_scales(n + 1, 1 - q)
                    if within(n - 2, B):
                        rt.pool_scatter(pool, n - 2, q)
                over_batches(pool, -2, step)

            @block.scalar
            def _(act):
                act.wait_ge(consts_ready, 1)

                def front_cols(m):
                    act.wait_ge(s1_ssk, count(m))
                    act.wait_ge(s1_turned, 2 * m + 1)
                    for k in range(KC):
                        ins = act.activation(lT[:, k, :], RB[0][:, k * S:(k + 1) * S], ACT.Identity, bias=lnb[:, k:k + 1], scale=lng[:, k:k + 1])
                    ins.then_inc(s1_cols, 1)
                    act.wait_ge(s1_turned, 2 * m + 2)
                    for k, (o, w) in enumerate(CTX_CHUNKS):
                        ins = act.activation(cT[0:w, k, :], RB[1][0:w, k * S:(k + 1) * S], ACT.Identity, bias=cnb[0:w, k:k + 1], scale=cng[0:w, k:k + 1])
                    ins.then_inc(s1_cols, 1)

                def front_qk(m, p):
                    act.wait_ge(s1_qn, count(m))
                    act.wait_ge(proj_ready, 4 * m + 1)
                    act.activation(qs[:].rearrange("p h d -> p (h d)"), RB[0][:], ACT.Copy).then_inc(freed_act, 1)
                    act.wait_ge(scores, count(8 * (m - 1)))
                    for i in range(2):
                        act.wait_ge(proj_ready, 4 * m + 2 + i)
                        act.activation(kT[p][:, i, :], RB[1 - i][:], ACT.Copy).then_inc(freed_act, 1)

                def front_q(m, p):
                    act.wait_ge(s1_qturned, m + 1)
                    act.activation(qT[p][:].rearrange("p k s -> p (k s)"), RB[1][:], ACT.Copy, scale=gqk[:, 0:1]).then_inc(s1_qT, 1)

                def head(m, p, h):
                    for jp in range(2):
                        if jp == 0:
                            act.wait_ge(pv, count(4 * m + h - 1) if h else count(4 * m))
                        act.wait_ge(scores, 8 * m + 2 * h + jp + 1)
                        if h == 0 and jp == 0:
                            act.wait_ge(s1_rr, m + 1)
                        for j in range(2):
                            jt = jp + 2 * (1 - j)
                            b = maskf[:, ds(m, 1), jt] if jt < 2 else bias[:, 0:1]
                            act.activation(pm[h % 2][:, jt, :], SC[jp][:, j * S:(j + 1) * S], ACT.Exp, bias=b,
                                           scale=rr[p][:, jt * 4 + h:jt * 4 + h + 1]).then_inc(exps, 1)

                def tail_cols(m):
                    act.wait_ge(s2_wo, count(m))
                    act.wait_ge(s2_turned, m + 1)
                    act.activation(onT[:].rearrange("p k s -> p (k s)"), TA[:], ACT.Copy).then_inc(s2_cols, 1)

                def step(n, q):
                    core, front, tail = within(n, B), within(n + 1, B), within(n - 1, B)
                    if core:
                        head(n, q, 0)
                    if tail:
                        tail_cols(n - 1)
                    if front:
                        front_cols(n + 1)
                    if core:
                        head(n, q, 1)
                    if front:
                        front_qk(n + 1, 1 - q)
                    if core:
                        head(n, q, 2)
                    if tail:
                        rt.act_cols(act, n - 1, TA[:].rearrange("p (k s) -> p k s", k=KC))
                    if core:
                        head(n, q, 3)
                    if front:
                        front_q(n + 1, 1 - q)
                    if tail:
                        rt.act_exp(act, n - 1)
                over_batches(act, -1, step)

            @block.vector
            def _(v):
                v.wait_ge(consts_in, n_consts)
                ch = Chain(v, const_step)
                ch.link(v.scalar_tensor_tensor(gqk[:], gqk[:], D ** -0.5, knraw[:], ALU.mult, ALU.mult))
                ch.link(v.tensor_tensor(gneg[:], gains[:, 0, :], gains[:, 1, :], ALU.mult))
                ch.link(v.tensor_reduce(gmax[:], gneg[:], AX.X, ALU.max, apply_absolute_value=True))
                ch.link(v.tensor_scalar(bias[:], gmax[:], -(D ** 0.5), None, ALU.mult))
                ch.link(v.tensor_copy(maskf[:].rearrange("p b t -> p (b t)"), masku[:]))
                ch.link(v.tensor_scalar(maskf[:], maskf[:], BIG, -BIG, ALU.mult, ALU.add))
                ch.link(v.tensor_scalar(maskf[:], maskf[:], bias[:, 0:1], None, ALU.add))
                ch.link(v.tensor_scalar(bo[:], bo[:], g["gate"][:, 0:1], None, ALU.mult))
                for p in range(2):
                    ch.mark(v.memset(va[p][:], 1.0))
                ch.wait()
                v.sem_inc(consts_ready, 3)
                chains = {}

                def pre_stats(m, p):
                    ch = chains["front"] = Chain(v, d0, m * D0)
                    v.wait_ge(landed[p], (m - p) * 16 + 32)
                    x = XRTile(g["XR"], m)
                    for t in range(T):
                        ch.mark(v.bn_stats(st[:, 2 + t, :], cin[p][:, t, :]))
                        ch.mark(v.bn_stats(st[:, t, :], x[:, t, :]))
                    ch.wait()
                    v.sem_inc(g["carried_v"], 1)
                    for t in range(4):
                        ins = v.bn_aggr(mv[:, t, :], st[:, t, :])
                    ins.then_inc(s1_stats, 1)

                def pre_norm(m, p):
                    v.wait_ge(s1_turned, count(2 * m))
                    v.wait_ge(s1_rstd, m + 1)
                    x = XRTile(g["XR"], m)
                    for t in range(T):
                        v.tensor_scalar(xn[:, t, :], x[:, t, :], mv[:, t, 0:1], r1[:, t:t + 1], ALU.subtract, ALU.mult)
                        ins = v.tensor_scalar(cn[:, t, :], cin[p][:, t, :], mv[:, 2 + t, 0:1], r1[:, 2 + t:3 + t], ALU.subtract, ALU.mult)
                    ins.then_inc(s1_norm, 1)

                def front_squares(m, p):
                    ch = chains["front1"] = Chain(v, d1, m * D1)
                    v.wait_ge(freed_act, 3 * m + 1)
                    ch.link(v.tensor_tensor(sq[:], qs[:], qs[:], ALU.mult))
                    v.wait_ge(s1_rq, count(m))
                    ch.link(v.tensor_reduce(ss[:, 0:8], sq[:], AX.X, ALU.add))
                    ch.mark(v.tensor_scalar(ss[:, 0:8], ss[:, 0:8], 1.0 / D, 1e-16, ALU.mult, ALU.max))
                    ch.wait()
                    v.sem_inc(s1_ssq, 1)

                def front_v(m, p, i):
                    v.tensor_copy(va[p][:, 2 * i:2 * i + 2, :, 0:D].rearrange("p j h d -> p (j h) d"),
                                  RB[1 - i][:].rearrange("p (x d) -> p x d", d=D)).then_inc(freed_dve, 1)

                def front_sums(m):
                    ch = chains["front1"]
                    v.wait_ge(s1_rr, count(m))
                    ch.link(v.tensor_scalar(ss[:, 8:24], KSUM, 1.0 / D, 1e-16, ALU.mult, ALU.max))
                    v.sem_inc(s1_ss, 1)
                    assert ch.n == D1, ch.n

                def front_qn(m):
                    v.wait_ge(s1_qturned, count(m))
                    v.wait_ge(s1_rq, m + 1)
                    v.tensor_tensor(qn[:].rearrange("p t (h d) -> p (t h) d", d=D), qs[:], rq[:].unsqueeze(2).to_broadcast([P, 8, D]),
                                    ALU.mult).then_inc(s1_qn, 1)

                def tail_on(m):
                    ch = chains["tail"] = Chain(v, d2, m * D2)
                    v.wait_ge(pv, 4 * m + 4)
                    ov = [O[t][:, 0:H * (D + 1)].rearrange("p (h e) -> p h e", h=H) for t in range(T)]
                    for t in range(T):
                        ch.mark(v.reciprocal(rs[:, t, :], ov[t][:, :, D]))
                    ch.wait()
                    v.wait_ge(s2_turned, count(m))
                    for t in range(T):
                        ins = v.tensor_tensor(on[:, t, :].rearrange("p (h d) -> p h d", h=H), ov[t][:, :, 0:D],
                                              rs[:, t, :].unsqueeze(2).to_broadcast([P, H, D]), ALU.mult)
                    ins.then_inc(s2_on, 1)

                def tail_x1(m):
                    ch = chains["tail"]
                    xr = g["XR"][:, ds(m * T, T), :]
                    v.wait_ge(s2_wo, m + 1)
                    ch.link(v.scalar_tensor_tensor(xo[:], TB[:].rearrange("p (t c) -> p t c", t=T), g["gate"][:, 0:1], xr, ALU.mult, ALU.add))
                    ch.link(v.tensor_tensor(xr, xo[:], bo[:].unsqueeze(1).to_broadcast([P, T, C]), ALU.add))
                    assert ch.n == D2, ch.n
                    chains["route"] = Chain(v, rt.step, m * rt.steps)
                    rt.vector_stats(v, m, XRTile(g["XR"], m), chains["route"])

                def step(n, q):
                    front, tail = within(n + 1, B), within(n - 1, B)
                    m = n - 1
                    if tail:
                        tail_on(m)
                    if within(n - 2, B):
                        rt.vector_slots(v, n - 2, q, TB[:, 128:128 + (T + 1) * E].rearrange("p (t e) -> p t e", t=T + 1))
                    if within(n + 2, B):
                        pre_stats(n + 2, q)
                    if tail:
                        tail_x1(m)
                    if within(n + 2, B):
                        pre_norm(n + 2, q)
                    if tail:
                        rt.vector_z(v, m, 1 - q, XRTile(g["XR"], m), True)
                    if front:
                        front_squares(n + 1, 1 - q)
                        v.wait_ge(pv, count(4 * n))
                        v.wait_ge(proj_ready, 4 * n + 8)
                        front_v(n + 1, 1 - q, 0)
                        front_qn(n + 1)
                        v.wait_ge(s1_ssk, n + 2)
                        front_v(n + 1, 1 - q, 1)
                        front_sums(n + 1)
                    if tail:
                        rt.vector_choose(v, m, 1 - q, TB[:, 0:T * E].rearrange("p (t e) -> p t e", t=T), chains["route"])
                over_batches(v, -2, step)

            @block.tensor
            def _(pe):
                pe.wait_ge(consts_ready, 2)
                ident = g["ident"]

                def turn(m):
                    pe.wait_ge(s1_norm, m + 1)
                    pe.wait_ge(freed_dve, count(2 * m))
                    for k in range(KC):
                        for t in range(T):
                            ins = pe.transpose(RB[0][:, k * S + t * P:k * S + (t + 1) * P], xn[:, t, k * P:(k + 1) * P], ident[:])
                    ins.then_inc(s1_turned, 1)
                    pe.wait_ge(s1_qT, count(m))
                    for t in range(T):
                        for k, (o, w) in enumerate(CTX_CHUNKS):
                            ins = pe.transpose(RB[1][0:w, k * S + t * P:k * S + (t + 1) * P], cn[:, t, o:o + w], ident[:])
                    ins.then_inc(s1_turned, 1)

                def project_qk(m):
                    pe.wait_ge(s1_cols, 2 * m + 1)
                    for t in range(T):
                        for k in range(KC):
                            ins = pe.matmul(RB[0][:, t * C:(t + 1) * C], lT[:, k, t * P:(t + 1) * P], wq[:, k, :], start=k == 0, stop=k == KC - 1)
                    ins.then_inc(proj_ready, 1)
                    pe.wait_ge(s1_cols, 2 * m + 2)
                    for i in range(2):
                        bank = RB[1 - i]
                        if i == 1:
                            pe.wait_ge(freed_act, 3 * m + 1)
                        for k, (o, w) in enumerate(CTX_CHUNKS):
                            pe.matmul(bank[:, 0:S], wc[0:w, k, i * P:(i + 1) * P], cT[0:w, k, :], start=k == 0, stop=k == 1)
                        for k in range(KC):
                            ins = pe.matmul(bank[:, S:2 * S], wl[:, k, i * P:(i + 1) * P], lT[:, k, :], start=k == 0, stop=k == KC - 1)
                        ins.then_inc(proj_ready, 1)

                def project_v_ctx(m):
                    pe.wait_ge(freed_act, 3 * m + 2)
                    for t in range(T):
                        for k, (o, w) in enumerate(CTX_CHUNKS):
                            ins = pe.matmul(RB[1][:, t * C:(t + 1) * C], cT[0:w, k, t * P:(t + 1) * P], wc[0:w, k, C:2 * C], start=k == 0, stop=k == 1)
                    ins.then_inc(proj_ready, 1)

                def project_v_lat_key_sums(m):
                    pe.wait_ge(freed_act, 3 * m + 3)
                    for t in range(T):
                        for k in range(KC):
                            pe.matmul(RB[0][:, t * C:(t + 1) * C], lT[:, k, t * P:(t + 1) * P], wl[:, k, C:2 * C], start=k == 0, stop=k == KC - 1)
                            if t == 0 and k == 0:
                                pe.wait_ge(s1_ksq, m + 1)
                            jt = t * KC + k
                            for i in range(2):
                                ins = pe.matmul(KSUM[:, jt * 4 + i * 2:jt * 4 + i * 2 + 2], ksq[:, i, jt * P:(jt + 1) * P], g["headsel"][:], start=True, stop=True)
                    ins.then_inc(s1_ssk, 1)

                def turn_q(m):
                    pe.wait_ge(freed_dve, 2 * m + 1)
                    pe.wait_ge(s1_qn, m + 1)
                    for i in range(2):
                        for t in range(T):
                            ins = pe.transpose(RB[1][:, i * S + t * P:i * S + (t + 1) * P], qn[:, t, i * P:(i + 1) * P], ident[:])
                    ins.then_inc(s1_qturned, 1)

                def score(m, p, h):
                    lo = (h % 2) * D
                    for jp in range(2):
                        i = 2 * h + jp
                        pe.wait_ge(exps, count(16 * m + 2 * i - 2) if i else count(16 * m))
                        if i == 0:
                            pe.wait_ge(s1_qT, m + 1)
                            pe.wait_ge(freed_act, 3 * m + 3)
                        for j in range(2):
                            jt = jp + 2 * (1 - j)
                            ins = pe.matmul(SC[jp][:, j * S:(j + 1) * S], kT[p][lo:lo + D, h // 2, jt * P:(jt + 1) * P],
                                            qT[p][lo:lo + D, h // 2, :], start=True, stop=True)
                        ins.then_inc(scores, 1)

                def products(m, p, h):
                    if h == 0:
                        pe.wait_ge(freed_dve, 2 * m + 2)
                        pe.wait_ge(s2_on, count(m))
                    pe.wait_ge(exps, 16 * m + 4 * h + 4)
                    for t in range(T):
                        for jt in range(4):
                            ins = pe.matmul(O[t][:, h * (D + 1):(h + 1) * (D + 1)], pm[h % 2][:, jt, t * P:(t + 1) * P], va[p][:, jt, h, :],
                                            start=jt == 0, stop=jt == 3)
                    ins.then_inc(pv, 1)

                def turn_o(m):
                    pe.wait_ge(rt.cols_ready, count(m))
                    pe.wait_ge(s2_on, m + 1)
                    for k in range(KC):
                        for t in range(T):
                            ins = pe.transpose(TA[:, k * S + t * P:k * S + (t + 1) * P], on[:, t, k * P:(k + 1) * P], ident[:])
                    ins.then_inc(s2_turned, 1)

                def project_o(m):
                    pe.wait_ge(rt.idx_ready, count(m))
                    pe.wait_ge(s2_cols, m + 1)
                    for t in range(T):
                        for k in range(KC):
                            ins = pe.matmul(TB[:, t * C:(t + 1) * C], onT[:, k, t * P:(t + 1) * P], wo[:, k, :], start=k == 0, stop=k == KC - 1)
                    ins.then_inc(s2_wo, 1)

                def step(n, q):
                    core, front, tail = within(n, B), within(n + 1, B), within(n - 1, B)
                    m, f, fq = n - 1, n + 1, 1 - q
                    if core:
                        score(n, q, 0)
                    if within(n - 2, B):
                        rt.pe_prefix(pe, n - 2, TB[:, 128:128 + (T + 1) * E].rearrange("p (t e) -> p t e", t=T + 1))
                    if tail:
                        turn_o(m)
                    if front:
                        turn(f)
                    if core:
                        score(n, q, 1)
                        products(n, q, 0)
                    if tail:
                        project_o(m)
                    if front:
                        project_qk(f)
                    if core:
                        score(n, q, 2)
                        products(n, q, 1)
                    if tail:
                        rt.pe_turn(pe, m, 1 - q, TA[:].rearrange("p (k s) -> p k s", k=KC))
                    if core:
                        score(n, q, 3)
                    if front:
                        project_v_ctx(f)
                    if core:
                        products(n, q, 2)
                    if tail:
                        rt.pe_logits(pe, m, TB[:, 0:T * E].rearrange("p (t e) -> p t e", t=T))
                    if front:
                        project_v_lat_key_sums(f)
                        turn_q(f)
                    if core:
                        products(n, q, 3)
                over_batches(pe, -1, step)


class XRTile:

    def __init__(self, xr, n):
        self.xr, self.n = xr, n

    def __getitem__(self, k):
        _, t, _ = k
        return self.xr[:, ds(self.n * T + t, 1), :].rearrange("p o c -> p (o c)")



def phase_table(nc, a, g, layer):
    RUN, routed, dummy, zd = ((g["RUN0"], ROUTED0, DUMMY0, g["z0"]), (g["RUN1"], ROUTED1, DUMMY1, g["z1"]))[layer]
    tiles = TILES0 if layer == 0 else ROUTED1
    E1 = E + 1
    with ExitStack() as c:
        sb = lambda n, s, d=F32: c.enter_context(nc.sbuf_tensor(f"t{layer}_{n}", s, d))
        sem = lambda n: phase_semaphore(nc, g, f"t{layer}_{n}")
        tiota, tf = sb("tile_iota", [P, tiles], I32), sb("tile_number", [P, tiles])
        jiota, jf = sb("fill_iota", [P, NT], I32), sb("fill", [P, NT])
        eiota, ef = sb("expert_iota", [P, E1], I32), sb("expert", [P, E1])
        cnt, more = sb("count", [P, E]), sb("more", [P, E, NT])
        nt, before, upto, base = sb("tiles_of", [P, E]), sb("tiles_before", [P, E1]), sb("tiles_upto", [P, E1]), sb("base", [P, E1])
        ge, lt = sb("after_first", [P, routed, E1]), sb("before_last", [P, routed, E1])
        row, ex, runi = sb("row", [P, tiles]), sb("ex", [P, tiles]), sb("run_int", [P, E], I32)
        iotas, step, run_ready, padded = sem("iotas"), sem("step"), sem("run_ready"), sem("padded")
        K = 2 - layer
        SL = g[f"SL{layer}"][:].rearrange("p n k -> p (n k)")
        slf, sel, less, dbase = sb("slots", [P, NT * K]), sb("slot_after", [P, NT * K, E]), sb("slot_less", [P, NT * K]), sb("base_steps", [P, E])
        with nc.Block() as block:
            @block.gpsimd
            def _(pool):
                pool.iota(tiota[:], pattern=[[1, tiles]], base=0, channel_multiplier=0).then_inc(iotas, 1)
                pool.iota(jiota[:], pattern=[[P, NT]], base=0, channel_multiplier=0).then_inc(iotas, 1)
                pool.iota(eiota[:], pattern=[[1, E1]], base=0, channel_multiplier=0).then_inc(iotas, 1)

            @block.vector
            def _(v):
                ch = Chain(v, step)
                tt = v.tensor_tensor
                ch.link(v.tensor_copy(runi[:], RUN[:]))
                v.sem_inc(run_ready, 1)
                v.wait_ge(iotas, 3)
                ch.mark(v.tensor_copy(tf[:], tiota[:]))
                ch.mark(v.tensor_copy(jf[:], jiota[:]))
                ch.mark(v.tensor_copy(ef[:], eiota[:]))
                ch.link(tt(cnt[:], RUN[:], g["regbase"][:], ALU.subtract))
                ch.link(tt(more[:], cnt[:].unsqueeze(2).to_broadcast([P, E, NT]), jf[:].unsqueeze(1).to_broadcast([P, E, NT]), ALU.is_gt))
                ch.mark(v.tensor_reduce(nt[:], more[:], AX.X, ALU.add))
                ch.mark(v.memset(before[:, 0:1], 0.0))
                ch.mark(v.memset(upto[:, E:E + 1], BIG))
                ch.wait()
                for e in range(E):
                    ch.link(tt(upto[:, e:e + 1], before[:, e:e + 1], nt[:, e:e + 1], ALU.add))
                    ch.link(v.tensor_copy(before[:, e + 1:e + 2], upto[:, e:e + 1]))
                ch.mark(v.tensor_copy(base[:, 0:E], g["regbase"][:]))
                ch.mark(v.memset(base[:, E:E1], float(dummy)))
                ch.wait()
                ch.link(v.scalar_tensor_tensor(base[:], before[:], -float(P), base[:], ALU.mult, ALU.add))
                full = [P, routed, E1]
                tb = tf[:, 0:routed].unsqueeze(2).to_broadcast(full)
                ch.mark(tt(ge[:], tb, before[:].unsqueeze(1).to_broadcast(full), ALU.is_ge))
                ch.link(tt(lt[:], tb, upto[:].unsqueeze(1).to_broadcast(full), ALU.is_lt))
                ch.link(tt(ge[:], ge[:], lt[:], ALU.mult))
                ch.link(tt(lt[:], ge[:], base[:].unsqueeze(1).to_broadcast(full), ALU.mult))
                ch.link(v.tensor_reduce(row[:, 0:routed], lt[:], AX.X, ALU.add))
                ch.link(v.scalar_tensor_tensor(row[:, 0:routed], tf[:, 0:routed], float(P), row[:, 0:routed], ALU.mult, ALU.add))
                ch.link(tt(lt[:, :, 0:E], ge[:, :, 0:E], ef[:, 0:E].unsqueeze(1).to_broadcast([P, routed, E]), ALU.mult))
                ch.link(v.tensor_reduce(ex[:, 0:routed], lt[:, :, 0:E], AX.X, ALU.add))
                if layer == 0:
                    ch.mark(v.tensor_scalar(row[:, routed:tiles], tf[:, routed:tiles], float(P), float(SHARED - P * routed), ALU.mult, ALU.add))
                    ch.link(v.memset(ex[:, routed:tiles], float(E)))
                ch.mark(v.tensor_copy(g["tabrow"][:, 0:tiles], row[0:1, :]))
                ch.link(v.tensor_copy(g["tabexp"][:, 0:tiles], ex[0:1, :]))

                ch.mark(v.tensor_copy(slf[:], SL))
                ch.mark(v.tensor_copy(dbase[:, 0:1], base[:, 0:1]))
                ch.link(tt(dbase[:, 1:E], base[:, 1:E], base[:, 0:E - 1], ALU.subtract))
                full = [P, NT * K, E]
                ch.link(tt(sel[:], slf[:].unsqueeze(2).to_broadcast(full), g["regbase"][:].unsqueeze(1).to_broadcast(full), ALU.is_ge))
                ch.link(tt(sel[:], sel[:], dbase[:].unsqueeze(1).to_broadcast(full), ALU.mult))
                ch.link(v.tensor_reduce(less[:], sel[:], AX.X, ALU.add))
                ch.link(tt(SL, slf[:], less[:], ALU.subtract))

            @block.sync
            def _(sp):
                for d in range(E):
                    sp.dma_start(zd[dummy + d * P:dummy + (d + 1) * P, :], g["zeros"][:]).then_inc(padded, 16)
                sp.wait_ge(run_ready, 1)
                for e in range(E):
                    r = sp.value_load(runi[0:1, e:e + 1], min_val=e * REG, max_val=e * REG + NTOK)
                    sp.dma_start(zd[ds(r, P), :], g["zeros"][:]).then_inc(padded, 16)
                sp.wait_ge(padded, 16 * 2 * E)


def over_tiles(eng, step, n):
    for s in range(-3, 8):
        step(s, s % 4)
    end = 8 + (n - 3 - 8) // 4 * 4
    with eng.Fori(8, end - 3, 4) as s:
        for q in range(4):
            step(s + q, q)
    for s in range(end, n + 3):
        step(s, s % 4)


def phase_experts(nc, a, g, layer):
    if layer == 0:
        tiles, F, zd, yd, EW = TILES0, F0, g["z0"], g["y0"], E + 1
        wh, wl, uh, ul, NF = g["w13h"], g["w13l"], g["w2h"], g["w2l"], 2
        chunks = F0_CHUNKS
    else:
        tiles, F, zd, yd, EW = ROUTED1, F1, g["z1"], g["y1"], E
        wh, wl, uh, ul, NF = g["v1h"], g["v1l"], g["v2h"], g["v2l"], 1
        chunks = [(k * P, P) for k in range(F1 // P)]
    NCH = len(chunks)
    HW = NCH * P
    rows = zd.shape[0]
    with ExitStack() as c:
        sb = lambda n, s, d=F32: c.enter_context(nc.sbuf_tensor(f"e{layer}_{n}", s, d))
        pb = lambda n: c.enter_context(nc.psum_tensor(f"e{layer}_{n}", [P, 512], F32))
        sem = lambda n: phase_semaphore(nc, g, f"e{layer}_{n}")
        NZ = 4
        zs = [sb(f"z_rows{p}", [P, C]) for p in range(NZ)]
        xh = [sb(f"z_high{p}", [P, KC, P], F16) for p in range(2)]
        xl = [sb(f"z_low{p}", [P, KC, P], F16) for p in range(2)]
        act_out = sb("act_out", [P, F])
        hs = [sb(f"hidden{p}", [P, F]) for p in range(2)]
        hh = [sb(f"hidden_high{p}", [P, NCH, P], F16) for p in range(2)]
        hl = [sb(f"hidden_low{p}", [P, NCH, P], F16) for p in range(2)]
        ys = [sb(f"y_rows{p}", [P, C]) for p in range(2)]
        ZT, HT, Y = pb("z_cols"), pb("hidden_cols"), pb("y")
        GU = [[pb(f"first{f}_{p}") for f in range(NF)] for p in range(2)]
        landed, stored = [sem(f"landed{p}") for p in range(NZ)], [sem(f"stored{p}") for p in range(2)]
        turned, zhigh, zlow, first_done, act_done, hidden_done = (sem(x) for x in ("turned", "zhigh", "zlow", "first_done", "act_done", "hidden_done"))
        h_turned, hhigh, hlow, y_done, y_out, blank = (sem(x) for x in ("h_turned", "hhigh", "hlow", "y_done", "y_out", "blank"))
        biased = sem("biased")

        def expert(eng, i):
            return eng.value_load(g["tabexp"][0:1, ds(i, 1)], min_val=0, max_val=EW - 1)

        with nc.Block() as block:
            @block.sync
            def _(sp):
                def step(s, q):
                    i, p = s + 3, (q + 3) % NZ
                    if within(i, tiles):
                        r = sp.value_load(g["tabrow"][0:1, ds(i, 1)], min_val=0, max_val=rows - P)
                        sp.wait_ge(turned, count(i - NZ + 1))
                        sp.dma_start(zs[p][:], zd[ds(r, P), :]).then_inc(landed[p], 16)
                    i, p = s - 2, (q + 2) % 2
                    if within(i, tiles):
                        sp.wait_ge(y_out, i + 1)
                        sp.dma_start(yd[ds(i * P, P), :], ys[p][:]).then_inc(stored[p], 16)
                over_tiles(sp, step, tiles)
                for p in range(2):
                    sp.wait_ge(stored[p], 8 * tiles)

            @block.tensor
            def _(pe):
                pe.wait_ge(blank, 1)

                def step(s, q):
                    i, p = s + 1, (q + 1) % 2
                    if within(i, tiles):
                        z = (q + 1) % NZ
                        pe.wait_ge(landed[z], (i - z) * (16 // NZ) + 16)
                        pe.wait_ge(zlow, count(i))
                        for k in range(KC):
                            ins = pe.transpose(ZT[:, k * P:(k + 1) * P], zs[z][:, k * P:(k + 1) * P], g["ident"][:])
                        ins.then_inc(turned, 1)
                    i, p = s, q % 2
                    if within(i, tiles):
                        e = expert(pe, i)
                        pe.wait_ge(hidden_done, count(i - 1))
                        pe.wait_ge(zlow, i + 1)
                        for k in range(KC):
                            for x, w in ((xh, wh), (xh, wl), (xl, wh)):
                                for f in range(NF):
                                    off = e * (NF * F) + (k * EW * NF * F + f * F)
                                    ins = pe.matmul(GU[p][f][:, 0:F], x[p][:, k, :], w[:, ds(off, F)],
                                                    start=(k == 0 and x is xh and w is wh), stop=(k == KC - 1 and x is xl))
                        ins.then_inc(first_done, 1)
                    i, p = s - 2, q % 2
                    if within(i, tiles):
                        e = expert(pe, i)
                        pe.wait_ge(y_out, count(i))
                        pe.wait_ge(hlow, i + 1)
                        for n, (o, m) in enumerate(chunks):
                            for x, w in ((hh, uh), (hh, ul), (hl, uh)):
                                ins = pe.matmul(Y[:, 0:C], x[p][0:m, n, :], w[0:m, ds(e * C + n * EW * C, C)],
                                                start=(n == 0 and x is hh and w is uh), stop=(n == NCH - 1 and x is hl))
                        ins.then_inc(y_done, 1)
                    i, p = s - 1, (q + 1) % 2
                    if within(i, tiles):
                        pe.wait_ge(hlow, count(i))
                        pe.wait_ge(hidden_done, i + 1)
                        for n, (o, m) in enumerate(chunks):
                            ins = pe.transpose(HT[0:m, n * P:(n + 1) * P], hs[p][:, o:o + m], g["ident"][:])
                        ins.then_inc(h_turned, 1)
                over_tiles(pe, step, tiles)

            @block.scalar
            def _(act):
                def step(s, q):
                    i, p = s + 1, (q + 1) % 2
                    if within(i, tiles):
                        act.wait_ge(first_done, count(i - 1))
                        act.wait_ge(turned, i + 1)
                        act.activation(xh[p][:].rearrange("p k s -> p (k s)"), ZT[:, 0:KC * P], ACT.Copy).then_inc(zhigh, 1)
                    i, p = s, q % 2
                    if within(i, tiles):
                        if layer == 0:
                            act.wait_ge(hidden_done, count(i))
                            act.wait_ge(first_done, i + 1)
                            act.activation(act_out[:], GU[p][0][:, 0:F], ACT.Silu, scale=1.0 / WSCALE).then_inc(act_done, 1)
                        else:
                            act.wait_ge(h_turned, count(i - 1))
                            act.wait_ge(biased, i + 1)
                            act.activation(hs[p][:], act_out[:], ACT.Gelu).then_inc(hidden_done, 1)
                    i, p = s - 2, q % 2
                    if within(i, tiles) and layer == 0:
                        act.wait_ge(stored[p], count((i - p) * 8))
                        act.wait_ge(y_done, i + 1)
                        act.activation(ys[p][:], Y[:, 0:C], ACT.Copy, scale=1.0 / WSCALE).then_inc(y_out, 1)
                    i, p = s - 1, (q + 1) % 2
                    if within(i, tiles):
                        act.wait_ge(y_done, count(i - 1))
                        act.wait_ge(h_turned, i + 1)
                        act.activation(hh[p][:].rearrange("p k s -> p (k s)"), HT[:, 0:HW], ACT.Copy).then_inc(hhigh, 1)
                over_tiles(act, step, tiles)

            @block.vector
            def _(v):
                v.memset(HT[:], 0.0).then_inc(blank, 1)

                def step(s, q):
                    i, p = s + 1, (q + 1) % 2
                    if within(i, tiles):
                        v.wait_ge(first_done, count(i - 1))
                        v.wait_ge(zhigh, i + 1)
                        v.tensor_tensor(xl[p][:].rearrange("p k s -> p (k s)"), ZT[:, 0:KC * P], xh[p][:].rearrange("p k s -> p (k s)"), ALU.subtract).then_inc(zlow, 1)
                    i, p = s, q % 2
                    if within(i, tiles):
                        if layer == 0:
                            v.wait_ge(h_turned, count(i - 1))
                            v.wait_ge(act_done, i + 1)
                            v.scalar_tensor_tensor(hs[p][:], GU[p][1][:, 0:F], 1.0 / WSCALE, act_out[:], ALU.mult, ALU.mult).then_inc(hidden_done, 1)
                        else:
                            e = expert(v, i)
                            v.wait_ge(hidden_done, count(i))
                            v.wait_ge(first_done, i + 1)
                            v.scalar_tensor_tensor(act_out[:], GU[p][0][:, 0:F], 1.0 / WSCALE, g["b1"][:, ds(e * F, F)], ALU.mult, ALU.add).then_inc(biased, 1)
                    i, p = s - 2, q % 2
                    if within(i, tiles) and layer == 1:
                        e = expert(v, i)
                        v.wait_ge(stored[p], count((i - p) * 8))
                        v.wait_ge(y_done, i + 1)
                        v.scalar_tensor_tensor(ys[p][:], Y[:, 0:C], 1.0 / WSCALE, g["b2"][:, ds(e * C, C)], ALU.mult, ALU.add).then_inc(y_out, 1)
                    i, p = s - 1, (q + 1) % 2
                    if within(i, tiles):
                        v.wait_ge(y_done, count(i - 1))
                        v.wait_ge(hhigh, i + 1)
                        v.tensor_tensor(hl[p][:].rearrange("p k s -> p (k s)"), HT[:, 0:HW], hh[p][:].rearrange("p k s -> p (k s)"), ALU.subtract).then_inc(hlow, 1)
                over_tiles(v, step, tiles)


def gather(pool, idx, k, t, rows, dst, done):
    pool.indirect_dma_start(dst, None, rows, bass.IndirectOffsetOnAxis(ap=idx[:, k, t:t + 1], axis=0)).then_inc(done, 16)


def phase_attn1(nc, a, g):
    with ExitStack() as c:
        sb = lambda n, s, d=F32: c.enter_context(nc.sbuf_tensor(f"a1_{n}", s, d))
        pb = lambda n: c.enter_context(nc.psum_tensor(f"a1_{n}", [P, 512], F32))
        sem = lambda n: phase_semaphore(nc, g, f"a1_{n}")
        wq, wk, wv = sb("wq", [P, KC, C]), sb("wk", [P, 2, C]), sb("wv", [P, 2, C])
        bq, bk, bv = sb("bq", [P, KC]), sb("bk", [P, KC]), sb("bv", [P, C])
        w_red, wg1, wgn, wg = sb("w_red", [16, C]), sb("wg1", [E, 16]), sb("wg_norm", [16, E]), sb("wg_joint", [P, KC, E])
        wsq, wnorm = sb("wg_squares", [E, 16]), sb("wg_norms", [E, 1])
        idx = [sb(f"slots{p}", [P, 2, T], I32) for p in range(2)]
        pr = [sb(f"probs_chosen{p}", [P, T, 2]) for p in range(2)]
        yk = [sb(f"y_chosen{p}", [P, 2, T, C]) for p in range(2)]
        ysh = [sb(f"y_shared{p}", [P, T, C]) for p in range(2)]
        cin = [sb(f"ctx_in{p}", [P, T, DC]) for p in range(2)]
        st, mv, r1 = sb("stats", [P, T, 6]), sb("mean_var", [P, T, 2]), sb("rstd", [P, T])
        xn = sb("x_norm", [P, T, C])
        lT, cT = sb("x_cols", [P, KC, S]), sb("ctx_cols", [P, 2, S])
        qT = [sb(f"q_cols{p}", [P, KC, S]) for p in range(2)]
        kT = [sb(f"k_cols{p}", [P, KC, S]) for p in range(2)]
        vt = [sb(f"v_tokens{p}", [P, T, C]) for p in range(2)]
        nmax, esum, rs = sb("minus_max", [P, T]), sb("exp_sum", [P, T]), sb("exp_rsum", [P, T])
        pm, pT = sb("probs", [P, T, S]), sb("prob_cols", [P, T, S])
        BT, BC = pb("turn"), pb("turn_ctx")
        PJ = [pb("proj0"), pb("proj1")]
        SC, PT, O, R = pb("scores"), pb("prob_turn"), pb("out"), pb("route")
        rt = Route(nc, g, c, "r1", 1, g["SL1"], g["PR1"], g["RUN1"], g["z1"], wg)

        consts_in, consts_ready, cstep, wg_turned, wg_norms = (sem(x) for x in ("consts_in", "consts_ready", "cstep", "wg_turned", "wg_norms"))
        landed_y, landed_c = [sem(f"landed_y{p}") for p in range(2)], [sem(f"landed_ctx{p}") for p in range(2)]
        gathered = [sem(f"gathered{p}") for p in range(2)]
        slots_ready, s1_x2, s1_stats, s1_rstd, s1_norm, s1_turned, s1_cols = (sem(f"s1_{x}") for x in ("slots", "x2", "stats", "rstd", "norm", "turned", "cols"))
        proj_ready, freed_act, freed_dve = sem("proj_ready"), sem("proj_freed_act"), sem("proj_freed_dve")
        scored, maxed, expd, p_turned, p_cols, pv = (sem(x) for x in ("scored", "maxed", "expd", "p_turned", "p_cols", "pv"))
        d1, d2, p1 = sem("dve_step1"), sem("dve_step2"), sem("pool_step1")
        D1, D2, P1 = 7, 4, 2
        loads = [(wq[:], a["wq1"].rearrange("(k p) f -> p k f", p=P)),
                 (wk[:, 0, :], a["wk1"][0:P]), (wk[0:DC - P, 1, :], a["wk1"][P:DC]),
                 (wv[:, 0, :], a["wv1"][0:P]), (wv[0:DC - P, 1, :], a["wv1"][P:DC]),
                 (bv[:], a["bv1"].rearrange("(o n) -> o n", o=1).to_broadcast([P, C])),
                 (w_red[:], a["w_red"]), (wg1[:], a["wg1"])] + \
                [(t[:, k:k + 1], a[n][k * P:(k + 1) * P].rearrange("(p o) -> p o", o=1)) for t, n in ((bq, "bq1"), (bk, "bk1")) for k in range(KC)]
        n_consts = 16 * len(loads)

        with nc.Block() as block:
            @block.sync
            def _(sp):
                for dst, src in loads:
                    sp.dma_start(dst, src).then_inc(consts_in, 16)

                def load_y(m, p):
                    sp.wait_ge(s1_x2, count(m - 1))
                    sp.dma_start(ysh[p][:], g["y0"][ds(m * S + ROUTED0 * P, S), :].rearrange("(t p) c -> p t c", p=P)).then_inc(landed_y[p], 16)

                def load_ctx(m, p):
                    sp.wait_ge(s1_turned, count(m - 1))
                    sp.dma_start(cin[p][:], a["ctx"][ds(m * S, S), :].rearrange("(t p) c -> p t c", p=P)).then_inc(landed_c[p], 16)

                def step(n, q):
                    if within(n + 4, B):
                        load_y(n + 4, q)
                    if within(n + 3, B):
                        load_ctx(n + 3, 1 - q)
                over_batches(sp, -4, step, B - 5)
                rt.finish(sp, False)

            @block.gpsimd
            def _(pool):
                pool.wait_ge(wg_norms, 1)
                pool.tensor_tensor(wnorm[:], wnorm[:], g["mhalf"][0:E, 0:1], ALU.pow).then_inc(wg_norms, 1)

                def fetch(n, p):
                    pool.wait_ge(slots_ready, n + 1)
                    pool.sem_inc(g["carried"], 1)
                    for k in range(2):
                        for t in range(T):
                            gather(pool, idx[p], k, t, g["y0"], yk[p][:, k, t, :], gathered[p])

                def rstd(m):
                    ch = Chain(pool, p1, m * P1)
                    pool.wait_ge(s1_stats, m + 1)
                    ch.link(pool.tensor_tensor(r1[:], mv[:, :, 1], g["epst"][:, 0:T], ALU.add))
                    ch.link(pool.tensor_tensor(r1[:], r1[:], g["mhalf"][:, 0:T], ALU.pow))
                    pool.sem_inc(s1_rstd, 1)
                    assert ch.n == P1

                def step(n, q):
                    if within(n - 1, B):
                        rt.pool_rstd(pool, n - 1)
                    if within(n + 2, B):
                        rstd(n + 2)
                    if within(n + 4, B):
                        fetch(n + 4, q)
                    if within(n - 2, B):
                        rt.pool_scatter(pool, n - 2, q)
                over_batches(pool, -4, step, B - 5)

            @block.scalar
            def _(act):
                act.wait_ge(consts_ready, 1)

                def columns(m):
                    act.wait_ge(proj_ready, count(3 * m))
                    act.wait_ge(s1_turned, m + 1)
                    act.activation(lT[:].rearrange("p k s -> p (k s)"), BT[:], ACT.Copy)
                    for k, (o, w) in enumerate(CTX_CHUNKS):
                        ins = act.activation(cT[0:w, k, :], BC[0:w, k * S:(k + 1) * S], ACT.Copy)
                    ins.then_inc(s1_cols, 1)

                def bias_qk(m, p):
                    act.wait_ge(scored, count(m - 1))
                    for i, (dst, b) in enumerate(((qT, bq), (kT, bk))):
                        act.wait_ge(proj_ready, 3 * m + 1 + i)
                        for k in range(KC):
                            ins = act.activation(dst[p][:, k, :], PJ[i][:, k * S:(k + 1) * S], ACT.Identity, bias=b[:, k:k + 1])
                        ins.then_inc(freed_act, 1)

                def exps(n):
                    act.wait_ge(p_turned, count(n))
                    act.wait_ge(maxed, n + 1)
                    for t in range(T):
                        ins = act.activation(pm[:, t, :], SC[:, t * S:(t + 1) * S], ACT.Exp, bias=nmax[:, t:t + 1], accum_out=esum[:, t:t + 1])
                    ins.then_inc(expd, 1)

                def prob_columns(n):
                    act.wait_ge(pv, count(n))
                    act.wait_ge(p_turned, n + 1)
                    act.activation(pT[:].rearrange("p j s -> p (j s)"), PT[:], ACT.Copy).then_inc(p_cols, 1)

                def step(n, q):
                    core, front, tail = within(n, B), within(n + 1, B), within(n - 1, B)
                    if front:
                        columns(n + 1)
                    if core:
                        exps(n)
                    if tail:
                        rt.act_cols(act, n - 1, O[:].rearrange("p (k s) -> p k s", k=KC))
                    if core:
                        prob_columns(n)
                    if front:
                        bias_qk(n + 1, 1 - q)
                    if tail:
                        rt.act_exp(act, n - 1)
                over_batches(act, -1, step)

            @block.vector
            def _(v):
                v.wait_ge(consts_in, n_consts)
                ch = Chain(v, cstep)
                ch.link(v.tensor_tensor(wsq[:], wg1[:], wg1[:], ALU.mult))
                ch.link(v.tensor_reduce(wnorm[:], wsq[:], AX.X, ALU.add))
                ch.link(v.tensor_scalar(wnorm[:], wnorm[:], 1e-8, None, ALU.max))
                v.sem_inc(wg_norms, 1)
                v.wait_ge(wg_norms, 2)
                ch.link(v.tensor_scalar(wg1[:], wg1[:], wnorm[:, 0:1], None, ALU.mult))
                v.sem_inc(consts_ready, 1)
                v.wait_ge(wg_turned, 1)
                ch.link(v.tensor_copy(wgn[:], R[0:16, 0:E]))
                v.sem_inc(consts_ready, 1)
                v.wait_ge(wg_turned, 2)
                ch.link(v.tensor_copy(wg[:].rearrange("p k e -> p (k e)"), R[:, 16:16 + KC * E]))
                v.sem_inc(consts_ready, 1)

                chains = {}

                def slots(m, p):
                    v.wait_ge(gathered[p], count((m - p) * 32))
                    v.tensor_copy(pr[p][:], g["PR0"][:, ds(m * T, T), :])
                    v.tensor_copy(idx[p][:].rearrange("p k t -> p t k"), g["SL0"][:, ds(m * T, T), :]).then_inc(slots_ready, 1)

                def pre_x2(m, p):
                    ch = Chain(v, d1, m * D1)
                    xr = g["XR"][:, ds(m * T, T), :]
                    v.wait_ge(landed_y[p], (m - p) * 8 + 16)
                    v.wait_ge(gathered[p], (m - p) * 32 + 64)
                    for k in range(2):
                        for t in range(T):
                            ch.mark(v.scalar_tensor_tensor(ysh[p][:, t, :], yk[p][:, k, t, :], pr[p][:, t, k:k + 1], ysh[p][:, t, :], ALU.mult, ALU.add))
                        ch.wait()
                    ch.link(v.scalar_tensor_tensor(xr, ysh[p][:], g["gate"][:, 2:3], xr, ALU.mult, ALU.add))
                    v.sem_inc(s1_x2, 1)
                    x = XRTile(g["XR"], m)
                    for t in range(T):
                        ch.mark(v.bn_stats(st[:, t, :], x[:, t, :]))
                    ch.wait()
                    v.sem_inc(g["carried_v"], 1)
                    for t in range(T):
                        ins = v.bn_aggr(mv[:, t, :], st[:, t, :])
                    ins.then_inc(s1_stats, 1)
                    assert ch.n == D1, ch.n

                def pre_norm(m):
                    v.wait_ge(s1_turned, count(m))
                    v.wait_ge(s1_rstd, m + 1)
                    x = XRTile(g["XR"], m)
                    for t in range(T):
                        ins = v.tensor_scalar(xn[:, t, :], x[:, t, :], mv[:, t, 0:1], r1[:, t:t + 1], ALU.subtract, ALU.mult)
                    ins.then_inc(s1_norm, 1)

                def bias_v(m, p):
                    v.wait_ge(pv, count(m - 1))
                    v.wait_ge(proj_ready, 3 * m + 3)
                    v.tensor_tensor(vt[p][:], PJ[0][:].rearrange("p (t c) -> p t c", t=T), bv[:].unsqueeze(1).to_broadcast([P, T, C]), ALU.add).then_inc(freed_dve, 1)

                def maxima(n):
                    v.wait_ge(expd, count(n))
                    v.wait_ge(scored, n + 1)
                    v.tensor_reduce(nmax[:], SC[:].rearrange("p (t s) -> p t s", t=T), AX.X, ALU.max, negate=True).then_inc(maxed, 1)

                def tail_x3(m):
                    ch = Chain(v, d2, m * D2)
                    v.wait_ge(expd, m + 1)
                    ch.link(v.reciprocal(rs[:], esum[:]))
                    ch.link(v.tensor_scalar(rs[:], rs[:], g["gate"][:, 1:2], None, ALU.mult))
                    v.wait_ge(pv, m + 1)
                    xr = XRTile(g["XR"], m)
                    for t in range(T):
                        ch.mark(v.scalar_tensor_tensor(xr[:, t, :], O[:, t * C:(t + 1) * C], rs[:, t:t + 1], xr[:, t, :], ALU.mult, ALU.add))
                    ch.wait()
                    assert ch.n == D2, ch.n
                    chains["route"] = Chain(v, rt.step, m * rt.steps)
                    rt.vector_stats(v, m, xr, chains["route"])

                def step(n, q):
                    core, front, tail = within(n, B), within(n + 1, B), within(n - 1, B)
                    m = n - 1
                    if within(n - 2, B):
                        rt.vector_slots(v, n - 2, q, R[:, 128:128 + (T + 1) * E].rearrange("p (t e) -> p t e", t=T + 1))
                    if tail:
                        tail_x3(m)
                    if core:
                        maxima(n)
                    if within(n + 2, B):
                        pre_x2(n + 2, q)
                    if tail:
                        rt.vector_z(v, m, 1 - q, XRTile(g["XR"], m), False)
                    if within(n + 4, B):
                        slots(n + 4, q)
                    if within(n + 2, B):
                        pre_norm(n + 2)
                    if front:
                        bias_v(n + 1, 1 - q)
                    if tail:
                        rt.vector_choose(v, m, 1 - q, R[:, 0:T * E].rearrange("p (t e) -> p t e", t=T), chains["route"])
                over_batches(v, -4, step, B - 5)

            @block.tensor
            def _(pe):
                ident = g["ident"]
                pe.wait_ge(consts_ready, 1)
                pe.transpose(R[0:16, 0:E], wg1[:], ident[0:E, 0:E]).then_inc(wg_turned, 1)
                pe.wait_ge(consts_ready, 2)
                for k in range(KC):
                    ins = pe.matmul(R[:, 16 + k * E:16 + (k + 1) * E], w_red[:, k * P:(k + 1) * P], wgn[:], start=True, stop=True)
                ins.then_inc(wg_turned, 1)
                pe.wait_ge(consts_ready, 3)

                def turn(m, p):
                    pe.wait_ge(s1_norm, m + 1)
                    pe.wait_ge(s1_cols, count(m))
                    for k in range(KC):
                        for t in range(T):
                            pe.transpose(BT[:, k * S + t * P:k * S + (t + 1) * P], xn[:, t, k * P:(k + 1) * P], ident[:])
                    pe.wait_ge(landed_c[p], (m - p) * 8 + 16)
                    for k, (o, w) in enumerate(CTX_CHUNKS):
                        for t in range(T):
                            ins = pe.transpose(BC[0:w, k * S + t * P:k * S + (t + 1) * P], cin[p][:, t, o:o + w], ident[:])
                    ins.then_inc(s1_turned, 1)

                def project_qk(m):
                    pe.wait_ge(s1_cols, m + 1)
                    pe.wait_ge(freed_dve, count(m))
                    for i in range(KC):
                        for k in range(KC):
                            ins = pe.matmul(PJ[0][:, i * S:(i + 1) * S], wq[:, k, i * P:(i + 1) * P], lT[:, k, :], start=k == 0, stop=k == KC - 1)
                    ins.then_inc(proj_ready, 1)
                    pe.wait_ge(freed_act, count(2 * m))
                    for i in range(KC):
                        for k, (o, w) in enumerate(CTX_CHUNKS):
                            ins = pe.matmul(PJ[1][:, i * S:(i + 1) * S], wk[0:w, k, i * P:(i + 1) * P], cT[0:w, k, :], start=k == 0, stop=k == 1)
                    ins.then_inc(proj_ready, 1)

                def project_v(m):
                    pe.wait_ge(freed_act, 2 * m + 1)
                    for t in range(T):
                        for k, (o, w) in enumerate(CTX_CHUNKS):
                            ins = pe.matmul(PJ[0][:, t * C:(t + 1) * C], cT[0:w, k, t * P:(t + 1) * P], wv[0:w, k, :], start=k == 0, stop=k == 1)
                    ins.then_inc(proj_ready, 1)

                def score(n, p):
                    pe.wait_ge(freed_act, 2 * n + 2)
                    pe.wait_ge(expd, count(n))
                    for t in range(T):
                        for k in range(KC):
                            ins = pe.matmul(SC[:, t * S:(t + 1) * S], qT[p][:, k, t * P:(t + 1) * P], kT[p][:, k, :], start=k == 0, stop=k == KC - 1)
                    ins.then_inc(scored, 1)

                def turn_probs(n):
                    pe.wait_ge(p_cols, count(n))
                    pe.wait_ge(expd, n + 1)
                    for j in range(T):
                        for t in range(T):
                            ins = pe.transpose(PT[:, j * S + t * P:j * S + (t + 1) * P], pm[:, t, j * P:(j + 1) * P], ident[:])
                    ins.then_inc(p_turned, 1)

                def products(n, p):
                    pe.wait_ge(rt.cols_ready, count(n))
                    pe.wait_ge(freed_dve, n + 1)
                    pe.wait_ge(p_cols, n + 1)
                    for t in range(T):
                        for j in range(T):
                            ins = pe.matmul(O[:, t * C:(t + 1) * C], pT[:, j, t * P:(t + 1) * P], vt[p][:, j, :], start=j == 0, stop=j == T - 1)
                    ins.then_inc(pv, 1)

                def step(n, q):
                    core, front, tail = within(n, B), within(n + 1, B), within(n - 1, B)
                    m = n - 1
                    if within(n - 2, B):
                        rt.pe_prefix(pe, n - 2, R[:, 128:128 + (T + 1) * E].rearrange("p (t e) -> p t e", t=T + 1))
                    if front:
                        turn(n + 1, 1 - q)
                    if core:
                        score(n, q)
                    if front:
                        project_qk(n + 1)
                    if tail:
                        rt.pe_turn(pe, m, 1 - q, O[:].rearrange("p (k s) -> p k s", k=KC))
                    if core:
                        turn_probs(n)
                    if front:
                        project_v(n + 1)
                    if tail:
                        pe.wait_ge(rt.idx_ready, count(m))
                        rt.pe_logits(pe, m, R[:, 0:T * E].rearrange("p (t e) -> p t e", t=T))
                    if core:
                        products(n, q)
                over_batches(pe, -1, step)


def phase_out(nc, a, g, out):
    with ExitStack() as c:
        sb = lambda n, s, d=F32: c.enter_context(nc.sbuf_tensor(f"o_{n}", s, d))
        sem = lambda n: phase_semaphore(nc, g, f"o_{n}")
        NB = 4
        prs = sb("scaled_probs", [P, NT])
        idx = [sb(f"slots{p}", [P, 1, T], I32) for p in range(NB)]
        y = [sb(f"y{p}", [P, T, C]) for p in range(NB)]
        o = [sb(f"x4_{p}", [P, T, C]) for p in range(NB)]
        pb = [sb(f"scale{p}", [P, T]) for p in range(NB)]
        scaled, slots_ready, done = sem("scaled"), sem("slots_ready"), sem("done")
        gathered, stored = [sem(f"gathered{p}") for p in range(NB)], [sem(f"stored{p}") for p in range(NB)]
        with nc.Block() as block:
            @block.vector
            def _(v):
                v.tensor_scalar(prs[:], g["PR1"][:].rearrange("p n o -> p (n o)"), g["gate"][:, 3:4], None, ALU.mult).then_inc(scaled, 1)
                v.wait_ge(scaled, 1)

                def slots(n, p):
                    v.wait_ge(done, count(n - NB + 1))
                    v.tensor_copy(pb[p][:], prs[:, ds(n * T, T)])
                    v.tensor_copy(idx[p][:].rearrange("p k t -> p t k"), g["SL1"][:, ds(n * T, T), :]).then_inc(slots_ready, 1)

                def add(n, p):
                    v.wait_ge(slots_ready, n + 1)
                    v.wait_ge(stored[p], count((n - p) * (16 // NB)))
                    v.wait_ge(gathered[p], count((n - p) * (32 // NB) + 32))
                    for t in range(T):
                        ins = v.scalar_tensor_tensor(o[p][:, t, :], y[p][:, t, :], pb[p][:, t:t + 1], XRTile(g["XR"], n)[:, t, :], ALU.mult, ALU.add)
                    ins.then_inc(done, 1)
                for p in range(NB):
                    slots(p, p)
                for p in range(NB):
                    add(p, p)
                    slots(p + NB, p)
                with v.Fori(NB, B - 2 * NB + 1, NB) as n:
                    for p in range(NB):
                        add(n + p, p)
                        slots(n + p + NB, p)
                for p in range(NB):
                    add(B - NB + p, p)

            @block.gpsimd
            def _(pool):
                with pool.Fori(0, B - NB + 1, NB) as n:
                    for p in range(NB):
                        pool.wait_ge(slots_ready, n + p + 1)
                        pool.sem_inc(g["carried"], 1)
                        for t in range(T):
                            gather(pool, idx[p], 0, t, g["y1"], y[p][:, t, :], gathered[p])

            @block.sync
            def _(sp):
                with sp.Fori(0, B - NB + 1, NB) as n:
                    for p in range(NB):
                        sp.wait_ge(done, n + p + 1)
                        sp.dma_start(out[ds((n + p) * S, S), :].rearrange("(t p) c -> p t c", p=P), o[p][:]).then_inc(stored[p], 16)
                for p in range(NB):
                    sp.wait_ge(stored[p], B // NB * 16)


def lay_out(inputs):
    i = {k: np.asarray(v) for k, v in inputs.items()}
    T_ = lambda x: np.ascontiguousarray(np.swapaxes(x, -1, -2))
    return {
        "x": i["x"].reshape(NTOK, C), "ctx": i["ctx_768"].reshape(NTOK, DC),
        "mask": np.ascontiguousarray(i["mask_BxS2_bk0"].reshape(B * T, P).T),
        "g_xattn": i["g_xattn"], "g_ffn": i["g_ffn"],
        "ln_x_g": i["L0_xattn_ln_x_g"], "ln_x_b": i["L0_xattn_ln_x_b"], "ln_l_g": i["L0_xattn_ln_l_g"], "ln_l_b": i["L0_xattn_ln_l_b"],
        "qn": i["L0_xattn_qn_g"], "kn": i["L0_xattn_kn_g"],
        "wq0": T_(i["L0_xattn_Wq"]), "wkv0": T_(i["L0_xattn_Wkv"]), "wlkv0": T_(i["L0_xattn_Wlkv"]), "wo0": T_(i["L0_xattn_Wo"]), "bo0": i["L0_xattn_bo"],
        "wg0": T_(i["L0_ffn_Wg"]),
        "w13": np.concatenate([np.concatenate([T_(i["L0_ffn_W1"]), T_(i["L0_ffn_Ws1"])[None]]),
                               np.concatenate([T_(i["L0_ffn_W2"]), T_(i["L0_ffn_Ws2"])[None]])], axis=2),
        "w2": np.concatenate([T_(i["L0_ffn_W3"]), T_(i["L0_ffn_Ws3"])[None]]),
        "wq1": i["L1_xattn_Wq"], "bq1": i["L1_xattn_bq"], "wk1": i["L1_xattn_Wk"], "bk1": i["L1_xattn_bk"],
        "wv1": i["L1_xattn_Wv"], "bv1": i["L1_xattn_bv"],
        "w_red": T_(i["L1_ffn_w_red"]), "wg1": i["L1_ffn_wg"],
        "v1": i["L1_ffn_W1"], "b1": i["L1_ffn_b1"], "v2": i["L1_ffn_W2"], "b2": i["L1_ffn_b2"],
    }


def kernel(**inputs):
    import concourse.bacc as bacc
    from concourse.bass_utils import run_bass_kernel_spmd

    nc = bacc.Bacc("TRN2", target_bir_lowering=False, num_devices=1)
    arrays, args = {}, {}
    for name, array in lay_out(inputs).items():
        array = np.ascontiguousarray(array)
        arrays[f"in_{name}"] = array
        args[name] = nc.dram_tensor(f"in_{name}", array.shape, mybir.dt.from_np(array.dtype), kind="ExternalInput").ap()
    out = nc.dram_tensor("out_x", (NTOK, C), F32, kind="ExternalOutput").ap()
    program(nc, args, out)
    result = run_bass_kernel_spmd(nc, [arrays], core_ids=[0])
    return np.asarray(result.results[0]["out_x"]).reshape(B, S, C)
```

```python
import numpy as np
import concourse.bass as bass
from concourse import mybir
from contextlib import ExitStack

F32 = mybir.dt.float32
F16 = mybir.dt.float16
I32 = mybir.dt.int32
U8 = mybir.dt.uint8
ALU = mybir.AluOpType
ACT = mybir.ActivationFunctionType
AX = mybir.AxisListType
ds = bass.ds

P = 128
B, S, C = 16, 256, 256
DC = 192
H, D = 4, 64
T = S // P
KC = C // P
NT = B * T
NTOK = B * S
E = 8
CTX_CHUNKS = [(0, P), (P, DC - P)]
F0 = 352
F0_CHUNKS = [(0, P), (P, P), (2 * P, F0 - 2 * P)]
F1 = 512
REG = NTOK + P
SHARED = E * REG
DUMMY0 = SHARED + NTOK
DUMMY1 = E * REG
WSCALE = 64.0
ROUTED0 = 2 * NT + E - 1
ROUTED1 = NT + E - 1
TILES0 = ROUTED0 + NT
TOKEN, NUMBER, SCALE, W1 = C, 2 * C, 2 * C + 1, 2 * C + 2
EPS = 1e-5
BIG = 1e30


class Chain:

    def __init__(self, eng, sem, base=0):
        self.eng, self.sem, self.base, self.n = eng, sem, base, 0

    def link(self, ins):
        self.mark(ins)
        self.wait()

    def mark(self, ins):
        self.n += 1
        ins.then_inc(self.sem, 1)

    def wait(self):
        self.eng.wait_ge(self.sem, self.base + self.n)


def phase_semaphore(nc, g, name):
    g["semaphores"].append(nc.alloc_semaphore(name=name))
    return g["semaphores"][-1]


def end_of_phase(nc, g):
    nc.clear_and_free_semaphores(g["semaphores"])
    nc.all_engine_barrier()
    g["semaphores"] = []


def program(nc, a, out):
    root = ExitStack()
    with root:
        def sb(name, shape, dt=F32, ctx=root):
            return ctx.enter_context(nc.sbuf_tensor(name, shape, dt))

        def sem(name, ctx=root):
            return ctx.enter_context(nc.semaphore(name))

        def dram(name, shape, dt=F32):
            return nc.dram_tensor(name, shape, dt, kind="Internal").ap()

        g = {"semaphores": []}
        g["z0"] = dram("z0_rows", (DUMMY0 + E * P, C))
        g["y0"] = dram("y0_rows", (TILES0 * P, C))
        g["z1"] = dram("z1_rows", (DUMMY1 + E * P, W1))
        g["XR"] = sb("residual", [P, NT, C])
        g["ident"] = sb("ident", [P, P])
        g["ones"] = sb("ones", [P, P], F16)
        g["triu"] = sb("strictly_upper", [P, P], F16)
        g["headsel"] = sb("head_select", [P, 2])
        g["reviota"] = sb("reverse_iota", [P, T, E])
        g["regbase"] = sb("region_base", [P, E])
        g["mhalf"] = sb("minus_half", [P, 32])
        g["epst"] = sb("eps_tile", [P, 4])
        g["gate"] = sb("tanh_gates", [P, 4])
        g["SL0"] = sb("slots0", [P, NT, 2], I32)
        g["PR0"] = sb("probs0", [P, NT, 2])
        g["base_steps"] = sb("base_steps", [P, E])
        g["RUN0"] = sb("running0", [P, E])
        g["RUN1"] = sb("running1", [P, E])
        g["tabrow"] = sb("tile_rows", [1, TILES0], I32)
        g["tabexp"] = sb("tile_experts", [1, TILES0], I32)
        g["carried"], g["carried_v"], g["carried_a"] = sem("carried_pool"), sem("carried_dve"), sem("carried_act")
        g["padding"] = sb("padding_rows", [P, W1])
        with ExitStack() as l0:
            g["w13h"] = sb("w13_high", [P, KC * (E + 1) * 2 * F0], F16, l0)
            g["w13l"] = sb("w13_low", [P, KC * (E + 1) * 2 * F0], F16, l0)
            g["w2h"] = sb("w2_high", [P, 3 * (E + 1) * C], F16, l0)
            g["w2l"] = sb("w2_low", [P, 3 * (E + 1) * C], F16, l0)
            phase_constants(nc, a, g)
            end_of_phase(nc, g)
            phase_attn0(nc, a, g)
            end_of_phase(nc, g)
            phase_experts(nc, a, g, 0)
            end_of_phase(nc, g)
        with ExitStack() as l1:
            g["v1h"] = sb("v1_high", [P, KC * E * F1], F16, l1)
            g["v1l"] = sb("v1_low", [P, KC * E * F1], F16, l1)
            g["v2h"] = sb("v2_high", [P, 4 * E * C], F16, l1)
            g["v2l"] = sb("v2_low", [P, 4 * E * C], F16, l1)
            g["b1"] = sb("b1_rows", [P, E * F1], F32, l1)
            g["b2"] = sb("b2_rows", [P, E * C], F32, l1)
            phase_attn1(nc, a, g)
            end_of_phase(nc, g)
            phase_experts(nc, a, g, 1, out)
            end_of_phase(nc, g)


def phase_constants(nc, a, g):
    with ExitStack() as c:
        sem = lambda n: phase_semaphore(nc, g, n)
        filled, chosen, gates_in, gates_done = sem("c_filled"), sem("c_chosen"), sem("c_gates_in"), sem("c_gates_done")
        graw = c.enter_context(nc.sbuf_tensor("gates_raw", [P, 4], F32))
        with nc.Block() as block:
            @block.sync
            def _(sp):
                sp.dma_start(graw[:, 0:2], a["g_xattn"].rearrange("(o n) -> o n", o=1).to_broadcast([P, 2])).then_inc(gates_in, 16)
                sp.dma_start(graw[:, 2:4], a["g_ffn"].rearrange("(o n) -> o n", o=1).to_broadcast([P, 2])).then_inc(gates_in, 16)

            @block.scalar
            def _(act):
                act.wait_ge(gates_in, 32)
                act.activation(g["gate"][:], graw[:], ACT.Tanh).then_inc(gates_done, 1)

            @block.vector
            def _(v):
                v.memset(g["ones"][:], 1.0)
                v.memset(g["mhalf"][:], -0.5)
                v.memset(g["epst"][:], EPS)
                v.memset(g["padding"][:], 0.0)
                v.memset(g["headsel"][:], 0.0).then_inc(filled, 1)
                v.wait_ge(filled, 1)
                v.memset(g["headsel"][0:D, 0:1], 1.0)
                v.memset(g["padding"][:, NUMBER:NUMBER + 1], float(NTOK))
                v.memset(g["headsel"][D:P, 1:2], 1.0)
                for e in range(E):
                    v.memset(g["regbase"][:, e:e + 1], float(e * REG))
                    v.memset(g["RUN0"][:, e:e + 1], float(e * REG))
                    v.memset(g["RUN1"][:, e:e + 1], float(e * REG))
                    v.memset(g["reviota"][:, :, e:e + 1], float(E - e))

            @block.gpsimd
            def _(pool):
                pool.memset(g["ident"][:], 0.0).then_inc(chosen, 1)
                pool.memset(g["triu"][:], 1.0).then_inc(chosen, 1)
                pool.wait_ge(chosen, 2)
                pool.affine_select(out=g["ident"][:], in_=g["ident"][:], compare_op=ALU.not_equal, fill=1.0,
                                   base=0, pattern=[[-1, P]], channel_multiplier=1)
                pool.affine_select(out=g["triu"][:], in_=g["triu"][:], compare_op=ALU.is_gt, fill=0.0,
                                   base=0, pattern=[[1, P]], channel_multiplier=-1)


class Weights:

    def __init__(self, nc, g, a, c, layer):
        self.g, self.layer = g, layer
        if layer == 0:
            self.parts, self.first_rows, self.second_rows = 2 * (E + 1), a["w13"], a["w2"]
            self.F, self.EW, names = 2 * F0, E + 1, ("w13h", "w13l", "w2h", "w2l")
        else:
            self.parts, self.first_rows, self.second_rows = 2 * E, a["v1"], a["v2"]
            self.F, self.EW, names = F1, E, ("v1h", "v1l", "v2h", "v2l")
        self.first_rows = self.first_rows.rearrange("e c f -> (e c) f")
        self.second_rows = self.second_rows.rearrange("e f c -> (e f) c")
        self.high1, self.low1, self.high2, self.low2 = (g[x][:] for x in names)
        self.stage1 = [c.enter_context(nc.sbuf_tensor(f"w{layer}_stage_first{p}", [P, self.F], F32)) for p in range(2)]
        self.stage2 = [c.enter_context(nc.sbuf_tensor(f"w{layer}_stage_second{p}", [P, 2 * C], F32)) for p in range(2)]
        sem = lambda n: phase_semaphore(nc, g, f"w{layer}_{n}")
        self.landed = [sem(f"landed{p}") for p in range(2)]
        self.high_done, self.low_done = sem("high_done"), sem("low_done")
        if layer == 0:
            self.second = [[(0, P, 0, 0)], [(P, P, 1, 0), (2 * P, F0 - 2 * P, 2, 1)]]
        else:
            self.second = [[(0, P, 0, 0), (P, P, 1, 1)], [(2 * P, P, 2, 0), (3 * P, P, 3, 1)]]

    def pieces(self, j, q):
        expert = j - q
        yield self.stage1[q][:, :], P, self.F, self.high1, self.low1, q * self.EW * self.F + expert * (self.F // 2)
        for _, rows, chunk, place in self.second[q]:
            yield self.stage2[q][0:rows, place * C:(place + 1) * C], rows, C, self.high2, self.low2, chunk * self.EW * C + expert * (C // 2)

    def load(self, sp, j, q):
        sp.wait_ge(self.low_done, count(j - 1))
        inner = F0 if self.layer == 0 else F1
        sp.dma_start(self.stage1[q][:], self.first_rows[ds(j * P, P), :]).then_inc(self.landed[q], 16)
        for row, rows, _, place in self.second[q]:
            sp.dma_start(self.stage2[q][0:rows, place * C:(place + 1) * C],
                         self.second_rows[ds((j - q) * (inner // 2) + row, rows), :]).then_inc(self.landed[q], 16)

    def high(self, act, j, q):
        loads = 1 + len(self.second[q])
        act.wait_ge(self.landed[q], (j - q) * (8 * loads) + 16 * loads)
        act.sem_inc(self.g["carried_a"], 1)
        for stage, rows, width, high, _, at in self.pieces(j, q):
            ins = act.activation(high[0:rows, ds(at, width)], stage, ACT.Copy, scale=WSCALE)
        ins.then_inc(self.high_done, 1)

    def low(self, v, j, q):
        v.wait_ge(self.high_done, j + 1)
        for stage, rows, width, high, low, at in self.pieces(j, q):
            ins = v.scalar_tensor_tensor(low[0:rows, ds(at, width)], stage, WSCALE, high[0:rows, ds(at, width)], ALU.mult, ALU.subtract)
        ins.then_inc(self.low_done, 1)


def count(value):
    return max(value, 0) if isinstance(value, int) else value


def within(i, n):
    return not isinstance(i, int) or 0 <= i < n


def over_batches(eng, first, step, last=B - 3, peeled=4):
    for n in range(first, peeled):
        step(n, n % 2)
    end = peeled + (last + 1 - peeled) // 2 * 2
    with eng.Fori(peeled, end - 1, 2) as n:
        step(n, 0)
        step(n + 1, 1)
    for n in range(end, B + 2):
        step(n, n % 2)


class Route:

    def __init__(self, nc, g, c, tag, K, SL, PR, RUN, rows, wg):
        self.nc, self.g, self.K, self.SL, self.PR, self.RUN, self.rows, self.wg = nc, g, K, SL, PR, RUN, rows, wg
        sb = lambda n, s, d=F32: c.enter_context(nc.sbuf_tensor(f"{tag}_{n}", s, d))
        sem = lambda n: phase_semaphore(nc, g, f"{tag}_{n}")
        self.mv = sb("mean_var", [P, T, 2])
        self.st = sb("stats", [P, T, 6])
        self.rstd = sb("rstd", [P, T])
        self.L = sb("logits", [P, T, E])
        self.work = sb("logits_rest", [P, T, E])
        self.eq = sb("equal", [P, T, E])
        self.m = [sb(f"max{k}", [P, T]) for k in range(2)]
        self.best = sb("best", [P, T])
        self.oh = [sb(f"onehot{k}", [P, T, E]) for k in range(K)]
        self.A = sb("assigned", [P, T, E], F16)
        self.d = sb("shifted", [P, T, E + 1])
        self.ex = sb("exps", [P, T, E + 1])
        self.sum = sb("expsum", [P, T])
        self.pos = sb("position", [P, T, E])
        self.slf = sb("slot_f", [P, T, K])
        self.idx = [sb(f"slot_idx{p}", [P, K, T], I32) for p in range(2)]
        self.z = [sb(f"z_tokens{p}", [P, T, rows.shape[1]]) for p in range(2)]
        self.zT = sb("z_cols", [P, KC, S])
        self.stats_ready = sem("stats_ready")
        self.rstd_ready = sem("rstd_ready")
        self.z_ready = sem("z_ready")
        self.z_turned = sem("z_turned")
        if K == 1:
            self.number = sb("token_numbers", [P, T])
            self.tokens_copied = sem("tokens_copied")
        self.cols_ready = sem("cols_ready")
        self.logits_ready = sem("logits_ready")
        self.shifted_ready = sem("shifted_ready")
        self.exp_ready = sem("exp_ready")
        self.assigned_ready = sem("assigned_ready")
        self.prefix_ready = sem("prefix_ready")
        self.idx_ready = sem("idx_ready")
        self.scattered = [sem(f"scattered{p}") for p in range(2)]
        self.stored = [sem(f"stored{p}") for p in range(2)]
        self.step = sem("route_step")
        self.stat_step = sem("route_stat_step")
        self.pool_step = sem("route_pool_step")
        self.steps = 27 if K == 2 else 19
        self.chosen_steps = 15 if K == 2 else 9

    def pool_rstd(self, pool, n):
        ch = Chain(pool, self.pool_step, n * 2)
        pool.wait_ge(self.stats_ready, n + 1)
        ch.link(pool.tensor_tensor(self.rstd[:], self.mv[:, :, 1], self.g["epst"][:, 0:T], ALU.add))
        ch.mark(pool.tensor_tensor(self.rstd[:], self.rstd[:], self.g["mhalf"][:, 0:T], ALU.pow))
        ch.wait()
        pool.sem_inc(self.rstd_ready, 1)

    def vector_stats(self, v, n, x):
        ch = Chain(v, self.stat_step, n * T)
        v.sem_inc(self.g["carried_v"], 1)
        for t in range(T):
            ch.mark(v.bn_stats(self.st[:, t, :], x[:, t, :]))
        ch.wait()
        v.sem_inc(self.g["carried_v"], 1)
        for t in range(T):
            ins = v.bn_aggr(self.mv[:, t, :], self.st[:, t, :])
        ins.then_inc(self.stats_ready, 1)

    def vector_z(self, v, n, p, x, shared):
        v.wait_ge(self.rstd_ready, n + 1)
        v.wait_ge(self.scattered[p], count((n - p) * (8 * self.K * T)))
        if shared:
            v.wait_ge(self.stored[p], count((n - p) * 8))
        for t in range(T):
            ins = v.tensor_scalar(self.z[p][:, t, 0:C], x[:, t, :], self.mv[:, t, 0:1], self.rstd[:, t:t + 1], ALU.subtract, ALU.mult)
        ins.then_inc(self.z_ready, 1)

    def pe_turn(self, pe, n, p, bank):
        pe.wait_ge(self.z_ready, n + 1)
        for k in range(KC):
            for t in range(T):
                ins = pe.transpose(bank[:, k, t * P:(t + 1) * P], self.z[p][:, t, k * P:(k + 1) * P], self.g["ident"][:])
        ins.then_inc(self.z_turned, 1)

    def act_cols(self, act, n, bank):
        act.wait_ge(self.logits_ready, count(n))
        act.wait_ge(self.z_turned, n + 1)
        act.activation(self.zT[:], bank, ACT.Copy).then_inc(self.cols_ready, 1)

    def pe_logits(self, pe, n, bank):
        pe.wait_ge(self.cols_ready, n + 1)
        for t in range(T):
            for k in range(KC):
                ins = pe.matmul(bank[:, t, :], self.zT[:, k, t * P:(t + 1) * P], self.wg[:, k, :], start=k == 0, stop=k == KC - 1)
        ins.then_inc(self.logits_ready, 1)

    def pe_prefix(self, pe, n, bank):
        pe.wait_ge(self.assigned_ready, n + 1)
        g = self.g
        pe.matmul(bank[:, 0, :], g["triu"][:], self.A[:, 0, :], start=True, stop=True)
        pe.matmul(bank[:, 1, :], g["triu"][:], self.A[:, 1, :], start=True, stop=False)
        pe.matmul(bank[:, 1, :], g["ones"][:], self.A[:, 0, :], start=False, stop=True)
        pe.matmul(bank[:, 2, :], g["ones"][:], self.A[:, 0, :], start=True, stop=False)
        pe.matmul(bank[:, 2, :], g["ones"][:], self.A[:, 1, :], start=False, stop=True).then_inc(self.prefix_ready, 1)

    def act_exp(self, act, n):
        act.wait_ge(self.shifted_ready, n + 1)
        act.activation(self.ex[:], self.d[:], ACT.Exp).then_inc(self.exp_ready, 1)

    def vector_choose(self, v, n, p, logits, beside=None):
        ch = Chain(v, self.step, n * self.steps)
        bc = lambda x: x.unsqueeze(2).to_broadcast([P, T, E])

        def link(ins):
            ch.mark(ins)
            if beside:
                beside(ch.n - 1)
            ch.wait()
        v.wait_ge(self.logits_ready, n + 1)
        link(v.tensor_copy(self.L[:], logits))
        src = self.L
        for k in range(self.K):
            link(v.tensor_reduce(self.m[k][:], src[:], AX.X, ALU.max))
            link(v.tensor_tensor(self.eq[:], src[:], bc(self.m[k][:]), ALU.is_equal))
            link(v.tensor_tensor(self.eq[:], self.eq[:], self.g["reviota"][:], ALU.mult))
            link(v.tensor_reduce(self.best[:], self.eq[:], AX.X, ALU.max))
            link(v.tensor_tensor(self.oh[k][:], self.eq[:], bc(self.best[:]), ALU.is_equal))
            if k == 0 and self.K == 2:
                link(v.scalar_tensor_tensor(self.work[:], self.oh[0][:], -BIG, self.L[:], ALU.mult, ALU.add))
                src = self.work
        if self.K == 2:
            ch.link(v.tensor_tensor(self.A[:], self.oh[0][:], self.oh[1][:], ALU.add))
        else:
            link(v.tensor_copy(self.A[:], self.oh[0][:]))
        v.sem_inc(self.assigned_ready, 1)
        ch.mark(v.tensor_tensor(self.d[:, :, 0:E], self.L[:], bc(self.m[0][:]), ALU.subtract))
        ch.mark(v.tensor_tensor(self.d[:, :, E], self.m[self.K - 1][:], self.m[0][:], ALU.subtract))
        ch.wait()
        v.sem_inc(self.shifted_ready, 1)
        assert ch.n == self.chosen_steps, ch.n

    def vector_slots(self, v, n, p, prefix):
        ch = Chain(v, self.step, n * self.steps)
        ch.n = self.chosen_steps
        v.wait_ge(self.exp_ready, n + 1)
        ch.link(v.tensor_reduce(self.sum[:], self.ex[:, :, 0:E], AX.X, ALU.add))
        ch.link(v.reciprocal(self.sum[:], self.sum[:]))
        if self.K == 1:
            ch.mark(v.tensor_scalar(self.z[p][:, :, SCALE], self.sum[:], self.g["gate"][:, 3:4], None, ALU.mult))
            ch.mark(v.tensor_copy(self.z[p][:, :, NUMBER], self.number[:]))
            ch.mark(v.tensor_scalar(self.number[:], self.number[:], float(S), None, ALU.add))
        else:
            ch.mark(v.tensor_copy(self.PR[:, ds(n * T, T), 0], self.sum[:]))
            ch.mark(v.tensor_tensor(self.PR[:, ds(n * T, T), 1], self.sum[:], self.ex[:, :, E], ALU.mult))
        v.wait_ge(self.prefix_ready, n + 1)
        ch.link(v.tensor_tensor(self.pos[:], prefix[:, 0:T, :], self.RUN[:].unsqueeze(1).to_broadcast([P, T, E]), ALU.add))
        ch.mark(v.tensor_tensor(self.RUN[:], self.RUN[:], prefix[:, T, :], ALU.add))
        for k in range(self.K):
            ch.link(v.tensor_tensor(self.eq[:], self.oh[k][:], self.pos[:], ALU.mult))
            ch.link(v.tensor_reduce(self.slf[:, :, k], self.eq[:], AX.X, ALU.add))
        if self.K == 2:
            ch.mark(v.tensor_copy(self.SL[:, ds(n * T, T), :], self.slf[:]))
        ch.link(v.tensor_copy(self.idx[p][:].rearrange("p k t -> p t k"), self.slf[:]))
        v.sem_inc(self.idx_ready, 1)
        assert ch.n == self.steps, ch.n

    def act_tokens(self, act, n, p):
        act.wait_ge(self.scattered[p], count((n - p) * (8 * T)))
        act.wait_ge(self.stats_ready, n + 1)
        act.sem_inc(self.g["carried_a"], 1)
        act.activation(self.z[p][:, :, TOKEN:TOKEN + C], self.g["XR"][:, ds(n * T, T), :], ACT.Copy).then_inc(self.tokens_copied, 1)

    def pool_scatter(self, pool, n, p):
        if self.K == 1:
            pool.wait_ge(self.tokens_copied, n + 1)
        pool.wait_ge(self.idx_ready, n + 1)
        pool.sem_inc(self.g["carried"], 1)
        for k in range(self.K):
            for t in range(T):
                pool.indirect_dma_start(self.rows, bass.IndirectOffsetOnAxis(ap=self.idx[p][:, k, t:t + 1], axis=0),
                                        self.z[p][:, t, :], None).then_inc(self.scattered[p], 16)

    def finish(self, eng, shared):
        for p in range(2):
            eng.wait_ge(self.scattered[p], (B // 2) * self.K * T * 16)
            if shared:
                eng.wait_ge(self.stored[p], (B // 2) * 16)


class Table:

    def __init__(self, nc, g, c, layer, space):
        self.g, self.layer = g, layer
        self.RUN, self.routed, self.dummy, self.rows = ((g["RUN0"], ROUTED0, DUMMY0, g["z0"]), (g["RUN1"], ROUTED1, DUMMY1, g["z1"]))[layer]
        self.tiles = tiles = TILES0 if layer == 0 else ROUTED1
        self.E1 = E1 = E + 1
        sem = lambda n: phase_semaphore(nc, g, f"t{layer}_{n}")
        left = [(x, 0) for x in space]

        def take(*shape, dt=F32):
            size = int(np.prod(shape))
            z = next(z for z, (x, at) in enumerate(left) if at + size <= x.shape[1])
            x, at = left[z]
            left[z] = (x, at + size)
            x = x[:, at:at + size] if dt == F32 else x[:, at:at + size].bitcast(dt)
            return x.rearrange("p (a b) -> p a b", b=shape[-1]) if len(shape) == 2 else x
        self.after, self.part, self.more = take(self.routed, E1), take(self.routed, E1), take(E, NT)
        self.tiota, self.tf, self.jiota, self.jf = take(tiles, dt=I32), take(tiles), take(NT, dt=I32), take(NT)
        self.cnt, self.nt, self.before, self.base, self.steps = take(E), take(E), take(E1), take(E1), take(E1)
        self.row, self.ex, self.runi = take(tiles), take(tiles), take(E, dt=I32)
        self.iotas, self.numbered, self.step, self.run_ready, self.padded = (sem(x) for x in ("iotas", "numbered", "step", "run_ready", "padded"))

    def pool_iotas(self, pool):
        pool.iota(self.jiota, pattern=[[P, NT]], base=0, channel_multiplier=0).then_inc(self.iotas, 1)
        pool.iota(self.tiota, pattern=[[1, self.tiles]], base=0, channel_multiplier=0).then_inc(self.iotas, 1)

    def vector_numbers(self, v):
        v.wait_ge(self.iotas, 2)
        v.tensor_copy(self.jf, self.jiota).then_inc(self.numbered, 1)
        v.tensor_copy(self.tf, self.tiota).then_inc(self.numbered, 1)
        v.memset(self.before[:, 0:1], 0.0).then_inc(self.numbered, 1)
        v.tensor_copy(self.base[:, 0:E], self.g["regbase"][:]).then_inc(self.numbered, 1)
        v.memset(self.base[:, E:self.E1], float(self.dummy)).then_inc(self.numbered, 1)

    def vector_table(self, v):
        RUN, g, tiles, routed, E1, dummy = self.RUN, self.g, self.tiles, self.routed, self.E1, self.dummy
        tf, jf, cnt, more, nt, before, base, steps = self.tf, self.jf, self.cnt, self.more, self.nt, self.before, self.base, self.steps
        after, part, row, ex = self.after, self.part, self.row, self.ex
        ch = Chain(v, self.step)
        tt = v.tensor_tensor
        ch.link(v.tensor_copy(self.runi, RUN[:]))
        v.sem_inc(self.run_ready, 1)
        ch.link(tt(cnt[:], RUN[:], g["regbase"][:], ALU.subtract))
        v.wait_ge(self.numbered, 5)
        ch.link(tt(more[:], cnt[:].unsqueeze(2).to_broadcast([P, E, NT]), jf[:].unsqueeze(1).to_broadcast([P, E, NT]), ALU.is_gt))
        ch.link(v.tensor_reduce(nt[:], more[:], AX.X, ALU.add))
        for e in range(E):
            ch.link(tt(before[:, e + 1:e + 2], before[:, e:e + 1], nt[:, e:e + 1], ALU.add))
        ch.link(v.scalar_tensor_tensor(base[:], before[:], -float(P), base[:], ALU.mult, ALU.add))
        ch.mark(v.tensor_copy(steps[:, 0:1], base[:, 0:1]))
        ch.mark(tt(steps[:, 1:E1], base[:, 1:E1], base[:, 0:E], ALU.subtract))
        full = [P, routed, E1]
        ch.link(tt(after[:], tf[:, 0:routed].unsqueeze(2).to_broadcast(full), before[:].unsqueeze(1).to_broadcast(full), ALU.is_ge))
        ch.mark(tt(part[:], after[:], steps[:].unsqueeze(1).to_broadcast(full), ALU.mult))
        ch.link(v.tensor_reduce(ex[:, 0:routed], after[:, :, 1:E], AX.X, ALU.add))
        ch.link(v.tensor_reduce(row[:, 0:routed], part[:], AX.X, ALU.add))
        ch.mark(v.scalar_tensor_tensor(row[:, 0:routed], tf[:, 0:routed], float(P), row[:, 0:routed], ALU.mult, ALU.add))
        if self.layer == 0:
            ch.mark(v.tensor_scalar(row[:, routed:tiles], tf[:, routed:tiles], float(P), float(SHARED - P * routed), ALU.mult, ALU.add))
            ch.mark(v.memset(ex[:, routed:tiles], float(E)))
            ch.mark(v.tensor_copy(g["base_steps"][:], steps[:, 0:E]))
        ch.wait()
        ch.mark(v.tensor_copy(g["tabrow"][:, 0:tiles], row[0:1, :]))
        ch.link(v.tensor_copy(g["tabexp"][:, 0:tiles], ex[0:1, :]))

    def pad(self, eng, experts):
        eng.wait_ge(self.run_ready, 1)
        for e in experts:
            r = eng.value_load(self.runi[0:1, e:e + 1], min_val=e * REG, max_val=e * REG + NTOK)
            eng.dma_start(self.rows[ds(r, P), :], self.g["padding"][:, 0:self.rows.shape[1]]).then_inc(self.padded, 16)

    def finish(self, eng):
        eng.wait_ge(self.padded, 16 * E)


def phase_attn0(nc, a, g):
    NS1 = DC - P
    with ExitStack() as c:
        sb = lambda n, s, d=F32: c.enter_context(nc.sbuf_tensor(f"a0_{n}", s, d))
        pb = lambda n: c.enter_context(nc.psum_tensor(f"a0_{n}", [P, 512], F32))
        sem = lambda n: phase_semaphore(nc, g, f"a0_{n}")
        halves = lambda n, shape: [sb(f"{n}_{x}", shape, F16) for x in ("high", "low")]
        wqs, wos, wls, wcs = halves("wq", [P, KC, C]), halves("wo", [P, KC, C]), halves("wlkv", [P, KC, 2 * C]), halves("wkv", [P, 2, 2 * C])
        PASSES = ((0, 0), (0, 1), (1, 0))
        wg = sb("wg", [P, KC, E])
        cols = sb("columns", [P, 10])
        lng, lnb, cng, cnb, gqk, knraw = (cols[:, i:i + w] for i, w in ((0, 2), (2, 2), (4, 2), (6, 2), (8, 1), (9, 1)))
        gains, gmax, gneg = sb("gain_rows", [P, 2, D]), sb("gain_bound", [P, 1]), sb("gain_products", [P, D])
        masku, maskf, bias = sb("mask_bytes", [P, B * T], U8), sb("mask_bias", [P, B, T]), sb("latent_bias", [P, 1])
        bo = sb("bo", [P, C])
        cin = [sb(f"ctx_in{p}", [P, T, DC]) for p in range(2)]
        st, mv, r1, r2 = sb("stats", [P, 4, 6]), sb("mean_var", [P, 4, 2]), sb("rstd", [P, 4]), sb("rstd2", [P, 2])
        xn, cn = sb("x_norm", [P, T, C]), sb("ctx_norm", [P, T, DC])
        lT, cT = sb("lat_cols", [P, KC, S]), sb("ctx_cols", [P, 2, S])
        lTs, cTs = halves("lat_cols", [P, KC, S]), halves("ctx_cols", [P, 2, S])
        qs, sq = sb("q_tokens", [P, T * H, D]), sb("q_squares", [P, T * H, D])
        qn = sb("q_norm", [P, T, C])
        ksq = sb("k_squares", [P, 2, 512])
        ss = sb("square_sums", [P, 24])
        rq = sb("q_scales", [P, 8])
        rr = [sb(f"k_scales{p}", [P, 16]) for p in range(2)]
        qTs = [halves(f"q_cols{p}", [P, 2, S]) for p in range(2)]
        kT = sb("k_cols", [P, 2, 2 * S])
        kTs = [halves(f"k_cols{p}", [P, 2, 2 * S]) for p in range(2)]
        va = [sb(f"v_ones{p}", [P, 4, H, D + 1]) for p in range(2)]
        pm = [sb(f"probs{i}", [P, 4, S]) for i in range(2)]
        rs = sb("o_rsum", [P, T, H])
        on = sb("o_norm", [P, T, C])
        onTs = halves("o_cols", [P, KC, S])
        gate64 = sb("gate_over_64", [P, 1])
        xo = sb("x_mid", [P, T, C])
        wq, wo = qn[:].rearrange("p t c -> p (t c)").rearrange("p (k c) -> p k c", k=KC), on[:].rearrange("p t c -> p (t c)").rearrange("p (k c) -> p k c", k=KC)
        wl, wc = (x[:].rearrange("p j s -> p (j s)").rearrange("p (k c) -> p k c", k=KC) for x in pm)
        RB = [pb("front0"), pb("front1")]
        TA, TB = pb("tail_cols"), pb("tail_rows")
        SC = [pb("scores0"), pb("scores1")]
        O = [pb("out0"), pb("out1")]
        rt = Route(nc, g, c, "r0", 2, g["SL0"], g["PR0"], g["RUN0"], g["z0"], wg)
        weights, table, dummies_padded = Weights(nc, g, a, c, 0), Table(nc, g, c, 0, [x[:].rearrange("p j s -> p (j s)") for x in (pm[0], pm[1], ksq)]), sem("dummies_padded")

        consts_in, consts_ready, const_step = sem("consts_in"), sem("consts_ready"), sem("const_step")
        landed = [sem(f"landed{p}") for p in range(2)]
        s1_stats, s1_rstd, s1_norm, s1_turned, s1_cols = (sem(f"s1_{x}") for x in ("stats", "rstd", "norm", "turned", "cols"))
        proj_ready, freed_act, freed_dve = sem("proj_ready"), sem("proj_freed_act"), sem("proj_freed_dve")
        s1_ksq, s1_ssq, s1_ssk, s1_ss, s1_rq, s1_rr = (sem(f"s1_{x}") for x in ("ksq", "ssq", "ssk", "ss", "rq", "rr"))
        KSUM = TA[:, 0:16]
        s1_qn, s1_qturned, s1_qT = (sem(f"s1_{x}") for x in ("qn", "qturned", "qT"))
        scores, exps, pv = sem("scores"), sem("exps"), sem("pv")
        s2_on, s2_turned, s2_cols, s2_wo = (sem(f"s2_{x}") for x in ("on", "turned", "cols", "wo"))
        w_high, w_low, s1_high, s1_low, k_low, q_low, o_low = (sem(x) for x in ("w_high", "w_low", "s1_high", "s1_low", "k_low", "q_low", "o_low"))
        split = [(wq[:], [x[:] for x in wqs]), (wc[:, 0, :], [x[:, 0, :] for x in wcs]), (wc[0:NS1, 1, :], [x[0:NS1, 1, :] for x in wcs]),
                 (wl[:], [x[:] for x in wls]), (wo[:], [x[:] for x in wos])]
        d0, d1, d2, p1 = sem("dve_step0"), sem("dve_step1"), sem("dve_step2"), sem("pool_step1")
        D0, D1, D2, P1 = 4, 4, 4, 7

        loads = [(cols[:], a["cols0"]), (wq[:], a["wq0"].rearrange("(k p) f -> p k f", p=P)), (wo[:], a["wo0"].rearrange("(k p) f -> p k f", p=P)),
                 (wl[:], a["wlkv0"].rearrange("(k p) f -> p k f", p=P)),
                 (wc[:, 0, :], a["wkv0"][0:P]), (wc[0:NS1, 1, :], a["wkv0"][P:DC]),
                 (wg[:], a["wg0"].rearrange("(k p) e -> p k e", p=P)),
                 (bo[:], a["bo0"].rearrange("(o n) -> o n", o=1).to_broadcast([P, C])),
                 (gains[:].rearrange("p k d -> p (k d)"), a["gains"].rearrange("(o n) -> o n", o=1).to_broadcast([P, 2 * D])),
                 (masku[:], a["mask"])]
        n_consts = 16 * len(loads)

        with nc.Block() as block:
            @block.sync
            def _(sp):
                def load(m, p):
                    sp.wait_ge(landed[p], count((m - p) * 16))
                    sp.dma_start(g["XR"][:, ds(m * T, T), :], a["x"][ds(m * S, S), :].rearrange("(t p) c -> p t c", p=P)).then_inc(landed[p], 16)
                    sp.wait_ge(s1_norm, count(m - 1))
                    sp.dma_start(cin[p][:], a["ctx"][ds(m * S, S), :].rearrange("(t p) c -> p t c", p=P)).then_inc(landed[p], 16)

                def store(m, p):
                    sp.wait_ge(rt.z_ready, m + 1)
                    sp.dma_start(g["z0"][ds(m * S + SHARED, S), :].rearrange("(t p) c -> p t c", p=P), rt.z[p][:]).then_inc(rt.stored[p], 16)

                def step(n, q):
                    if within(n + 3, B):
                        load(n + 3, 1 - q)
                    if isinstance(n, int) and n == 2:
                        pad_dummies(sp, g, g["z0"], DUMMY0, dummies_padded)
                    if isinstance(n, int) and n == -3:
                        for dst, src in loads:
                            sp.dma_start(dst, src).then_inc(consts_in, 16)
                    if within(n - 1, B):
                        store(n - 1, 1 - q)
                    if within(n + 3, weights.parts):
                        weights.load(sp, n + 3, 1 - q)
                over_batches(sp, -3, step, B - 4)
                table.pad(sp, range(0, E, 2))
                table.finish(sp)
                rt.finish(sp, True)
                sp.wait_ge(dummies_padded, 16 * E)

            @block.gpsimd
            def _(pool):
                def rstd(m):
                    ch = Chain(pool, p1, m * P1)
                    pool.wait_ge(s1_stats, m + 1)
                    ch.link(pool.tensor_tensor(r1[:], mv[:, :, 1], g["epst"][:], ALU.add))
                    ch.link(pool.tensor_tensor(r1[:], r1[:], g["mhalf"][:, 0:4], ALU.pow))
                    ch.link(pool.tensor_tensor(r2[:], mv[:, 0:T, 1], r1[:, 0:T], ALU.mult))
                    ch.link(pool.tensor_tensor(r2[:], r2[:], r1[:, 0:T], ALU.mult))
                    ch.link(pool.tensor_tensor(r2[:], r2[:], g["epst"][:, 0:T], ALU.add))
                    ch.link(pool.tensor_tensor(r2[:], r2[:], g["mhalf"][:, 0:T], ALU.pow))
                    ch.link(pool.tensor_tensor(r1[:, 0:T], r1[:, 0:T], r2[:], ALU.mult))
                    pool.sem_inc(s1_rstd, 1)
                    assert ch.n == P1, ch.n

                def squares(m, p):
                    pool.wait_ge(s1_ssk, count(m))
                    for i in range(2):
                        pool.wait_ge(freed_act, 3 * m + 2 + i)
                        ins = pool.tensor_tensor(ksq[:, i, :], kT[:, i, :], kT[:, i, :], ALU.mult)
                    ins.then_inc(s1_ksq, 1)

                def q_scales(m):
                    pool.wait_ge(s1_qn, count(m))
                    pool.wait_ge(s1_ssq, m + 1)
                    pool.tensor_tensor(rq[:], ss[:, 0:8], g["mhalf"][:, 0:8], ALU.pow).then_inc(s1_rq, 1)

                def k_scales(m, p):
                    pool.wait_ge(exps, count(16 * (m - 1)))
                    pool.wait_ge(s1_ss, m + 1)
                    pool.tensor_tensor(rr[p][:], ss[:, 8:24], g["mhalf"][:, 0:16], ALU.pow).then_inc(s1_rr, 1)

                def step(n, q):
                    if within(n + 2, B):
                        rstd(n + 2)
                    if within(n - 1, B):
                        rt.pool_rstd(pool, n - 1)
                    if within(n + 1, B):
                        squares(n + 1, 1 - q)
                        q_scales(n + 1)
                        k_scales(n + 1, 1 - q)
                    if isinstance(n, int) and n == B + 1:
                        pool.wait_ge(pv, 4 * B)
                        table.pool_iotas(pool)
                    if within(n - 2, B):
                        rt.pool_scatter(pool, n - 2, q)
                over_batches(pool, -2, step)

            @block.scalar
            def _(act):
                act.wait_ge(consts_in, n_consts)
                for w, halved in split:
                    act.activation(halved[0], w, ACT.Copy, scale=WSCALE).then_inc(w_high, 1)

                def front_cols(m):
                    act.wait_ge(s1_ssk, count(m))
                    act.wait_ge(s1_turned, 2 * m + 1)
                    for k in range(KC):
                        ins = act.activation(lT[:, k, :], RB[0][:, k * S:(k + 1) * S], ACT.Identity, bias=lnb[:, k:k + 1], scale=lng[:, k:k + 1])
                    ins.then_inc(s1_cols, 1)
                    act.wait_ge(s1_turned, 2 * m + 2)
                    for k, (o, w) in enumerate(CTX_CHUNKS):
                        ins = act.activation(cT[0:w, k, :], RB[1][0:w, k * S:(k + 1) * S], ACT.Identity, bias=cnb[0:w, k:k + 1], scale=cng[0:w, k:k + 1])
                    ins.then_inc(s1_cols, 1)
                    act.wait_ge(s1_cols, 2 * m + 2)
                    act.activation(lTs[0][:], lT[:], ACT.Copy).then_inc(s1_high, 1)
                    for k, (o, w) in enumerate(CTX_CHUNKS):
                        ins = act.activation(cTs[0][0:w, k, :], cT[0:w, k, :], ACT.Copy)
                    ins.then_inc(s1_high, 1)

                def front_qk(m, p):
                    act.wait_ge(s1_qn, count(m))
                    act.wait_ge(proj_ready, 4 * m + 1)
                    act.activation(qs[:].rearrange("p h d -> p (h d)"), RB[0][:], ACT.Copy, scale=1.0 / WSCALE).then_inc(freed_act, 1)
                    act.wait_ge(s1_ksq, count(m))
                    act.wait_ge(scores, count(8 * (m - 1)))
                    for i in range(2):
                        act.wait_ge(proj_ready, 4 * m + 2 + i)
                        act.activation(kT[:, i, :], RB[1 - i][:], ACT.Copy, scale=1.0 / WSCALE)
                        act.activation(kTs[p][0][:, i, :], RB[1 - i][:], ACT.Copy, scale=1.0 / WSCALE).then_inc(freed_act, 1)

                def front_q(m, p):
                    act.wait_ge(s1_qturned, m + 1)
                    act.activation(qTs[p][0][:].rearrange("p k s -> p (k s)"), RB[1][:], ACT.Copy, scale=gqk[:, 0:1]).then_inc(s1_qT, 1)

                def head(m, p, h):
                    for jp in range(2):
                        if jp == 0:
                            act.wait_ge(pv, count(4 * m + h - 1) if h else count(4 * m))
                        act.wait_ge(scores, 8 * m + 2 * h + jp + 1)
                        if h == 0 and jp == 0:
                            act.wait_ge(s1_rr, m + 1)
                        for j in range(2):
                            jt = jp + 2 * (1 - j)
                            b = maskf[:, ds(m, 1), jt] if jt < 2 else bias[:, 0:1]
                            act.activation(pm[h % 2][:, jt, :], SC[jp][:, j * S:(j + 1) * S], ACT.Exp, bias=b,
                                           scale=rr[p][:, jt * 4 + h:jt * 4 + h + 1]).then_inc(exps, 1)

                def tail_cols(m):
                    act.wait_ge(s2_wo, count(m))
                    act.wait_ge(s2_turned, m + 1)
                    act.activation(onTs[0][:].rearrange("p k s -> p (k s)"), TA[:], ACT.Copy).then_inc(s2_cols, 1)

                def step(n, q):
                    core, front, tail = within(n, B), within(n + 1, B), within(n - 1, B)
                    if core:
                        head(n, q, 0)
                    if tail:
                        tail_cols(n - 1)
                    if front:
                        front_cols(n + 1)
                    if core:
                        head(n, q, 1)
                    if within(n + 1, weights.parts):
                        weights.high(act, n + 1, 1 - q)
                    if front:
                        front_qk(n + 1, 1 - q)
                    if core:
                        head(n, q, 2)
                    if tail:
                        rt.act_cols(act, n - 1, TA[:].rearrange("p (k s) -> p k s", k=KC))
                    if core:
                        head(n, q, 3)
                    if tail:
                        rt.act_exp(act, n - 1)
                    if isinstance(n, int) and n == -1:
                        act.wait_ge(consts_ready, 1)
                    if front:
                        front_q(n + 1, 1 - q)
                over_batches(act, -1, step)
                table.pad(act, range(1, E, 2))

            @block.vector
            def _(v):
                def split_weights():
                    for i, (w, halved) in enumerate(split):
                        v.wait_ge(w_high, i + 1)
                        v.scalar_tensor_tensor(halved[1], w, WSCALE, halved[0], ALU.mult, ALU.subtract).then_inc(w_low, 1)

                def constants():
                    v.wait_ge(consts_in, n_consts)
                    ch = Chain(v, const_step)
                    ch.link(v.tensor_scalar(gate64[:], g["gate"][:, 0:1], 1.0 / WSCALE, None, ALU.mult))
                    ch.link(v.scalar_tensor_tensor(gqk[:], gqk[:], D ** -0.5, knraw[:], ALU.mult, ALU.mult))
                    ch.link(v.tensor_tensor(gneg[:], gains[:, 0, :], gains[:, 1, :], ALU.mult))
                    ch.link(v.tensor_reduce(gmax[:], gneg[:], AX.X, ALU.max, apply_absolute_value=True))
                    ch.link(v.tensor_scalar(bias[:], gmax[:], -(D ** 0.5), None, ALU.mult))
                    ch.link(v.tensor_copy(maskf[:].rearrange("p b t -> p (b t)"), masku[:]))
                    ch.link(v.tensor_scalar(maskf[:], maskf[:], BIG, -BIG, ALU.mult, ALU.add))
                    ch.link(v.tensor_scalar(maskf[:], maskf[:], bias[:, 0:1], None, ALU.add))
                    ch.link(v.tensor_scalar(bo[:], bo[:], g["gate"][:, 0:1], None, ALU.mult))
                    for p in range(2):
                        ch.mark(v.memset(va[p][:, :, :, D:D + 1], 1.0))
                    ch.wait()
                    v.sem_inc(consts_ready, 3)

                chains = {}

                def pre_stats(m, p):
                    ch = chains["front"] = Chain(v, d0, m * D0)
                    v.wait_ge(landed[p], (m - p) * 16 + 32)
                    x = XRTile(g["XR"], m)
                    for t in range(T):
                        ch.mark(v.bn_stats(st[:, 2 + t, :], cin[p][:, t, :]))
                        ch.mark(v.bn_stats(st[:, t, :], x[:, t, :]))
                    ch.wait()
                    v.sem_inc(g["carried_v"], 1)
                    for t in range(4):
                        ins = v.bn_aggr(mv[:, t, :], st[:, t, :])
                    ins.then_inc(s1_stats, 1)

                def pre_norm(m, p):
                    v.wait_ge(s1_turned, count(2 * m))
                    v.wait_ge(s1_rstd, m + 1)
                    x = XRTile(g["XR"], m)
                    for t in range(T):
                        v.tensor_scalar(xn[:, t, :], x[:, t, :], mv[:, t, 0:1], r1[:, t:t + 1], ALU.subtract, ALU.mult)
                        ins = v.tensor_scalar(cn[:, t, :], cin[p][:, t, :], mv[:, 2 + t, 0:1], r1[:, 2 + t:3 + t], ALU.subtract, ALU.mult)
                    ins.then_inc(s1_norm, 1)

                def front_low(m):
                    v.wait_ge(s1_high, 2 * m + 1)
                    v.tensor_tensor(lTs[1][:], lT[:], lTs[0][:], ALU.subtract).then_inc(s1_low, 1)
                    v.wait_ge(s1_high, 2 * m + 2)
                    for k, (o, w) in enumerate(CTX_CHUNKS):
                        ins = v.tensor_tensor(cTs[1][0:w, k, :], cT[0:w, k, :], cTs[0][0:w, k, :], ALU.subtract)
                    ins.then_inc(s1_low, 1)

                def front_k_low(m, p):
                    for i in range(2):
                        v.wait_ge(freed_act, 3 * m + 2 + i)
                        v.tensor_tensor(kTs[p][1][:, i, :], kT[:, i, :], kTs[p][0][:, i, :], ALU.subtract).then_inc(k_low, 1)

                def front_q_low(m, p):
                    v.wait_ge(s1_qT, m + 1)
                    v.scalar_tensor_tensor(qTs[p][1][:].rearrange("p k s -> p (k s)"), RB[1][:], gqk[:, 0:1],
                                           qTs[p][0][:].rearrange("p k s -> p (k s)"), ALU.mult, ALU.subtract).then_inc(q_low, 1)

                def tail_o_low(m):
                    v.wait_ge(s2_cols, m + 1)
                    v.tensor_tensor(onTs[1][:].rearrange("p k s -> p (k s)"), TA[:], onTs[0][:].rearrange("p k s -> p (k s)"), ALU.subtract).then_inc(o_low, 1)

                def front_squares(m, p):
                    ch = chains["front1"] = Chain(v, d1, m * D1)
                    v.wait_ge(freed_act, 3 * m + 1)
                    ch.link(v.tensor_tensor(sq[:], qs[:], qs[:], ALU.mult))
                    v.wait_ge(s1_rq, count(m))
                    ch.link(v.tensor_reduce(ss[:, 0:8], sq[:], AX.X, ALU.add))
                    ch.mark(v.tensor_scalar(ss[:, 0:8], ss[:, 0:8], 1.0 / D, 1e-16, ALU.mult, ALU.max))
                    ch.wait()
                    v.sem_inc(s1_ssq, 1)

                def front_v(m, p, i):
                    v.tensor_scalar(va[p][:, 2 * i:2 * i + 2, :, 0:D].rearrange("p j h d -> p (j h) d"),
                                    RB[1 - i][:].rearrange("p (x d) -> p x d", d=D), 1.0 / WSCALE, None, ALU.mult).then_inc(freed_dve, 1)

                def front_sums(m):
                    ch = chains["front1"]
                    v.wait_ge(s1_rr, count(m))
                    ch.link(v.tensor_scalar(ss[:, 8:24], KSUM, 1.0 / D, 1e-16, ALU.mult, ALU.max))
                    v.sem_inc(s1_ss, 1)
                    assert ch.n == D1, ch.n

                def front_qn(m):
                    v.wait_ge(s1_qturned, count(m))
                    v.wait_ge(s1_rq, m + 1)
                    v.tensor_tensor(qn[:].rearrange("p t (h d) -> p (t h) d", d=D), qs[:], rq[:].unsqueeze(2).to_broadcast([P, 8, D]),
                                    ALU.mult).then_inc(s1_qn, 1)

                def tail_on(m):
                    ch = chains["tail"] = Chain(v, d2, m * D2)
                    v.wait_ge(pv, 4 * m + 4)
                    ov = [O[t][:, 0:H * (D + 1)].rearrange("p (h e) -> p h e", h=H) for t in range(T)]
                    for t in range(T):
                        ch.mark(v.reciprocal(rs[:, t, :], ov[t][:, :, D]))
                    ch.wait()
                    v.wait_ge(s2_turned, count(m))
                    for t in range(T):
                        ins = v.tensor_tensor(on[:, t, :].rearrange("p (h d) -> p h d", h=H), ov[t][:, :, 0:D],
                                              rs[:, t, :].unsqueeze(2).to_broadcast([P, H, D]), ALU.mult)
                    ins.then_inc(s2_on, 1)

                def tail_x1(m):
                    ch = chains["tail"]
                    xr = g["XR"][:, ds(m * T, T), :]
                    v.wait_ge(s2_wo, m + 1)
                    ch.link(v.scalar_tensor_tensor(xo[:], TB[:].rearrange("p (t c) -> p t c", t=T), gate64[:, 0:1], xr, ALU.mult, ALU.add))
                    ch.link(v.tensor_tensor(xr, xo[:], bo[:].unsqueeze(1).to_broadcast([P, T, C]), ALU.add))
                    assert ch.n == D2, ch.n
                    rt.vector_stats(v, m, XRTile(g["XR"], m))

                def step(n, q):
                    front, tail = within(n + 1, B), within(n - 1, B)
                    m = n - 1
                    if isinstance(n, int) and n == -1:
                        split_weights()
                    if tail:
                        tail_on(m)
                    if isinstance(n, int) and n == B + 1:
                        table.vector_numbers(v)
                    if within(n - 2, B):
                        rt.vector_slots(v, n - 2, q, TB[:, 128:128 + (T + 1) * E].rearrange("p (t e) -> p t e", t=T + 1))
                    if tail:
                        tail_o_low(m)
                    if within(n + 2, B):
                        pre_stats(n + 2, q)
                    if front:
                        front_low(n + 1)
                    if isinstance(n, int) and n == -1:
                        constants()
                    if tail:
                        tail_x1(m)
                    if within(n + 2, B):
                        pre_norm(n + 2, q)
                    if tail:
                        rt.vector_z(v, m, 1 - q, XRTile(g["XR"], m), True)
                    if front:
                        front_squares(n + 1, 1 - q)
                        front_k_low(n + 1, 1 - q)
                    if within(n + 1, weights.parts):
                        weights.low(v, n + 1, 1 - q)
                    if tail:
                        rt.vector_choose(v, m, 1 - q, TB[:, 0:T * E].rearrange("p (t e) -> p t e", t=T))
                    if front:
                        v.wait_ge(pv, count(4 * n))
                        v.wait_ge(proj_ready, 4 * n + 8)
                        front_v(n + 1, 1 - q, 0)
                        front_qn(n + 1)
                        v.wait_ge(s1_ssk, n + 2)
                        front_v(n + 1, 1 - q, 1)
                        front_sums(n + 1)
                        front_q_low(n + 1, 1 - q)
                over_batches(v, -2, step)
                table.vector_table(v)

            @block.tensor
            def _(pe):
                pe.wait_ge(consts_in, n_consts)
                ident = g["ident"]

                def turn(m):
                    pe.wait_ge(s1_norm, m + 1)
                    pe.wait_ge(freed_dve, count(2 * m))
                    for k in range(KC):
                        for t in range(T):
                            ins = pe.transpose(RB[0][:, k * S + t * P:k * S + (t + 1) * P], xn[:, t, k * P:(k + 1) * P], ident[:])
                    ins.then_inc(s1_turned, 1)
                    pe.wait_ge(q_low, count(m))
                    for t in range(T):
                        for k, (o, w) in enumerate(CTX_CHUNKS):
                            ins = pe.transpose(RB[1][0:w, k * S + t * P:k * S + (t + 1) * P], cn[:, t, o:o + w], ident[:])
                    ins.then_inc(s1_turned, 1)

                def project_qk(m):
                    pe.wait_ge(s1_low, 2 * m + 1)
                    for t in range(T):
                        for k in range(KC):
                            for x, w in PASSES:
                                ins = pe.matmul(RB[0][:, t * C:(t + 1) * C], lTs[x][:, k, t * P:(t + 1) * P], wqs[w][:, k, :],
                                                start=k + x + w == 0, stop=k == KC - 1 and x == 1)
                    ins.then_inc(proj_ready, 1)
                    pe.wait_ge(s1_low, 2 * m + 2)
                    for i in range(2):
                        bank = RB[1 - i]
                        if i == 1:
                            pe.wait_ge(freed_act, 3 * m + 1)
                        for k, (o, r) in enumerate(CTX_CHUNKS):
                            for x, w in PASSES:
                                pe.matmul(bank[:, 0:S], wcs[w][0:r, k, i * P:(i + 1) * P], cTs[x][0:r, k, :], start=k + x + w == 0, stop=k == 1 and x == 1)
                        for k in range(KC):
                            for x, w in PASSES:
                                ins = pe.matmul(bank[:, S:2 * S], wls[w][:, k, i * P:(i + 1) * P], lTs[x][:, k, :],
                                                start=k + x + w == 0, stop=k == KC - 1 and x == 1)
                        ins.then_inc(proj_ready, 1)

                def project_v_ctx(m):
                    pe.wait_ge(freed_act, 3 * m + 2)
                    for t in range(T):
                        for k, (o, r) in enumerate(CTX_CHUNKS):
                            for x, w in PASSES:
                                ins = pe.matmul(RB[1][:, t * C:(t + 1) * C], cTs[x][0:r, k, t * P:(t + 1) * P], wcs[w][0:r, k, C:2 * C],
                                                start=k + x + w == 0, stop=k == 1 and x == 1)
                    ins.then_inc(proj_ready, 1)

                def project_v_lat_key_sums(m):
                    pe.wait_ge(freed_act, 3 * m + 3)
                    for t in range(T):
                        for k in range(KC):
                            for x, w in PASSES:
                                pe.matmul(RB[0][:, t * C:(t + 1) * C], lTs[x][:, k, t * P:(t + 1) * P], wls[w][:, k, C:2 * C],
                                          start=k + x + w == 0, stop=k == KC - 1 and x == 1)
                            if t == 0 and k == 0:
                                pe.wait_ge(s1_ksq, m + 1)
                            jt = t * KC + k
                            for i in range(2):
                                ins = pe.matmul(KSUM[:, jt * 4 + i * 2:jt * 4 + i * 2 + 2], ksq[:, i, jt * P:(jt + 1) * P], g["headsel"][:], start=True, stop=True)
                    ins.then_inc(s1_ssk, 1)

                def turn_q(m):
                    pe.wait_ge(freed_dve, 2 * m + 1)
                    pe.wait_ge(s1_qn, m + 1)
                    for i in range(2):
                        for t in range(T):
                            ins = pe.transpose(RB[1][:, i * S + t * P:i * S + (t + 1) * P], qn[:, t, i * P:(i + 1) * P], ident[:])
                    ins.then_inc(s1_qturned, 1)

                def score(m, p, h):
                    lo = (h % 2) * D
                    for jp in range(2):
                        i = 2 * h + jp
                        pe.wait_ge(exps, count(16 * m + 2 * i - 2) if i else count(16 * m))
                        if i == 0:
                            pe.wait_ge(q_low, m + 1)
                            pe.wait_ge(k_low, 2 * m + 2)
                        for j in range(2):
                            jt = jp + 2 * (1 - j)
                            for x, w in PASSES:
                                ins = pe.matmul(SC[jp][:, j * S:(j + 1) * S], kTs[p][w][lo:lo + D, h // 2, jt * P:(jt + 1) * P],
                                                qTs[p][x][lo:lo + D, h // 2, :], start=x + w == 0, stop=x == 1)
                        ins.then_inc(scores, 1)

                def products(m, p, h):
                    if h == 0:
                        pe.wait_ge(freed_dve, 2 * m + 2)
                        pe.wait_ge(s2_on, count(m))
                    pe.wait_ge(exps, 16 * m + 4 * h + 4)
                    for t in range(T):
                        for jt in range(4):
                            ins = pe.matmul(O[t][:, h * (D + 1):(h + 1) * (D + 1)], pm[h % 2][:, jt, t * P:(t + 1) * P], va[p][:, jt, h, :],
                                            start=jt == 0, stop=jt == 3)
                    ins.then_inc(pv, 1)

                def turn_o(m):
                    pe.wait_ge(rt.cols_ready, count(m))
                    pe.wait_ge(s2_on, m + 1)
                    for k in range(KC):
                        for t in range(T):
                            ins = pe.transpose(TA[:, k * S + t * P:k * S + (t + 1) * P], on[:, t, k * P:(k + 1) * P], ident[:])
                    ins.then_inc(s2_turned, 1)

                def project_o(m):
                    pe.wait_ge(rt.idx_ready, count(m))
                    pe.wait_ge(o_low, m + 1)
                    for t in range(T):
                        for k in range(KC):
                            for x, w in PASSES:
                                ins = pe.matmul(TB[:, t * C:(t + 1) * C], onTs[x][:, k, t * P:(t + 1) * P], wos[w][:, k, :],
                                                start=k + x + w == 0, stop=k == KC - 1 and x == 1)
                    ins.then_inc(s2_wo, 1)

                def step(n, q):
                    core, front, tail = within(n, B), within(n + 1, B), within(n - 1, B)
                    m, f = n - 1, n + 1
                    if isinstance(n, int) and n == 0:
                        pe.wait_ge(consts_ready, 2)
                    if core:
                        score(n, q, 0)
                    if within(n - 2, B):
                        rt.pe_prefix(pe, n - 2, TB[:, 128:128 + (T + 1) * E].rearrange("p (t e) -> p t e", t=T + 1))
                    if tail:
                        turn_o(m)
                    if front:
                        turn(f)
                    if core:
                        score(n, q, 1)
                        products(n, q, 0)
                    if tail:
                        project_o(m)
                    if isinstance(n, int) and n == -1:
                        pe.wait_ge(w_low, len(split))
                    if front:
                        project_qk(f)
                    if core:
                        score(n, q, 2)
                        products(n, q, 1)
                    if tail:
                        rt.pe_turn(pe, m, 1 - q, TA[:].rearrange("p (k s) -> p k s", k=KC))
                    if core:
                        score(n, q, 3)
                    if tail:
                        rt.pe_logits(pe, m, TB[:, 0:T * E].rearrange("p (t e) -> p t e", t=T))
                    if front:
                        project_v_ctx(f)
                    if core:
                        products(n, q, 2)
                    if front:
                        project_v_lat_key_sums(f)
                        turn_q(f)
                    if core:
                        products(n, q, 3)
                over_batches(pe, -1, step)


class XRTile:

    def __init__(self, xr, n):
        self.xr, self.n = xr, n

    def __getitem__(self, k):
        _, t, _ = k
        return self.xr[:, ds(self.n * T + t, 1), :].rearrange("p o c -> p (o c)")



def pad_dummies(sp, g, rows, dummy, done):
    for d in range(E):
        sp.dma_start(rows[dummy + d * P:dummy + (d + 1) * P, :], g["padding"][:, 0:rows.shape[1]]).then_inc(done, 16)


class TileExperts:

    def __init__(self, eng, name, table, n, top):
        self.eng, self.table, self.n, self.top = eng, table, n, top
        self.register = [eng.alloc_register(f"{name}{z}") for z in range(4)]
        self.looping, self.loaded = False, {}

    def at(self, i):
        return self.table[0:1, ds(i, 1)]

    def enter_loop(self, s):
        self.looping = True
        for i in (s - 2, s - 1, s):
            self.eng.reg_load(self.register[i % 4], self.at(i))

    def leave_loop(self):
        self.looping, self.loaded = False, {}

    def of(self, k):
        if self.looping:
            return bass.RuntimeValue.of_register_unchecked(self.register[(self.q + k) % 4]).with_bounds(min_val=0, max_val=self.top)
        i = self.s + k
        if i not in self.loaded:
            self.loaded[i] = self.eng.value_load(self.at(i), min_val=0, max_val=self.top)
        return self.loaded[i]

    def ahead(self):
        if self.looping:
            self.eng.reg_load(self.register[(self.q + 1) % 4], self.at(self.s + 1))
        elif within(self.s + 1, self.n):
            self.of(1)


def over_tiles(eng, step, n, experts=None):
    def run(s, q):
        if experts:
            experts.s, experts.q = s, q
        step(s, q)
    for s in range(-3, 8):
        run(s, s % 4)
    if experts:
        experts.enter_loop(8)
    end = 8 + (n - 3 - 8) // 4 * 4
    with eng.Fori(8, end - 3, 4) as s:
        for q in range(4):
            run(s + q, q)
    if experts:
        experts.leave_loop()
    for s in range(end, n + 3):
        run(s, s % 4)


def phase_experts(nc, a, g, layer, out=None):
    if layer == 0:
        tiles, F, zd, yd, EW = TILES0, F0, g["z0"], g["y0"], E + 1
        wh, wl, uh, ul, NF = g["w13h"], g["w13l"], g["w2h"], g["w2l"], 2
        chunks = F0_CHUNKS
    else:
        tiles, F, zd, yd, EW = ROUTED1, F1, g["z1"], None, E
        wh, wl, uh, ul, NF = g["v1h"], g["v1l"], g["v2h"], g["v2l"], 1
        chunks = [(k * P, P) for k in range(F1 // P)]
    NCH = len(chunks)
    HW = NCH * P
    rows = zd.shape[0]
    with ExitStack() as c:
        sb = lambda n, s, d=F32: c.enter_context(nc.sbuf_tensor(f"e{layer}_{n}", s, d))
        pb = lambda n: c.enter_context(nc.psum_tensor(f"e{layer}_{n}", [P, 512], F32))
        sem = lambda n: phase_semaphore(nc, g, f"e{layer}_{n}")
        NZ = 4
        NY = 2 if layer == 0 else 4
        zs = [sb(f"z_rows{p}", [P, C]) for p in range(NZ)]
        tokens = [sb(f"token_rows{p}", [P, W1 - TOKEN]) for p in range(NZ)]
        xh = [sb(f"z_high{p}", [P, KC, P], F16) for p in range(2)]
        xl = [sb(f"z_low{p}", [P, KC, P], F16) for p in range(2)]
        act_out = sb("act_out", [P, F])
        hs = [sb(f"hidden{p}", [P, F]) for p in range(2)]
        hh = [sb(f"hidden_high{p}", [P, NCH, P], F16) for p in range(2)]
        hl = [sb(f"hidden_low{p}", [P, NCH, P], F16) for p in range(2)]
        ys = [sb(f"y_rows{p}", [P, C]) for p in range(NY)]
        yb, number = [sb(f"y_biased{p}", [P, C]) for p in range(2)], [sb(f"token_numbers{p}", [P, 1], I32) for p in range(NY)]
        ZT, Y = pb("z_cols"), [pb(f"y{p}") for p in range(2)]
        NH = 1 if layer == 0 else 2
        HT = [pb(f"hidden_cols{p}") for p in range(NH)]
        GU = [[pb(f"first{f}_{p}") for f in range(NF)] for p in range(2)]
        landed, stored = [sem(f"landed{p}") for p in range(NZ)], [sem(f"stored{p}") for p in range(NY)]
        turned, zhigh, zlow, first_done, act_done, hidden_done = (sem(x) for x in ("turned", "zhigh", "zlow", "first_done", "act_done", "hidden_done"))
        h_turned, hhigh, hlow, y_done, y_out, blank = (sem(x) for x in ("h_turned", "hhigh", "hlow", "y_done", "y_out", "blank"))
        tokens_landed = [sem(f"tokens_landed{p}") for p in range(NZ)]
        biased, y_biased, slot_step = sem("biased"), sem("y_biased"), sem("slot_step")
        slf, sel, less = sb("slots", [P, NT * 2]), sb("slot_after", [P, NT * 2, E]), sb("slot_less", [P, NT * 2])

        def experts_on(eng):
            return TileExperts(eng, f"expert{layer}_", g["tabexp"], tiles, EW - 1)

        with nc.Block() as block:
            @block.sync
            def _(sp):
                def step(s, q):
                    i, p = s + 3, (q + 3) % NZ
                    if within(i, tiles):
                        r = sp.value_load(g["tabrow"][0:1, ds(i, 1)], min_val=0, max_val=rows - P)
                        sp.wait_ge(turned, count(i - NZ + 1))
                        sp.dma_start(zs[p][:], zd[ds(r, P), 0:C]).then_inc(landed[p], 16)
                    i, p = s + 1, (q + 1) % NZ
                    if within(i, tiles) and layer == 1:
                        r = sp.value_load(g["tabrow"][0:1, ds(i, 1)], min_val=0, max_val=rows - P)
                        sp.wait_ge(y_out, count(i - NZ + 1))
                        sp.dma_start(tokens[p][:], zd[ds(r, P), TOKEN:W1]).then_inc(tokens_landed[p], 16)
                    i, p = s - 2, (q + 2) % 2
                    if within(i, tiles) and layer == 0:
                        sp.wait_ge(y_out, i + 1)
                        sp.dma_start(yd[ds(i * P, P), :], ys[p][:]).then_inc(stored[p], 16)
                over_tiles(sp, step, tiles)
                for p in range(NY):
                    sp.wait_ge(stored[p], 16 * len(range(p, tiles, NY)))

            @block.gpsimd
            def _(pool):
                def step(s, q):
                    i, p = s - 2, (q - 2) % NY
                    if within(i, tiles):
                        pool.wait_ge(y_out, i + 1)
                        pool.sem_inc(g["carried"], 1)
                        pool.indirect_dma_start(out, bass.IndirectOffsetOnAxis(ap=number[p][:], axis=0), ys[p][:], None,
                                                bounds_check=NTOK - 1, oob_is_err=False).then_inc(stored[p], 16)
                if layer == 1:
                    over_tiles(pool, step, tiles)

            @block.tensor
            def _(pe):
                pe.wait_ge(blank, NH)
                experts = experts_on(pe)

                def step(s, q):
                    i, p = s, q % 2
                    if within(i, tiles):
                        e = experts.of(0)
                        pe.wait_ge(hidden_done, count(i - 1))
                        pe.wait_ge(zlow, i + 1)
                        for k in range(KC):
                            for x, w in ((xh, wh), (xh, wl), (xl, wh)):
                                for f in range(NF):
                                    off = e * (NF * F) + (k * EW * NF * F + f * F)
                                    ins = pe.matmul(GU[p][f][:, 0:F], x[p][:, k, :], w[:, ds(off, F)],
                                                    start=(k == 0 and x is xh and w is wh), stop=(k == KC - 1 and x is xl))
                        ins.then_inc(first_done, 1)
                    experts.ahead()
                    i, p = s + 1, (q + 1) % 2
                    if within(i, tiles):
                        z = (q + 1) % NZ
                        pe.wait_ge(landed[z], (i - z) * (16 // NZ) + 16)
                        pe.wait_ge(zlow, count(i))
                        for k in range(KC):
                            ins = pe.transpose(ZT[:, k * P:(k + 1) * P], zs[z][:, k * P:(k + 1) * P], g["ident"][:])
                        ins.then_inc(turned, 1)
                    i, p = s - 1, (q + 1) % 2
                    if within(i, tiles):
                        pe.wait_ge(hlow, count(i - NH + 1))
                        pe.wait_ge(hidden_done, i + 1)
                        for n, (o, m) in enumerate(chunks):
                            ins = pe.transpose(HT[p % NH][0:m, n * P:(n + 1) * P], hs[p][:, o:o + m], g["ident"][:])
                        ins.then_inc(h_turned, 1)
                    i, p = s - 2, q % 2
                    if within(i, tiles):
                        e = experts.of(-2)
                        pe.wait_ge(y_out, count(i - 1))
                        pe.wait_ge(hlow, i + 1)
                        for n, (o, m) in enumerate(chunks):
                            for x, w in ((hh, uh), (hh, ul), (hl, uh)):
                                ins = pe.matmul(Y[p][:, 0:C], x[p][0:m, n, :], w[0:m, ds(e * C + n * EW * C, C)],
                                                start=(n == 0 and x is hh and w is uh), stop=(n == NCH - 1 and x is hl))
                        ins.then_inc(y_done, 1)
                over_tiles(pe, step, tiles, experts)

            @block.scalar
            def _(act):
                def step(s, q):
                    i, p = s + 1, (q + 1) % 2
                    if within(i, tiles):
                        act.wait_ge(first_done, count(i - 1))
                        act.wait_ge(turned, i + 1)
                        act.activation(xh[p][:].rearrange("p k s -> p (k s)"), ZT[:, 0:KC * P], ACT.Copy).then_inc(zhigh, 1)
                    i, p = s, q % 2
                    if within(i, tiles):
                        if layer == 0:
                            act.wait_ge(hidden_done, count(i))
                            act.wait_ge(first_done, i + 1)
                            act.activation(act_out[:], GU[p][0][:, 0:F], ACT.Silu, scale=1.0 / WSCALE).then_inc(act_done, 1)
                        else:
                            act.wait_ge(h_turned, count(i - 1))
                            act.wait_ge(biased, i + 1)
                            act.activation(hs[p][:], act_out[:], ACT.Gelu).then_inc(hidden_done, 1)
                    i, p = s - 1, (q + 1) % 2
                    if within(i, tiles):
                        act.wait_ge(y_done, count(i - 1))
                        act.wait_ge(h_turned, i + 1)
                        act.activation(hh[p][:].rearrange("p k s -> p (k s)"), HT[p % NH][:, 0:HW], ACT.Copy).then_inc(hhigh, 1)
                    i, p = s - 2, q % 2
                    if within(i, tiles) and layer == 0:
                        act.wait_ge(stored[p], count((i - p) * 8))
                        act.wait_ge(y_done, i + 1)
                        act.activation(ys[p][:], Y[p][:, 0:C], ACT.Copy, scale=1.0 / WSCALE).then_inc(y_out, 1)
                over_tiles(act, step, tiles)

            @block.vector
            def _(v):
                def slots_to_results():
                    ch = Chain(v, slot_step)
                    full = [P, NT * 2, E]
                    SL = g["SL0"][:].rearrange("p n k -> p (n k)")
                    ch.link(v.tensor_copy(slf[:], SL))
                    ch.link(v.tensor_tensor(sel[:], slf[:].unsqueeze(2).to_broadcast(full), g["regbase"][:].unsqueeze(1).to_broadcast(full), ALU.is_ge))
                    ch.link(v.tensor_tensor(sel[:], sel[:], g["base_steps"][:].unsqueeze(1).to_broadcast(full), ALU.mult))
                    ch.link(v.tensor_reduce(less[:], sel[:], AX.X, ALU.add))
                    ch.link(v.tensor_tensor(SL, slf[:], less[:], ALU.subtract))

                for bank in HT:
                    v.memset(bank[:], 0.0).then_inc(blank, 1)
                experts = experts_on(v)

                def step(s, q):
                    if layer == 0 and isinstance(s, int) and s == tiles:
                        slots_to_results()
                    i, p = s, q % 2
                    if within(i, tiles) and layer == 1:
                        e = experts.of(0)
                        v.wait_ge(hidden_done, count(i))
                        v.wait_ge(first_done, i + 1)
                        v.scalar_tensor_tensor(act_out[:], GU[p][0][:, 0:F], 1.0 / WSCALE, g["b1"][:, ds(e * F, F)], ALU.mult, ALU.add).then_inc(biased, 1)
                    if layer == 1:
                        experts.ahead()
                    i, p = s + 1, (q + 1) % 2
                    if within(i, tiles):
                        v.wait_ge(first_done, count(i - 1))
                        v.wait_ge(zhigh, i + 1)
                        v.tensor_tensor(xl[p][:].rearrange("p k s -> p (k s)"), ZT[:, 0:KC * P], xh[p][:].rearrange("p k s -> p (k s)"), ALU.subtract).then_inc(zlow, 1)
                    i, p = s, q % 2
                    if within(i, tiles) and layer == 0:
                        v.wait_ge(h_turned, count(i - 1))
                        v.wait_ge(act_done, i + 1)
                        v.scalar_tensor_tensor(hs[p][:], GU[p][1][:, 0:F], 1.0 / WSCALE, act_out[:], ALU.mult, ALU.mult).then_inc(hidden_done, 1)
                    i, p = s - 1, (q + 1) % 2
                    if within(i, tiles):
                        v.wait_ge(y_done, count(i - 1))
                        v.wait_ge(hhigh, i + 1)
                        v.tensor_tensor(hl[p][:].rearrange("p k s -> p (k s)"), HT[p % NH][:, 0:HW], hh[p][:].rearrange("p k s -> p (k s)"), ALU.subtract).then_inc(hlow, 1)
                    i, p = s - 2, q % 2
                    if within(i, tiles) and layer == 1:
                        e = experts.of(-2)
                        y = (q - 2) % NY
                        token = tokens[y]
                        v.wait_ge(stored[y], count((i - y) * (16 // NY)))
                        v.wait_ge(y_out, count(i - 1))
                        v.wait_ge(tokens_landed[y], (i - y) * (16 // NZ) + 16)
                        v.wait_ge(y_done, i + 1)
                        v.scalar_tensor_tensor(yb[p][:], Y[p][:, 0:C], 1.0 / WSCALE, g["b2"][:, ds(e * C, C)], ALU.mult, ALU.add).then_inc(y_biased, 1)
                        v.tensor_copy(number[y][:], token[:, NUMBER - TOKEN:NUMBER - TOKEN + 1])
                        v.wait_ge(y_biased, i + 1)
                        v.scalar_tensor_tensor(ys[y][:], yb[p][:], token[:, SCALE - TOKEN:SCALE - TOKEN + 1], token[:, 0:C], ALU.mult, ALU.add).then_inc(y_out, 1)
                over_tiles(v, step, tiles, experts)


def gather(pool, idx, k, t, rows, dst, done):
    pool.indirect_dma_start(dst, None, rows, bass.IndirectOffsetOnAxis(ap=idx[:, k, t:t + 1], axis=0)).then_inc(done, 16)


def phase_attn1(nc, a, g):
    with ExitStack() as c:
        sb = lambda n, s, d=F32: c.enter_context(nc.sbuf_tensor(f"a1_{n}", s, d))
        pb = lambda n: c.enter_context(nc.psum_tensor(f"a1_{n}", [P, 512], F32))
        sem = lambda n: phase_semaphore(nc, g, f"a1_{n}")
        wq, wk, wv = sb("wq", [P, KC, C]), sb("wk", [P, 2, C]), sb("wv", [P, 2, C])
        cols = sb("columns", [P, 2 * KC])
        numbers = sb("first_numbers", [P, T], I32)
        ONES = DC - P
        bq, bk = cols[:, 0:KC], cols[:, KC:2 * KC]
        w_red, wg1, wgn, wg = sb("w_red", [16, C]), sb("wg1", [E, 16]), sb("wg_norm", [16, E]), sb("wg_joint", [P, KC, E])
        wsq, wnorm = sb("wg_squares", [E, 16]), sb("wg_norms", [E, 1])
        idx = [sb(f"slots{p}", [P, 2, T], I32) for p in range(2)]
        pr = [sb(f"probs_chosen{p}", [P, T, 2]) for p in range(2)]
        yk = [sb(f"y_chosen{p}", [P, 2, T, C]) for p in range(2)]
        ysh = [sb(f"y_shared{p}", [P, T, C]) for p in range(2)]
        cin = [sb(f"ctx_in{p}", [P, T, DC]) for p in range(2)]
        st, mv, r1 = sb("stats", [P, T, 6]), sb("mean_var", [P, T, 2]), sb("rstd", [P, T])
        xn = sb("x_norm", [P, T, C])
        lT, cT = sb("x_cols", [P, KC, S]), sb("ctx_cols", [P, 2, S])
        qT = [sb(f"q_cols{p}", [P, KC, S]) for p in range(2)]
        kT = [sb(f"k_cols{p}", [P, KC, S]) for p in range(2)]
        vt = [sb(f"v_tokens{p}", [P, T, C]) for p in range(2)]
        nmax, esum, rs = sb("minus_max", [P, T]), sb("exp_sum", [P, T]), sb("exp_rsum", [P, T])
        pm, pT = sb("probs", [P, T, S]), sb("prob_cols", [P, T, S])
        BT, BC = pb("turn"), pb("turn_ctx")
        PJ = [pb("proj0"), pb("proj1")]
        SC, PT, O, R = pb("scores"), pb("prob_turn"), pb("out"), pb("route")
        rt = Route(nc, g, c, "r1", 1, None, None, g["RUN1"], g["z1"], wg)
        weights, table, dummies_padded = Weights(nc, g, a, c, 1), Table(nc, g, c, 1, [sb("table_space", [P, 2560])[:]]), sem("dummies_padded")

        consts_in, biases_in, consts_ready, cstep, wg_turned, wg_norms = (sem(x) for x in ("consts_in", "biases_in", "consts_ready", "cstep", "wg_turned", "wg_norms"))
        landed_y, landed_c = [sem(f"landed_y{p}") for p in range(2)], [sem(f"landed_ctx{p}") for p in range(2)]
        gathered = [sem(f"gathered{p}") for p in range(2)]
        slots_ready, s1_x2, s1_stats, s1_rstd, s1_norm, s1_turned, s1_cols = (sem(f"s1_{x}") for x in ("slots", "x2", "stats", "rstd", "norm", "turned", "cols"))
        proj_ready, freed_act, v_tokens, ones_ready = sem("proj_ready"), sem("proj_freed_act"), sem("v_tokens"), sem("ones_ready")
        numbered = sem("numbered")
        scored, maxed, expd, p_turned, p_cols, pv = (sem(x) for x in ("scored", "maxed", "expd", "p_turned", "p_cols", "pv"))
        d1, d2, p1 = sem("dve_step1"), sem("dve_step2"), sem("pool_step1")
        D1, D2, P1 = 7, 4, 2
        loads = [(cols[:], a["cols1"]), (wq[:], a["wq1"].rearrange("(k p) f -> p k f", p=P)),
                 (wk[:, 0, :], a["wk1"][0:P]), (wk[0:DC - P, 1, :], a["wk1"][P:DC]),
                 (wv[:, 0, :], a["wv1"][0:P]), (wv[0:DC - P, 1, :], a["wv1"][P:DC]),
                 (wv[ONES:ONES + 1, 1, :], a["bv1"].rearrange("(o n) -> o n", o=1)),
                 (w_red[:], a["w_red"]), (wg1[:], a["wg1"])]
        biases = [(g["b1"][:], a["b1"].rearrange("(o e) f -> o (e f)", o=1).to_broadcast([P, E * F1])),
                  (g["b2"][:], a["b2"].rearrange("(o e) f -> o (e f)", o=1).to_broadcast([P, E * C]))]
        n_consts = 16 * len(loads)

        with nc.Block() as block:
            @block.sync
            def _(sp):
                def load_y(m, p):
                    sp.wait_ge(s1_x2, count(m - 1))
                    sp.dma_start(ysh[p][:], g["y0"][ds(m * S + ROUTED0 * P, S), :].rearrange("(t p) c -> p t c", p=P)).then_inc(landed_y[p], 16)

                def load_ctx(m, p):
                    sp.wait_ge(s1_turned, count(m - 1))
                    sp.dma_start(cin[p][:], a["ctx"][ds(m * S, S), :].rearrange("(t p) c -> p t c", p=P)).then_inc(landed_c[p], 16)

                def step(n, q):
                    if within(n + 4, B):
                        load_y(n + 4, q)
                    if isinstance(n, int) and n == -4:
                        for dst, src in loads:
                            sp.dma_start(dst, src).then_inc(consts_in, 16)
                    if isinstance(n, int) and n == 2:
                        pad_dummies(sp, g, g["z1"], DUMMY1, dummies_padded)
                    if isinstance(n, int) and n == 0:
                        for dst, src in biases:
                            sp.dma_start(dst, src).then_inc(biases_in, 16)
                    if within(n + 3, B):
                        load_ctx(n + 3, 1 - q)
                    if within(n + 3, weights.parts):
                        weights.load(sp, n + 3, 1 - q)
                over_batches(sp, -4, step, B - 5)
                table.pad(sp, range(0, E, 2))
                table.finish(sp)
                rt.finish(sp, False)
                sp.wait_ge(biases_in, 32)
                sp.wait_ge(dummies_padded, 16 * E)

            @block.gpsimd
            def _(pool):
                pool.iota(numbers[:], pattern=[[P, T]], base=0, channel_multiplier=1).then_inc(numbered, 1)

                def fetch(n, p):
                    pool.wait_ge(slots_ready, n + 1)
                    pool.sem_inc(g["carried"], 1)
                    for k in range(2):
                        for t in range(T):
                            gather(pool, idx[p], k, t, g["y0"], yk[p][:, k, t, :], gathered[p])

                def rstd(m):
                    ch = Chain(pool, p1, m * P1)
                    pool.wait_ge(s1_stats, m + 1)
                    ch.link(pool.tensor_tensor(r1[:], mv[:, :, 1], g["epst"][:, 0:T], ALU.add))
                    ch.link(pool.tensor_tensor(r1[:], r1[:], g["mhalf"][:, 0:T], ALU.pow))
                    pool.sem_inc(s1_rstd, 1)
                    assert ch.n == P1

                def step(n, q):
                    if within(n - 1, B):
                        rt.pool_rstd(pool, n - 1)
                    if within(n + 3, B):
                        fetch(n + 3, 1 - q)
                    if isinstance(n, int) and n == -2:
                        pool.wait_ge(wg_norms, 1)
                        pool.tensor_tensor(wnorm[:], wnorm[:], g["mhalf"][0:E, 0:1], ALU.pow).then_inc(wg_norms, 1)
                    if within(n + 2, B):
                        rstd(n + 2)
                    if isinstance(n, int) and n == B + 1:
                        table.pool_iotas(pool)
                    if within(n - 2, B):
                        rt.pool_scatter(pool, n - 2, q)
                over_batches(pool, -4, step, B - 5)

            @block.scalar
            def _(act):
                act.wait_ge(consts_in, n_consts)

                def columns(m):
                    act.wait_ge(proj_ready, count(3 * m))
                    act.wait_ge(s1_turned, m + 1)
                    act.activation(lT[:].rearrange("p k s -> p (k s)"), BT[:], ACT.Copy)
                    for k, (o, w) in enumerate(CTX_CHUNKS):
                        ins = act.activation(cT[0:w, k, :], BC[0:w, k * S:(k + 1) * S], ACT.Copy)
                    ins.then_inc(s1_cols, 1)

                def bias_q_or_k(m, p, i):
                    dst, b = ((qT, bq), (kT, bk))[i]
                    act.wait_ge(scored, count(m - 1))
                    act.wait_ge(proj_ready, 3 * m + 1 + i)
                    for k in range(KC):
                        ins = act.activation(dst[p][:, k, :], PJ[i][:, k * S:(k + 1) * S], ACT.Identity, bias=b[:, k:k + 1])
                    ins.then_inc(freed_act, 1)

                def copy_v(m, p):
                    act.wait_ge(pv, count(m - 1))
                    act.wait_ge(proj_ready, 3 * m + 3)
                    act.activation(vt[p][:].rearrange("p t c -> p (t c)"), BT[:], ACT.Copy).then_inc(v_tokens, 1)

                def exps(n):
                    act.wait_ge(p_turned, count(n))
                    act.wait_ge(maxed, n + 1)
                    for t in range(T):
                        ins = act.activation(pm[:, t, :], SC[:, t * S:(t + 1) * S], ACT.Exp, bias=nmax[:, t:t + 1], accum_out=esum[:, t:t + 1])
                    ins.then_inc(expd, 1)

                def prob_columns(n):
                    act.wait_ge(pv, count(n))
                    act.wait_ge(p_turned, n + 1)
                    act.activation(pT[:].rearrange("p j s -> p (j s)"), PT[:], ACT.Copy).then_inc(p_cols, 1)

                def step(n, q):
                    core, front, tail = within(n, B), within(n + 1, B), within(n - 1, B)
                    early = isinstance(n, int) and n == -1
                    if early:
                        weights.high(act, n + 1, 1 - q)
                    if front:
                        columns(n + 1)
                    if core:
                        exps(n)
                    if front:
                        bias_q_or_k(n + 1, 1 - q, 0)
                    if core:
                        prob_columns(n)
                    if within(n - 2, B):
                        rt.act_exp(act, n - 2)
                    if tail:
                        rt.act_cols(act, n - 1, PT[:].rearrange("p (k s) -> p k s", k=KC))
                        rt.act_tokens(act, n - 1, 1 - q)
                    if front:
                        copy_v(n + 1, 1 - q)
                        bias_q_or_k(n + 1, 1 - q, 1)
                    if not early and within(n + 1, weights.parts):
                        weights.high(act, n + 1, 1 - q)
                over_batches(act, -1, step)
                table.pad(act, range(1, E, 2))

            @block.vector
            def _(v):
                v.memset(cT[ONES:ONES + 1, 1, :], 1.0).then_inc(ones_ready, 1)
                chains = {}

                def router_norms():
                    v.wait_ge(numbered, 1)
                    v.tensor_copy(rt.number[:], numbers[:])
                    v.wait_ge(consts_in, n_consts)
                    ch = Chain(v, cstep)
                    ch.link(v.tensor_tensor(wsq[:], wg1[:], wg1[:], ALU.mult))
                    ch.link(v.tensor_reduce(wnorm[:], wsq[:], AX.X, ALU.add))
                    ch.link(v.tensor_scalar(wnorm[:], wnorm[:], 1e-8, None, ALU.max))
                    v.sem_inc(wg_norms, 1)
                    return ch

                def router_joint(ch):
                    v.wait_ge(wg_norms, 2)
                    ch.link(v.tensor_scalar(wg1[:], wg1[:], wnorm[:, 0:1], None, ALU.mult))
                    v.sem_inc(consts_ready, 1)
                    v.wait_ge(wg_turned, 1)
                    ch.link(v.tensor_copy(wgn[:], R[0:16, 0:E]))
                    v.sem_inc(consts_ready, 1)
                    v.wait_ge(wg_turned, 2)
                    ch.link(v.tensor_copy(wg[:].rearrange("p k e -> p (k e)"), R[:, 16:16 + KC * E]))
                    v.sem_inc(consts_ready, 1)

                def slots(m, p):
                    v.wait_ge(gathered[p], count((m - p) * 32))
                    v.tensor_copy(pr[p][:], g["PR0"][:, ds(m * T, T), :])
                    v.tensor_copy(idx[p][:].rearrange("p k t -> p t k"), g["SL0"][:, ds(m * T, T), :]).then_inc(slots_ready, 1)

                def x2_step(m, p, i):
                    xr = g["XR"][:, ds(m * T, T), :]
                    if i == 0:
                        chains["x2"] = Chain(v, d1, m * D1)
                        v.wait_ge(landed_y[p], (m - p) * 8 + 16)
                        v.wait_ge(gathered[p], (m - p) * 32 + 64)
                    ch, (k, t) = chains["x2"], divmod(i, T)
                    if i in (2, 4, 5):
                        ch.wait()
                    if i < 4:
                        ch.mark(v.scalar_tensor_tensor(ysh[p][:, t, :], yk[p][:, k, t, :], pr[p][:, t, k:k + 1], ysh[p][:, t, :], ALU.mult, ALU.add))
                    elif i == 4:
                        ch.mark(v.scalar_tensor_tensor(xr, ysh[p][:], g["gate"][:, 2:3], xr, ALU.mult, ALU.add))
                    else:
                        if i == 5:
                            v.sem_inc(s1_x2, 1)
                        ch.mark(v.bn_stats(st[:, i - 5, :], XRTile(g["XR"], m)[:, i - 5, :]))

                def x2_mean_var():
                    ch = chains["x2"]
                    ch.wait()
                    v.sem_inc(g["carried_v"], 1)
                    for t in range(T):
                        ins = v.bn_aggr(mv[:, t, :], st[:, t, :])
                    ins.then_inc(s1_stats, 1)
                    assert ch.n == D1, ch.n

                def pre_norm(m):
                    v.wait_ge(s1_turned, count(m))
                    v.wait_ge(s1_rstd, m + 1)
                    x = XRTile(g["XR"], m)
                    for t in range(T):
                        ins = v.tensor_scalar(xn[:, t, :], x[:, t, :], mv[:, t, 0:1], r1[:, t:t + 1], ALU.subtract, ALU.mult)
                    ins.then_inc(s1_norm, 1)

                def maxima(n):
                    v.wait_ge(expd, count(n))
                    v.wait_ge(scored, n + 1)
                    v.tensor_reduce(nmax[:], SC[:].rearrange("p (t s) -> p t s", t=T), AX.X, ALU.max, negate=True).then_inc(maxed, 1)

                def scales(n):
                    ch = Chain(v, d2, n * D2)
                    v.wait_ge(expd, n + 1)
                    ch.link(v.reciprocal(rs[:], esum[:]))
                    ch.link(v.tensor_scalar(rs[:], rs[:], g["gate"][:, 1:2], None, ALU.mult))

                def x3(m):
                    ch = Chain(v, d2, m * D2)
                    ch.n = 2
                    v.wait_ge(pv, m + 1)
                    xr = XRTile(g["XR"], m)
                    for t in range(T):
                        ch.mark(v.scalar_tensor_tensor(xr[:, t, :], O[:, t * C:(t + 1) * C], rs[:, t:t + 1], xr[:, t, :], ALU.mult, ALU.add))
                    ch.wait()
                    assert ch.n == D2, ch.n
                    rt.vector_stats(v, m, xr)

                def step(n, q):
                    core, front, tail = within(n, B), within(n + 1, B), within(n - 1, B)
                    m = n - 1
                    if within(n + 3, B):
                        slots(n + 3, 1 - q)
                    if core:
                        maxima(n)
                    if within(n - 2, B):
                        rt.vector_choose(v, n - 2, q, R[:, 0:T * E].rearrange("p (t e) -> p t e", t=T),
                                         (lambda i: x2_step(n + 2, q, i)) if within(n + 2, B) else None)
                    elif within(n + 2, B):
                        for i in range(D1):
                            x2_step(n + 2, q, i)
                    if within(n + 2, B):
                        x2_mean_var()
                    if tail:
                        rt.vector_z(v, m, 1 - q, XRTile(g["XR"], m), False)
                    if core:
                        scales(n)
                    if isinstance(n, int) and n == B + 1:
                        table.vector_numbers(v)
                    if within(n - 2, B):
                        rt.vector_slots(v, n - 2, q, R[:, 128:128 + (T + 1) * E].rearrange("p (t e) -> p t e", t=T + 1))
                    if within(n + 2, B):
                        pre_norm(n + 2)
                    if core:
                        x3(n)
                    if within(n + 1, weights.parts):
                        weights.low(v, n + 1, 1 - q)
                    if isinstance(n, int) and n == -3:
                        chains["router"] = router_norms()
                    if isinstance(n, int) and n == -2:
                        router_joint(chains["router"])
                over_batches(v, -4, step, B - 5)
                table.vector_table(v)

            @block.tensor
            def _(pe):
                ident = g["ident"]
                pe.wait_ge(ones_ready, 1)
                pe.wait_ge(consts_in, n_consts)

                def router():
                    pe.wait_ge(consts_ready, 1)
                    pe.transpose(R[0:16, 0:E], wg1[:], ident[0:E, 0:E]).then_inc(wg_turned, 1)
                    pe.wait_ge(consts_ready, 2)
                    for k in range(KC):
                        ins = pe.matmul(R[:, 16 + k * E:16 + (k + 1) * E], w_red[:, k * P:(k + 1) * P], wgn[:], start=True, stop=True)
                    ins.then_inc(wg_turned, 1)
                    pe.wait_ge(consts_ready, 3)

                def turn(m, p):
                    pe.wait_ge(s1_norm, m + 1)
                    pe.wait_ge(v_tokens, count(m))
                    for k in range(KC):
                        for t in range(T):
                            pe.transpose(BT[:, k * S + t * P:k * S + (t + 1) * P], xn[:, t, k * P:(k + 1) * P], ident[:])
                    pe.wait_ge(landed_c[p], (m - p) * 8 + 16)
                    for k, (o, w) in enumerate(CTX_CHUNKS):
                        for t in range(T):
                            ins = pe.transpose(BC[0:w, k * S + t * P:k * S + (t + 1) * P], cin[p][:, t, o:o + w], ident[:])
                    ins.then_inc(s1_turned, 1)

                def project_qk(m):
                    pe.wait_ge(s1_cols, m + 1)
                    pe.wait_ge(freed_act, count(2 * m - 1))
                    for i in range(KC):
                        for k in range(KC):
                            ins = pe.matmul(PJ[0][:, i * S:(i + 1) * S], wq[:, k, i * P:(i + 1) * P], lT[:, k, :], start=k == 0, stop=k == KC - 1)
                    ins.then_inc(proj_ready, 1)
                    pe.wait_ge(freed_act, count(2 * m))
                    for i in range(KC):
                        for k, (o, w) in enumerate(CTX_CHUNKS):
                            ins = pe.matmul(PJ[1][:, i * S:(i + 1) * S], wk[0:w, k, i * P:(i + 1) * P], cT[0:w, k, :], start=k == 0, stop=k == 1)
                    ins.then_inc(proj_ready, 1)

                def project_v(m):
                    for t in range(T):
                        for k, w in enumerate((P, ONES + 1)):
                            ins = pe.matmul(BT[:, t * C:(t + 1) * C], cT[0:w, k, t * P:(t + 1) * P], wv[0:w, k, :], start=k == 0, stop=k == 1)
                    ins.then_inc(proj_ready, 1)

                def score(n, p):
                    pe.wait_ge(freed_act, 2 * n + 2)
                    pe.wait_ge(expd, count(n))
                    for t in range(T):
                        for k in range(KC):
                            ins = pe.matmul(SC[:, t * S:(t + 1) * S], qT[p][:, k, t * P:(t + 1) * P], kT[p][:, k, :], start=k == 0, stop=k == KC - 1)
                    ins.then_inc(scored, 1)

                def turn_probs(n):
                    pe.wait_ge(rt.cols_ready, count(n - 1))
                    pe.wait_ge(expd, n + 1)
                    for j in range(T):
                        for t in range(T):
                            ins = pe.transpose(PT[:, j * S + t * P:j * S + (t + 1) * P], pm[:, t, j * P:(j + 1) * P], ident[:])
                    ins.then_inc(p_turned, 1)

                def products(n, p):
                    pe.wait_ge(v_tokens, n + 1)
                    pe.wait_ge(p_cols, n + 1)
                    for t in range(T):
                        for j in range(T):
                            ins = pe.matmul(O[:, t * C:(t + 1) * C], pT[:, j, t * P:(t + 1) * P], vt[p][:, j, :], start=j == 0, stop=j == T - 1)
                    ins.then_inc(pv, 1)

                def step(n, q):
                    core, front, tail = within(n, B), within(n + 1, B), within(n - 1, B)
                    m = n - 1
                    if front:
                        turn(n + 1, 1 - q)
                    if isinstance(n, int) and n == -1:
                        router()
                    if core:
                        score(n, q)
                    if within(n - 2, B):
                        pe.wait_ge(rt.idx_ready, count(n - 2))
                        rt.pe_logits(pe, n - 2, R[:, 0:T * E].rearrange("p (t e) -> p t e", t=T))
                    if front:
                        project_qk(n + 1)
                    if core:
                        turn_probs(n)
                    if front:
                        project_v(n + 1)
                    if within(n - 2, B):
                        rt.pe_prefix(pe, n - 2, R[:, 128:128 + (T + 1) * E].rearrange("p (t e) -> p t e", t=T + 1))
                    if tail:
                        pe.wait_ge(p_cols, count(min(n + 1, B) if isinstance(n, int) else n + 1))
                        rt.pe_turn(pe, m, 1 - q, PT[:].rearrange("p (k s) -> p k s", k=KC))
                    if core:
                        products(n, q)
                over_batches(pe, -1, step)


def lay_out(inputs):
    i = {k: np.asarray(v) for k, v in inputs.items()}

    def columns(*vectors):
        return np.concatenate([np.pad(x, (0, -len(x) % P)).reshape(-1, P) for x in vectors]).T

    T_ = lambda x: np.ascontiguousarray(np.swapaxes(x, -1, -2))
    return {
        "x": i["x"].reshape(NTOK, C), "ctx": i["ctx_768"].reshape(NTOK, DC),
        "mask": np.ascontiguousarray(i["mask_BxS2_bk0"].reshape(B * T, P).T),
        "g_xattn": i["g_xattn"], "g_ffn": i["g_ffn"],
        "cols0": columns(i["L0_xattn_ln_l_g"], i["L0_xattn_ln_l_b"], i["L0_xattn_ln_x_g"], i["L0_xattn_ln_x_b"],
                         np.tile(i["L0_xattn_qn_g"], 2), np.tile(i["L0_xattn_kn_g"], 2)),
        "gains": np.concatenate([i["L0_xattn_qn_g"], i["L0_xattn_kn_g"]]),
        "wq0": T_(i["L0_xattn_Wq"]), "wkv0": T_(i["L0_xattn_Wkv"]), "wlkv0": T_(i["L0_xattn_Wlkv"]), "wo0": T_(i["L0_xattn_Wo"]), "bo0": i["L0_xattn_bo"],
        "wg0": T_(i["L0_ffn_Wg"]),
        "w13": np.concatenate([np.concatenate([T_(i["L0_ffn_W1"]), T_(i["L0_ffn_Ws1"])[None]]),
                               np.concatenate([T_(i["L0_ffn_W2"]), T_(i["L0_ffn_Ws2"])[None]])], axis=2),
        "w2": np.concatenate([T_(i["L0_ffn_W3"]), T_(i["L0_ffn_Ws3"])[None]]),
        "wq1": i["L1_xattn_Wq"], "wk1": i["L1_xattn_Wk"], "cols1": columns(i["L1_xattn_bq"], i["L1_xattn_bk"]),
        "wv1": i["L1_xattn_Wv"], "bv1": i["L1_xattn_bv"],
        "w_red": T_(i["L1_ffn_w_red"]), "wg1": i["L1_ffn_wg"],
        "v1": i["L1_ffn_W1"], "b1": i["L1_ffn_b1"], "v2": i["L1_ffn_W2"], "b2": i["L1_ffn_b2"],
    }


def kernel(**inputs):
    import concourse.bacc as bacc
    from concourse.bass_utils import run_bass_kernel_spmd

    nc = bacc.Bacc("TRN2", target_bir_lowering=False, num_devices=1)
    arrays, args = {}, {}
    for name, array in lay_out(inputs).items():
        array = np.ascontiguousarray(array)
        arrays[f"in_{name}"] = array
        args[name] = nc.dram_tensor(f"in_{name}", array.shape, mybir.dt.from_np(array.dtype), kind="ExternalInput").ap()
    out = nc.dram_tensor("out_x", (NTOK, C), F32, kind="ExternalOutput").ap()
    program(nc, args, out)
    result = run_bass_kernel_spmd(nc, [arrays], core_ids=[0])
    return np.asarray(result.results[0]["out_x"]).reshape(B, S, C)
```
